# Optimizing a Trainium2 kernel written in Bass

```python
import numpy as np
import jax
import jax.numpy as jnp

def _softmax(x, axis=-1):
    return jax.nn.softmax(x, axis=axis)

def _gelu(x):
    return jax.nn.gelu(x, approximate=True)

def _silu(x):
    return jax.nn.silu(x)

def _sigmoid(x):
    return jax.nn.sigmoid(x)

def _layernorm(x, axis=-1, eps=1e-05):
    m = jnp.mean(x, axis=axis, keepdims=True)
    v = jnp.var(x, axis=axis, keepdims=True)
    return (x - m) / jnp.sqrt(v + eps)

def _scatter_add(tgt, idx, src, axis=0):
    return tgt.at[idx].add(src)

def _segment_sum(src, seg, n):
    return jax.ops.segment_sum(src, seg, n)
kernel_name = 'mk_conv_attn_hybrid_d4_conv_nhwc384_r4_16881e'

def setup_inputs(seed: int=0):
    np.random.seed(seed)
    _w = jnp.asarray

    def _rec_inputs():
        import jax
        import jax.numpy as jnp
        _gk = jax.random.key(seed)
        x = -0.0002221 + 1 * jax.random.normal(jax.random.fold_in(_gk, 1), (16, 16, 16, 96), jnp.float32)
        return x
    x = _rec_inputs()

    def _L0_conv_setup():
        import jax, jax.numpy as jnp
        import numpy as np
        LN_EPS = 1e-05

        def _rel_pos_index(ws):
            coords = np.stack(np.meshgrid(np.arange(ws), np.arange(ws), indexing='ij')).reshape(2, -1)
            rel = (coords[:, :, None] - coords[:, None, :]).transpose(1, 2, 0)
            rel[:, :, 0] += ws - 1
            rel[:, :, 1] += ws - 1
            rel[:, :, 0] *= 2 * ws - 1
            return jnp.asarray(rel.sum(-1))

        def _layernorm(x, w, b):
            m = jnp.mean(x, axis=-1, keepdims=True)
            v = jnp.mean(jnp.square(x - m), axis=-1, keepdims=True)
            return (x - m) * jax.lax.rsqrt(v + LN_EPS) * w + b
        key = jax.random.key(seed)
        ks = jax.random.split(key, 8)
        B, H, W, C = (16, 16, 16, 96)
        ws, heads = (8, 12)
        hid = 4 * C
        s = 0.02
        return {'x': jax.random.normal(ks[0], (B, H, W, C), jnp.float32), 'ln1_w': jnp.ones((C,), jnp.float32), 'ln1_b': jnp.zeros((C,), jnp.float32), 'qkv_w': jax.random.normal(ks[1], (C, 3 * C), jnp.float32) * s, 'qkv_b': jnp.zeros((3 * C,), jnp.float32), 'proj_w': jax.random.normal(ks[2], (C, C), jnp.float32) * s, 'proj_b': jnp.zeros((C,), jnp.float32), 'rpb_table': jax.random.normal(ks[3], ((2 * ws - 1) ** 2, heads), jnp.float32) * s, 'ln2_w': jnp.ones((C,), jnp.float32), 'ln2_b': jnp.zeros((C,), jnp.float32), 'mlp_w1': jax.random.normal(ks[4], (C, hid), jnp.float32) * s, 'mlp_b1': jnp.zeros((hid,), jnp.float32), 'mlp_w2': jax.random.normal(ks[5], (hid, C), jnp.float32) * s, 'mlp_b2': jnp.zeros((C,), jnp.float32), 'window_size': ws, 'num_heads': heads}
    _L0_conv_all = _L0_conv_setup()
    _L0_conv_in = {k: v for k, v in _L0_conv_all.items() if k in ('ln1_w', 'ln1_b', 'qkv_w', 'qkv_b', 'proj_w', 'proj_b', 'rpb_table', 'ln2_w', 'ln2_b', 'mlp_w1', 'mlp_b1', 'mlp_w2', 'mlp_b2')}
    del _L0_conv_all

    def _L1_conv_setup():
        import jax, jax.numpy as jnp
        import numpy as np
        DECAY = 0.6
        GAIN = 0.4

        def _layernorm(x, g, b, eps=1e-05):
            m = x.mean(-1, keepdims=True)
            v = x.var(-1, keepdims=True)
            return (x - m) * jax.lax.rsqrt(v + eps) * g + b

        def _ema_scan(x, axis, reverse=False):
            a = jnp.full_like(x, DECAY)
            b = GAIN * x

            def comb(c1, c2):
                a1, b1 = c1
                a2, b2 = c2
                return (a1 * a2, a2 * b1 + b2)
            _, y = jax.lax.associative_scan(comb, (a, b), axis=axis, reverse=reverse)
            return y
        key = jax.random.key(seed)
        B, H, W, D = (16, 16, 16, 96)
        inner = 2 * D
        hidden = 4 * D
        ks = jax.random.split(key, 12)
        s = 0.02
        return {'x': jax.random.normal(ks[0], (B, H, W, D), jnp.float32), 'n1_g': jnp.ones((D,), jnp.float32), 'n1_b': jnp.zeros((D,), jnp.float32), 'w_in': s * jax.random.normal(ks[1], (D, inner), jnp.float32), 'b_in': jnp.zeros((inner,), jnp.float32), 'k_conv': s * jax.random.normal(ks[2], (3, 3, 1, inner), jnp.float32), 'on_g': jnp.ones((inner,), jnp.float32), 'on_b': jnp.zeros((inner,), jnp.float32), 'w_out': s * jax.random.normal(ks[3], (inner, D), jnp.float32), 'b_out': jnp.zeros((D,), jnp.float32), 'n2_g': jnp.ones((D,), jnp.float32), 'n2_b': jnp.zeros((D,), jnp.float32), 'w1': s * jax.random.normal(ks[4], (D, hidden), jnp.float32), 'b1': jnp.zeros((hidden,), jnp.float32), 'w2': s * jax.random.normal(ks[5], (hidden, D), jnp.float32), 'b2': jnp.zeros((D,), jnp.float32)}
    _L1_conv_all = _L1_conv_setup()
    _L1_conv_in = {k: v for k, v in _L1_conv_all.items() if k in ('n1_g', 'n1_b', 'w_in', 'b_in', 'k_conv', 'on_g', 'on_b', 'w_out', 'b_out', 'n2_g', 'n2_b', 'w1', 'b1', 'w2', 'b2')}
    del _L1_conv_all

    def _L2_attn_setup():
        import jax, jax.numpy as jnp
        import numpy as np
        NUM_HEADS = 8
        DIM_HEAD = 48
        SCALE = DIM_HEAD ** (-0.5)
        key = jax.random.key(seed)
        k1, k2, k3 = jax.random.split(key, 3)
        B, N, D = (4, 512, 96)
        inner = NUM_HEADS * DIM_HEAD
        x = jax.random.normal(k1, (B, N, D), dtype=jnp.float32)
        Wqkv = jax.random.normal(k2, (D, 3 * inner), dtype=jnp.float32) * D ** (-0.5)
        Wproj = jax.random.normal(k3, (inner, D), dtype=jnp.float32) * inner ** (-0.5)
        bproj = jnp.zeros((D,), dtype=jnp.float32)
        return {'x': x, 'Wqkv': Wqkv, 'Wproj': Wproj, 'bproj': bproj}
    _L2_attn_all = _L2_attn_setup()
    _L2_attn_in = {k: v for k, v in _L2_attn_all.items() if k in ('Wqkv', 'Wproj', 'bproj')}
    del _L2_attn_all

    def _L2_ffn_setup():
        import jax, jax.numpy as jnp
        import numpy as np
        NUM_GROUPS = 5
        EPS = 1e-05
        QB = 128.0

        def _binarize_weights_groupwise(W):
            n_out = W.shape[0]
            gs = n_out // NUM_GROUPS
            Wb = jnp.zeros_like(W)
            for g in range(NUM_GROUPS):
                wg = W[g * gs:(g + 1) * gs]
                z = wg - wg.mean()
                ste = z + jax.lax.stop_gradient(jnp.sign(z) - z)
                Wb = Wb.at[g * gs:(g + 1) * gs].set(ste)
            return Wb

        def _quantize_activations_groupwise(x):
            n = x.shape[0]
            gs = n // NUM_GROUPS
            xq = jnp.zeros_like(x)
            for g in range(NUM_GROUPS):
                ag = x[g * gs:(g + 1) * gs]
                gamma = jnp.max(jnp.abs(ag))
                xq = xq.at[g * gs:(g + 1) * gs].set(jnp.clip(ag * QB / (gamma + EPS), -QB + EPS, QB - EPS))
            return xq

        def _bitlinear(x, W, b):
            Wb = _binarize_weights_groupwise(W)
            y = jnp.einsum('btc,oc->bto', x, Wb) + b
            return _quantize_activations_groupwise(y)
        key = jax.random.key(seed)
        k1, k2, k3, k4, k5 = jax.random.split(key, 5)
        B, T, C = (10, 512, 96)
        H = 4 * C
        lim1 = 1.0 / np.sqrt(C)
        lim2 = 1.0 / np.sqrt(H)
        x = jax.random.normal(k1, (B, T, C), dtype=jnp.float32)
        W1 = jax.random.uniform(k2, (H, C), minval=-lim1, maxval=lim1, dtype=jnp.float32)
        b1 = jax.random.uniform(k3, (H,), minval=-lim1, maxval=lim1, dtype=jnp.float32)
        W2 = jax.random.uniform(k4, (C, H), minval=-lim2, maxval=lim2, dtype=jnp.float32)
        b2 = jax.random.uniform(k5, (C,), minval=-lim2, maxval=lim2, dtype=jnp.float32)
        return {'x': x, 'W1': W1, 'b1': b1, 'W2': W2, 'b2': b2}
    _L2_ffn_all = _L2_ffn_setup()
    _L2_ffn_in = {k: v for k, v in _L2_ffn_all.items() if k in ('W1', 'b1', 'W2', 'b2')}
    del _L2_ffn_all

    def _L3_attn_setup():
        import jax, jax.numpy as jnp
        import numpy as np
        N_HEADS = 6
        key = jax.random.key(seed)
        ks = jax.random.split(key, 5)
        B, T, C = (32, 64, 96)
        s = 0.02
        return {'x': jax.random.normal(ks[0], (B, T, C), jnp.float32), 'Wk': jax.random.normal(ks[1], (C, C), jnp.float32) * s, 'Wq': jax.random.normal(ks[2], (C, C), jnp.float32) * s, 'Wv': jax.random.normal(ks[3], (C, C), jnp.float32) * s, 'Wp': jax.random.normal(ks[4], (C, C), jnp.float32) * s, 'bp': jnp.zeros((C,), jnp.float32)}
    _L3_attn_all = _L3_attn_setup()
    _L3_attn_in = {k: v for k, v in _L3_attn_all.items() if k in ('Wk', 'Wq', 'Wv', 'Wp', 'bp')}
    del _L3_attn_all

    def _L3_ffn_setup():
        import jax, jax.numpy as jnp
        import numpy as np
        NUM_EXPERTS = 4
        TOP_K = 2
        DIM = 96
        HID = 4 * DIM
        key = jax.random.key(seed)
        ks = jax.random.split(key, 5)
        B, S = (16, 512)
        scale_in = 1.0 / np.sqrt(DIM)
        scale_hid = 1.0 / np.sqrt(HID)
        return {'x': jax.random.normal(ks[0], (B, S, DIM), dtype=jnp.float32), 'gate_w': jax.random.normal(ks[1], (DIM, NUM_EXPERTS), dtype=jnp.float32) * scale_in, 'gate_b': jnp.zeros((NUM_EXPERTS,), dtype=jnp.float32), 'w1': jax.random.normal(ks[2], (NUM_EXPERTS, DIM, HID), dtype=jnp.float32) * scale_in, 'b1': jnp.zeros((NUM_EXPERTS, HID), dtype=jnp.float32), 'w2': jax.random.normal(ks[3], (NUM_EXPERTS, HID, DIM), dtype=jnp.float32) * scale_hid, 'b2': jnp.zeros((NUM_EXPERTS, DIM), dtype=jnp.float32)}
    _L3_ffn_all = _L3_ffn_setup()
    _L3_ffn_in = {k: v for k, v in _L3_ffn_all.items() if k in ('gate_w', 'gate_b', 'w1', 'b1', 'w2', 'b2')}
    del _L3_ffn_all
    return {'x': x, 'L0_conv_ln1_w': _L0_conv_in['ln1_w'], 'L0_conv_ln1_b': _L0_conv_in['ln1_b'], 'L0_conv_qkv_w': _L0_conv_in['qkv_w'], 'L0_conv_qkv_b': _L0_conv_in['qkv_b'], 'L0_conv_proj_w': _L0_conv_in['proj_w'], 'L0_conv_proj_b': _L0_conv_in['proj_b'], 'L0_conv_rpb_table': _L0_conv_in['rpb_table'], 'L0_conv_ln2_w': _L0_conv_in['ln2_w'], 'L0_conv_ln2_b': _L0_conv_in['ln2_b'], 'L0_conv_mlp_w1': _L0_conv_in['mlp_w1'], 'L0_conv_mlp_b1': _L0_conv_in['mlp_b1'], 'L0_conv_mlp_w2': _L0_conv_in['mlp_w2'], 'L0_conv_mlp_b2': _L0_conv_in['mlp_b2'], 'L1_conv_n1_g': _L1_conv_in['n1_g'], 'L1_conv_n1_b': _L1_conv_in['n1_b'], 'L1_conv_w_in': _L1_conv_in['w_in'], 'L1_conv_b_in': _L1_conv_in['b_in'], 'L1_conv_k_conv': _L1_conv_in['k_conv'], 'L1_conv_on_g': _L1_conv_in['on_g'], 'L1_conv_on_b': _L1_conv_in['on_b'], 'L1_conv_w_out': _L1_conv_in['w_out'], 'L1_conv_b_out': _L1_conv_in['b_out'], 'L1_conv_n2_g': _L1_conv_in['n2_g'], 'L1_conv_n2_b': _L1_conv_in['n2_b'], 'L1_conv_w1': _L1_conv_in['w1'], 'L1_conv_b1': _L1_conv_in['b1'], 'L1_conv_w2': _L1_conv_in['w2'], 'L1_conv_b2': _L1_conv_in['b2'], 'L2_attn_Wqkv': _L2_attn_in['Wqkv'], 'L2_attn_Wproj': _L2_attn_in['Wproj'], 'L2_attn_bproj': _L2_attn_in['bproj'], 'L2_ffn_W1': _L2_ffn_in['W1'], 'L2_ffn_b1': _L2_ffn_in['b1'], 'L2_ffn_W2': _L2_ffn_in['W2'], 'L2_ffn_b2': _L2_ffn_in['b2'], 'L3_attn_Wk': _L3_attn_in['Wk'], 'L3_attn_Wq': _L3_attn_in['Wq'], 'L3_attn_Wv': _L3_attn_in['Wv'], 'L3_attn_Wp': _L3_attn_in['Wp'], 'L3_attn_bp': _L3_attn_in['bp'], 'L3_ffn_gate_w': _L3_ffn_in['gate_w'], 'L3_ffn_gate_b': _L3_ffn_in['gate_b'], 'L3_ffn_w1': _L3_ffn_in['w1'], 'L3_ffn_b1': _L3_ffn_in['b1'], 'L3_ffn_w2': _L3_ffn_in['w2'], 'L3_ffn_b2': _L3_ffn_in['b2']}

def reference(x, L0_conv_ln1_w, L0_conv_ln1_b, L0_conv_qkv_w, L0_conv_qkv_b, L0_conv_proj_w, L0_conv_proj_b, L0_conv_rpb_table, L0_conv_ln2_w, L0_conv_ln2_b, L0_conv_mlp_w1, L0_conv_mlp_b1, L0_conv_mlp_w2, L0_conv_mlp_b2, L1_conv_n1_g, L1_conv_n1_b, L1_conv_w_in, L1_conv_b_in, L1_conv_k_conv, L1_conv_on_g, L1_conv_on_b, L1_conv_w_out, L1_conv_b_out, L1_conv_n2_g, L1_conv_n2_b, L1_conv_w1, L1_conv_b1, L1_conv_w2, L1_conv_b2, L2_attn_Wqkv, L2_attn_Wproj, L2_attn_bproj, L2_ffn_W1, L2_ffn_b1, L2_ffn_W2, L2_ffn_b2, L3_attn_Wk, L3_attn_Wq, L3_attn_Wv, L3_attn_Wp, L3_attn_bp, L3_ffn_gate_w, L3_ffn_gate_b, L3_ffn_w1, L3_ffn_b1, L3_ffn_w2, L3_ffn_b2):
    import jax
    import jax.numpy as jnp

    def _L0_conv_ref(x, ln1_w, ln1_b, qkv_w, qkv_b, proj_w, proj_b, rpb_table, ln2_w, ln2_b, mlp_w1, mlp_b1, mlp_w2, mlp_b2, window_size, num_heads):
        import jax, jax.numpy as jnp
        import numpy as np
        LN_EPS = 1e-05

        def _rel_pos_index(ws):
            coords = np.stack(np.meshgrid(np.arange(ws), np.arange(ws), indexing='ij')).reshape(2, -1)
            rel = (coords[:, :, None] - coords[:, None, :]).transpose(1, 2, 0)
            rel[:, :, 0] += ws - 1
            rel[:, :, 1] += ws - 1
            rel[:, :, 0] *= 2 * ws - 1
            return jnp.asarray(rel.sum(-1))

        def _layernorm(x, w, b):
            m = jnp.mean(x, axis=-1, keepdims=True)
            v = jnp.mean(jnp.square(x - m), axis=-1, keepdims=True)
            return (x - m) * jax.lax.rsqrt(v + LN_EPS) * w + b
        B, H, W, C = x.shape
        ws = window_size
        hd = C // num_heads
        N = ws * ws
        shortcut = x
        h = _layernorm(x, ln1_w, ln1_b)
        pad_h = (ws - H % ws) % ws
        pad_w = (ws - W % ws) % ws
        if pad_h or pad_w:
            h = jnp.pad(h, ((0, 0), (0, pad_h), (0, pad_w), (0, 0)))
        Hp, Wp = (h.shape[1], h.shape[2])
        nH, nW = (Hp // ws, Wp // ws)
        hw = h.reshape(B, nH, ws, nW, ws, C).transpose(0, 1, 3, 2, 4, 5).reshape(B * nH * nW, N, C)
        qkv = hw @ qkv_w + qkv_b
        qkv = qkv.reshape(-1, N, 3, num_heads, hd).transpose(2, 0, 3, 1, 4)
        q, k, v = (qkv[0], qkv[1], qkv[2])
        scale = hd ** (-0.5)
        attn = jnp.einsum('bhnd,bhmd->bhnm', q, k) * scale
        rel_idx = _rel_pos_index(ws)
        bias = rpb_table[rel_idx]
        attn = attn + bias.transpose(2, 0, 1)[None]
        attn = jax.nn.softmax(attn, axis=-1)
        out = jnp.einsum('bhnm,bhmd->bhnd', attn, v).transpose(0, 2, 1, 3).reshape(-1, N, C)
        out = out @ proj_w + proj_b
        h = out.reshape(B, nH, nW, ws, ws, C).transpose(0, 1, 3, 2, 4, 5).reshape(B, Hp, Wp, C)
        if pad_h or pad_w:
            h = h[:, :H, :W, :]
        x = shortcut + h
        m = _layernorm(x, ln2_w, ln2_b)
        m = jax.nn.gelu(m @ mlp_w1 + mlp_b1, approximate=False) @ mlp_w2 + mlp_b2
        return x + m

    def _L1_conv_ref(x, n1_g, n1_b, w_in, b_in, k_conv, on_g, on_b, w_out, b_out, n2_g, n2_b, w1, b1, w2, b2):
        import jax, jax.numpy as jnp
        import numpy as np
        DECAY = 0.6
        GAIN = 0.4

        def _layernorm(x, g, b, eps=1e-05):
            m = x.mean(-1, keepdims=True)
            v = x.var(-1, keepdims=True)
            return (x - m) * jax.lax.rsqrt(v + eps) * g + b

        def _ema_scan(x, axis, reverse=False):
            a = jnp.full_like(x, DECAY)
            b = GAIN * x

            def comb(c1, c2):
                a1, b1 = c1
                a2, b2 = c2
                return (a1 * a2, a2 * b1 + b2)
            _, y = jax.lax.associative_scan(comb, (a, b), axis=axis, reverse=reverse)
            return y
        inner = w_in.shape[1]
        h = _layernorm(x, n1_g, n1_b)
        p = h @ w_in + b_in
        local = jax.lax.conv_general_dilated(p, k_conv, window_strides=(1, 1), padding='SAME', dimension_numbers=('NHWC', 'HWIO', 'NHWC'), feature_group_count=inner)
        lr = _ema_scan(local, axis=2)
        rl = _ema_scan(local, axis=2, reverse=True)
        tb = _ema_scan(local, axis=1)
        bt = _ema_scan(local, axis=1, reverse=True)
        mixed = 0.25 * (lr + rl + tb + bt) + local
        mixed = _layernorm(mixed, on_g, on_b)
        x = x + (mixed @ w_out + b_out)
        h2 = _layernorm(x, n2_g, n2_b)
        m = jax.nn.gelu(h2 @ w1 + b1, approximate=False) @ w2 + b2
        return x + m

    def _L2_attn_ref(x, Wqkv, Wproj, bproj):
        import jax, jax.numpy as jnp
        import numpy as np
        NUM_HEADS = 8
        DIM_HEAD = 48
        SCALE = DIM_HEAD ** (-0.5)
        B, N, D = x.shape
        h, dh = (NUM_HEADS, DIM_HEAD)
        C = h * dh
        qkv = (x @ Wqkv).reshape(B, N, 3, h, dh)
        q = qkv[:, :, 0].transpose(0, 2, 1, 3)
        k = qkv[:, :, 1].transpose(0, 2, 1, 3)
        v = qkv[:, :, 2].transpose(0, 2, 1, 3)
        sim = jnp.einsum('bhqd,bhkd->bhqk', q, k) * SCALE
        attn = jax.nn.softmax(sim, axis=-1)
        out = jnp.einsum('bhqk,bhkd->bhqd', attn, v)
        out = out.transpose(0, 2, 1, 3).reshape(B, N, C)
        return out @ Wproj + bproj

    def _L2_ffn_ref(x, W1, b1, W2, b2):
        import jax, jax.numpy as jnp
        import numpy as np
        NUM_GROUPS = 5
        EPS = 1e-05
        QB = 128.0

        def _binarize_weights_groupwise(W):
            n_out = W.shape[0]
            gs = n_out // NUM_GROUPS
            Wb = jnp.zeros_like(W)
            for g in range(NUM_GROUPS):
                wg = W[g * gs:(g + 1) * gs]
                z = wg - wg.mean()
                ste = z + jax.lax.stop_gradient(jnp.sign(z) - z)
                Wb = Wb.at[g * gs:(g + 1) * gs].set(ste)
            return Wb

        def _quantize_activations_groupwise(x):
            n = x.shape[0]
            gs = n // NUM_GROUPS
            xq = jnp.zeros_like(x)
            for g in range(NUM_GROUPS):
                ag = x[g * gs:(g + 1) * gs]
                gamma = jnp.max(jnp.abs(ag))
                xq = xq.at[g * gs:(g + 1) * gs].set(jnp.clip(ag * QB / (gamma + EPS), -QB + EPS, QB - EPS))
            return xq

        def _bitlinear(x, W, b):
            Wb = _binarize_weights_groupwise(W)
            y = jnp.einsum('btc,oc->bto', x, Wb) + b
            return _quantize_activations_groupwise(y)
        h = _bitlinear(x, W1, b1)
        h = jax.nn.gelu(h, approximate=False)
        out = _bitlinear(h, W2, b2)
        return out

    def _L3_attn_ref(x, Wk, Wq, Wv, Wp, bp):
        import jax, jax.numpy as jnp
        import numpy as np
        N_HEADS = 6
        B, T, C = x.shape
        H = N_HEADS
        hs = C // H
        k = (x @ Wk).reshape(B, H, T, hs)
        q = (x @ Wq).reshape(B, H, T, hs)
        v = (x @ Wv).reshape(B, H, T, hs)
        scale = C ** (-0.5)
        wei = jnp.einsum('bhtd,bhsd->bhts', q, k) * scale
        mask = jnp.tril(jnp.ones((T, T), dtype=bool))
        wei = jnp.where(mask, wei, -jnp.inf)
        wei = jax.nn.softmax(wei, axis=-1)
        out = jnp.einsum('bhts,bhsd->bhtd', wei, v).reshape(B, T, C)
        return out @ Wp + bp

    def _L3_ffn_ref(x, gate_w, gate_b, w1, b1, w2, b2):
        import jax, jax.numpy as jnp
        import numpy as np
        NUM_EXPERTS = 4
        TOP_K = 2
        DIM = 96
        HID = 4 * DIM
        scores = jnp.einsum('bsd,de->bse', x, gate_w) + gate_b
        probs = jax.nn.softmax(scores, axis=-1)
        topk_vals, topk_idx = jax.lax.top_k(probs, TOP_K)
        mask = jnp.sum(jax.nn.one_hot(topk_idx, NUM_EXPERTS, dtype=probs.dtype), axis=-2)
        masked = probs * mask
        masked = masked / (jnp.sum(masked, axis=-1, keepdims=True) + 1e-09)
        h = jax.nn.gelu(jnp.einsum('bsd,edh->ebsh', x, w1) + b1[:, None, None, :], approximate=False)
        y = jnp.einsum('ebsh,ehd->ebsd', h, w2) + b2[:, None, None, :]
        out = jnp.einsum('bse,ebsd->bsd', masked, y)
        return out

    def _gn(v, G=32, eps=1e-05):
        B_, H_, W_, C_ = v.shape
        g = v.reshape(B_, H_, W_, G, C_ // G)
        m = jnp.mean(g, axis=(1, 2, 4), keepdims=True)
        s = jnp.var(g, axis=(1, 2, 4), keepdims=True)
        return ((g - m) / jnp.sqrt(s + eps)).reshape(v.shape)

    def _ln_c(v, eps=1e-06):
        m = jnp.mean(v, axis=-1, keepdims=True)
        s = jnp.var(v, axis=-1, keepdims=True)
        return (v - m) / jnp.sqrt(s + eps)

    def _ln_t(v, eps=1e-05):
        m = jnp.mean(v, axis=-1, keepdims=True)
        s = jnp.var(v, axis=-1, keepdims=True)
        return (v - m) / jnp.sqrt(s + eps)

    def _to_tokens(v):
        B_, H_, W_, C_ = v.shape
        return v.reshape(B_, H_ * W_, C_)

    def _from_tokens(t, like):
        return t.reshape(like.shape)
    x = _L0_conv_ref(x, L0_conv_ln1_w, L0_conv_ln1_b, L0_conv_qkv_w, L0_conv_qkv_b, L0_conv_proj_w, L0_conv_proj_b, L0_conv_rpb_table, L0_conv_ln2_w, L0_conv_ln2_b, L0_conv_mlp_w1, L0_conv_mlp_b1, L0_conv_mlp_w2, L0_conv_mlp_b2, 8, 12)
    x = _L1_conv_ref(x, L1_conv_n1_g, L1_conv_n1_b, L1_conv_w_in, L1_conv_b_in, L1_conv_k_conv, L1_conv_on_g, L1_conv_on_b, L1_conv_w_out, L1_conv_b_out, L1_conv_n2_g, L1_conv_n2_b, L1_conv_w1, L1_conv_b1, L1_conv_w2, L1_conv_b2)
    t = _to_tokens(x)
    t = t + _L2_attn_ref(_ln_t(t), L2_attn_Wqkv, L2_attn_Wproj, L2_attn_bproj)
    t = t + _L2_ffn_ref(_ln_t(t), L2_ffn_W1, L2_ffn_b1, L2_ffn_W2, L2_ffn_b2)
    t = t + _L3_attn_ref(_ln_t(t), L3_attn_Wk, L3_attn_Wq, L3_attn_Wv, L3_attn_Wp, L3_attn_bp)
    t = t + _L3_ffn_ref(_ln_t(t), L3_ffn_gate_w, L3_ffn_gate_b, L3_ffn_w1, L3_ffn_b1, L3_ffn_w2, L3_ffn_b2)
    x = _from_tokens(t, x)
    return x

_drawn_inputs = setup_inputs


def setup_inputs(seed=0):
    import zlib

    import numpy as np

    out = dict(_drawn_inputs(seed))
    spreads = {'L0_conv_ln1_w': (1.0, 0.6),
     'L0_conv_ln1_b': (0.0, 0.8),
     'L0_conv_qkv_b': (0.0, 0.335),
     'L0_conv_proj_b': (0.0, 0.1),
     'L0_conv_ln2_w': (1.0, 0.6),
     'L0_conv_ln2_b': (0.0, 0.8),
     'L0_conv_mlp_b1': (0.0, 0.294),
     'L0_conv_mlp_b2': (0.0, 0.1),
     'L1_conv_n1_g': (1.0, 0.2),
     'L1_conv_n1_b': (0.0, 0.1),
     'L1_conv_b_in': (0.0, 0.1),
     'L1_conv_on_g': (1.0, 0.2),
     'L1_conv_on_b': (0.0, 0.1),
     'L1_conv_b_out': (0.0, 0.1),
     'L1_conv_n2_g': (1.0, 0.6),
     'L1_conv_n2_b': (0.0, 0.8),
     'L1_conv_b1': (0.0, 0.326),
     'L1_conv_b2': (0.0, 0.1),
     'L2_attn_bproj': (0.0, 0.1),
     'L3_attn_bp': (0.0, 0.8),
     'L3_ffn_gate_b': (0.0, 0.8),
     'L3_ffn_b1': (0.0, 0.8),
     'L3_ffn_b2': (0.0, 2.0)}
    factors = {'L0_conv_qkv_w': 7.359,
     'L0_conv_rpb_table': 23.842,
     'L2_ffn_b1': 8.0,
     'L2_ffn_b2': 200.0,
     'L3_attn_Wk': 8.0,
     'L3_attn_Wq': 8.0,
     'L3_attn_Wv': 8.0,
     'L3_attn_Wp': 8.0,
     'L3_ffn_gate_w': 3.652,
     'L3_ffn_w1': 3.667,
     'L3_ffn_w2': 3.143}
    for name, (base, spread) in spreads.items():
        noise = np.random.default_rng([zlib.crc32(name.encode()), seed]).standard_normal(out[name].shape)
        drawn = base * np.exp(spread * noise) if base else spread * noise
        out[name] = jnp.asarray(drawn.astype(out[name].dtype))
    for name, factor in factors.items():
        out[name] = (out[name] * factor).astype(out[name].dtype)
    return out
```

```python
from contextlib import ExitStack

import numpy as np

import concourse.bass as bass
from concourse import mybir

F32 = mybir.dt.float32
BF16 = mybir.dt.bfloat16
ALU = mybir.AluOpType
ACT = mybir.ActivationFunctionType
AX = mybir.AxisListType

P = 128
IMAGES = 16
SIDE = 16
TOK = SIDE * SIDE
C = 96
TILES = IMAGES * TOK // P
HID = 4 * C
KH = HID // P
LN_EPS = 1e-5
WS = 8
WTOK = WS * WS
H0 = 12
D0 = C // H0
CI = 2 * C
H2, D2 = 8, 48
PAIRS2 = H2 // 2
H3 = 6
D3 = C // H3
GRID = SIDE + 2
GROUPS = 5
GIMG = IMAGES // GROUPS
GT = 2 * GIMG
EXPERTS = 4
EPS_Q = 1e-5
QB = 128.0


def after(eng, sem, count):
    if not isinstance(count, int) or count > 0:
        eng.wait_ge(sem, count)


def alone(eng, k):
    eng.wait_ge(k.started, 1)


def pairs(eng, steps, body):
    for s in range(2):
        body(s, s, s == 0)
    with eng.Fori(1, steps // 2) as g:
        for s in range(2):
            body(g * 2 + s, s, False)


class Core:

    def __init__(self, nc, ctx):
        self.nc, self.ctx = nc, ctx
        self.started = nc.alloc_semaphore(name="started")

    def sb(self, name, shape, dt=F32, ctx=None):
        return (ctx or self.ctx).enter_context(self.nc.sbuf_tensor(name, shape, dt))

    def sems(self, prefix, names):
        self.live = {n: self.nc.alloc_semaphore(name=f"{prefix}_{n}") for n in names.split()}
        return self.live

    def end_phase(self):
        self.nc.clear_and_free_semaphores(list(self.live.values()))
        self.nc.all_engine_barrier()


def tiles_of(t, first, count):
    return t[:, bass.ds(first, count), :]


def normalise(pool, k, s, n, count, y, bias, v, r, free):
    x = tiles_of(k.X, n * count, count)
    mean = tiles_of(k.MV, n * count, count)[:, :, 0:1]
    var = tiles_of(k.MV, n * count, count)[:, :, 1:2]
    alone(pool, k)
    after(pool, s["T"], free)
    pool.tensor_tensor(v[:, 0:count, :], var, k.eps[:, 0:count, :], ALU.add).then_inc(s["var"], 1)
    pool.tensor_tensor(y, x, mean.broadcast_to([P, count, C]), ALU.subtract).then_inc(s["centred"], 1)
    after(pool, s["var"], n + 1)
    pool.tensor_tensor(r[:, 0:count, :], v[:, 0:count, :], k.minus_half[:, 0:count, :], ALU.pow).then_inc(s["rstd"], 1)
    alone(pool, k)
    after(pool, s["rstd"], n + 1)
    after(pool, s["centred"], n + 1)
    pool.tensor_tensor(y, y, r[:, 0:count, :].broadcast_to([P, count, C]), ALU.mult).then_inc(s["y"], 1)
    if bias is not None:
        pool.tensor_tensor(x, x, bias[:, None, :].broadcast_to([P, count, C]), ALU.add).then_inc(s["xb"], 1)


def add_and_stats(dve, k, s, n, count, new, stats, aggr, replace=False):
    x = tiles_of(k.X, n * count, count)
    (dve.tensor_copy(x, new) if replace else dve.tensor_tensor(x, x, new, ALU.add)).then_inc(s["x"], 1)
    alone(dve, k)
    after(dve, s["x"], n + 1)
    after(dve, s["mv"], n)
    for t in range(count):
        last = dve.bn_stats(stats[:, t, :], k.X[:, bass.ds(n * count + t, 1), :])
    last.then_inc(s["bn"], 1)
    alone(dve, k)
    after(dve, s["bn"], n + 1)
    for t in range(count):
        last = dve.bn_aggr(aggr[:, t, :], stats[:, t, :])
    last.then_inc(s["ag"], 1)
    after(dve, s["ag"], n + 1)
    dve.tensor_copy(tiles_of(k.MV, n * count, count), aggr[:, 0:count, :]).then_inc(s["mv"], 1)


LN_SEMS = "var centred rstd y xb x bn ag mv "


def setup(k, a):
    nc = k.nc
    s = k.sems("set", "x w cst bn ag mv zero")
    sb = k.sb
    k.X = sb("X", [P, TILES, C])
    k.MV = sb("MV", [P, TILES, 2])
    k.ident = sb("ident", [P, P])
    k.identb = sb("identb", [P, P], BF16)
    k.causal = sb("causal", [P, P], BF16)
    k.eps = sb("eps", [P, 8, 1])
    k.minus_half = sb("minus_half", [P, 8, 1])
    k.ones = sb("ones", [P, P])
    k.stats = sb("stats", [P, 8, 6])
    k.aggr = sb("aggr", [P, 8, 2])
    k.v, k.r = sb("ln_v", [P, 8, 1]), sb("ln_r", [P, 8, 1])
    k.Y = [sb(f"Y{i}", [P, 4, C]) for i in range(2)]
    k.hT = [sb(f"hT{i}", [C, 512]) for i in range(2)]
    loads = []

    def weight(name, shape, src, dst=None):
        t = sb(name, shape)
        loads.append((t[:] if dst is None else dst(t), src))
        return t

    def column(name, src):
        return weight(name, [src.shape[0], 1], src[:, None])

    def row(name, src):
        return weight(name, [P, src.shape[0]], src[None, :].broadcast_to([P, src.shape[0]]))

    k.g1, k.b1 = column("w_g1", a["L0_conv_ln1_w"]), column("w_b1", a["L0_conv_ln1_b"])
    k.wqkv0 = weight("w_qkv0", [C, 3 * C], a["L0_conv_qkv_w"])
    k.bq0 = column("w_bq0", a["L0_conv_qkv_b"][0:C])
    k.bk0 = column("w_bk0", a["L0_conv_qkv_b"][C:2 * C])
    k.bv0 = row("w_bv0", a["L0_conv_qkv_b"][2 * C:3 * C])
    k.wp0 = weight("w_p0", [C, C], a["L0_conv_proj_w"])
    k.bp0 = row("w_bp0", a["L0_conv_proj_b"])
    k.headmask = weight("headmask", [C, H0], a["headmask"])
    k.bias0 = sb("bias0", [P, WTOK, H0])
    bias0r = sb("bias0r", [P, WTOK, H0])
    table = a["L0_conv_rpb_table"]
    span = 2 * WS - 1
    for wx in range(2):
        for qy in range(WS):
            src = bass.AP(tensor=table.tensor, offset=qy * span * H0, ap=[[H0, WS], [span * H0, WS], [1, WS * H0]])
            p0 = wx * WTOK + qy * WS
            loads.append((bias0r[p0:p0 + WS].rearrange("q (y x) h -> q y (x h)", y=WS), src))

    def mlp(p, g, b, w1, b1, w2, b2):
        return dict(g=column(p + "g", g), b=column(p + "b", b), w1=weight(p + "w1", [C, HID], w1),
                    b1=weight(p + "b1", [P, KH], b1.rearrange("(k p) -> p k", p=P)),
                    w2=weight(p + "w2", [P, KH, C], w2.rearrange("(k p) c -> p k c", p=P)), b2=row(p + "b2", b2))

    k.mlp0 = mlp("m0", a["L0_conv_ln2_w"], a["L0_conv_ln2_b"], a["L0_conv_mlp_w1"], a["L0_conv_mlp_b1"],
                 a["L0_conv_mlp_w2"], a["L0_conv_mlp_b2"])
    k.g3, k.b3 = column("w_g3", a["L1_conv_n1_g"]), column("w_b3", a["L1_conv_n1_b"])
    k.win = weight("w_in", [C, CI], a["L1_conv_w_in"])
    k.bin = weight("b_in", [C, 2], a["L1_conv_b_in"].rearrange("(j p) -> p j", p=C))
    k.kconv = sb("k_conv", [C, 2, 9])
    for j in range(2):
        loads.append((k.kconv[:, j, :], a["L1_conv_k_conv"].rearrange("a b o (j p) -> j p (a b o)", p=C)[j]))
    k.ong = weight("on_g", [C, 2], a["L1_conv_on_g"].rearrange("(j p) -> p j", p=C))
    k.onb = weight("on_b", [C, 2], a["L1_conv_on_b"].rearrange("(j p) -> p j", p=C))
    k.wout = weight("w_out", [C, 2, C], a["L1_conv_w_out"].rearrange("(j p) c -> p j c", p=C))
    k.bout = row("b_out", a["L1_conv_b_out"])
    k.perm = weight("perm", [P, P], a["perm"])
    k.mixer = weight("mixer", [P, 2, TOK], a["mixer"].rearrange("(j p) t -> p j t", p=P))
    k.mlp1 = mlp("m1", a["L1_conv_n2_g"], a["L1_conv_n2_b"], a["L1_conv_w1"], a["L1_conv_b1"],
                 a["L1_conv_w2"], a["L1_conv_b2"])
    wide = [C, PAIRS2, 2, 64]
    k.wq2, k.wk2 = sb("w_q2", wide), sb("w_k2", wide)
    for part, t in enumerate((k.wq2, k.wk2)):
        for p in range(PAIRS2):
            base = part * H2 * D2 + p * 2 * D2
            loads.append((t[:, p, :, 0:D2], a["L2_attn_Wqkv"][:, base:base + 2 * D2].rearrange("c (h d) -> c h d", h=2)))
    k.wv2 = weight("w_v2", [C, H2 * D2], a["L2_attn_Wqkv"][:, 2 * H2 * D2:3 * H2 * D2])
    k.wp2 = sb("w_p2", [P, PAIRS2, C])
    for h in range(2):
        loads.append((k.wp2[64 * h:64 * h + D2, :, :],
                      a["L2_attn_Wproj"].rearrange("(p h d) c -> h d p c", h=2, d=D2)[h]))
    k.bp2 = row("w_bp2", a["L2_attn_bproj"])
    k.fb1 = weight("f_b1", [P, KH], a["L2_ffn_b1"].rearrange("(k p) -> p k", p=P))
    k.fb2 = row("f_b2", a["L2_ffn_b2"])
    k.wq3 = weight("w_q3", [C, C], a["L3_attn_Wq"])
    k.wkv3 = sb("w_kv3", [C, H3, C + D3])
    for g in range(H3):
        loads.append((k.wkv3[:, g, 0:C].rearrange("c (i d) -> c i d", d=D3),
                      a["L3_attn_Wk"][:, None, g * D3:(g + 1) * D3].broadcast_to([C, H3, D3])))
    loads.append((k.wkv3[:, :, C:C + D3], a["L3_attn_Wv"].rearrange("c (g d) -> c g d", d=D3)))
    k.groupmask = weight("groupmask", [C, H3], a["groupmask"])
    k.wp3 = sb("w_p3", [C, H3, C])
    for g in range(H3):
        loads.append((k.wp3[g * D3:(g + 1) * D3, g, :], a["L3_attn_Wp"][g * D3:(g + 1) * D3, :]))
    k.bp3 = row("w_bp3", a["L3_attn_bp"])
    k.gw = weight("w_gate", [C, EXPERTS], a["L3_ffn_gate_w"])
    k.gb = row("b_gate", a["L3_ffn_gate_b"])
    k.ew1 = weight("e_w1", [C, EXPERTS, HID], a["L3_ffn_w1"].rearrange("e c h -> c e h"))
    k.eb1 = weight("e_b1", [P, EXPERTS, KH], a["L3_ffn_b1"].rearrange("e (k p) -> p e k", p=P))
    k.ew2 = weight("e_w2", [P, EXPERTS, KH, C], a["L3_ffn_w2"].rearrange("e (k p) c -> p e k c", p=P))
    k.eb2 = weight("e_b2", [P, EXPERTS, C], a["L3_ffn_b2"][None, :, :].broadcast_to([P, EXPERTS, C]))
    k.lower = weight("lower", [P, EXPERTS, EXPERTS], a["lower"][None, :, :].broadcast_to([P, EXPERTS, EXPERTS]))
    k.g76, k.g19 = HID // GROUPS, C // GROUPS
    k.f1 = weight("f_w1", [k.g76, GROUPS, C], a["L2_ffn_W1"][0:GROUPS * k.g76, :].rearrange("(g o) c -> o g c", g=GROUPS))
    k.f2 = weight("f_w2", [k.g19, GROUPS, HID], a["L2_ffn_W2"][0:GROUPS * k.g19, :].rearrange("(g o) c -> o g c", g=GROUPS))
    loads.append((k.ident[:], a["ident"]))
    stage = weight("causal_f", [P, P], a["causal"])

    with nc.Block() as block:
        @block.sync
        def _(sp):
            for wx in range(2):
                for r in range(WS):
                    p0 = wx * WTOK + r * WS
                    src = a["x"].rearrange("b (y i) (v c) d -> v i c (b y) d", i=WS, c=WS)[wx, r]
                    sp.dma_start(k.X[p0:p0 + WS, :, :], src).then_inc(s["x"], 16)
            sp.wait_ge(s["x"], 16 * 2 * WS)

        @block.gpsimd
        def _(pool):
            pool.memset(k.eps[:], LN_EPS).then_inc(k.started, 1)
            pool.memset(k.minus_half[:], -0.5)
            for t in (k.wq2, k.wk2, k.wp2, k.wp3, k.ones):
                last = pool.memset(t[:], 1.0 if t is k.ones else 0.0)
            last.then_inc(s["zero"], 1)
            pool.wait_ge(s["w"], 16 * len(loads))
            pool.tensor_copy(k.identb[:], k.ident[:])
            pool.tensor_copy(k.bias0[:], bias0r[:, ::-1, :])
            pool.tensor_copy(k.causal[:], stage[:]).then_inc(s["cst"], 1)

        @block.scalar
        def _(act):
            act.wait_ge(s["zero"], 1)
            for dst, src in loads:
                act.dma_start(dst, src, allow_slow_non_contiguous=True).then_inc(s["w"], 16)
            act.wait_ge(s["w"], 16 * len(loads))

        @block.vector
        def _(dve):
            dve.wait_ge(s["x"], 16 * 2 * WS)
            for n in range(TILES // 4):
                for t in range(4):
                    last = dve.bn_stats(k.stats[:, t, :], k.X[:, bass.ds(n * 4 + t, 1), :])
                last.then_inc(s["bn"], 1)
                after(dve, s["bn"], n + 1)
                for t in range(4):
                    last = dve.bn_aggr(k.aggr[:, t, :], k.stats[:, t, :])
                last.then_inc(s["ag"], 1)
                after(dve, s["ag"], n + 1)
                dve.tensor_copy(tiles_of(k.MV, n * 4, 4), k.aggr[:, 0:4, :]).then_inc(s["mv"], 1)
                after(dve, s["mv"], n + 1)


def window_attention(k, bank):
    nc = k.nc
    s = k.sems("wa", LN_SEMS + "init bq T hT qk q kb kx vp v sc add mx sub exp pt pte av rec a oT oTe pj")
    with ExitStack() as ctx:
        def sb(name, shape, dt=F32):
            return k.sb("wa_" + name, shape, dt, ctx)

        bqs = sb("bqs", [C, 1])
        h2 = [sb(f"h2{i}", [C, 4, 2, WTOK]) for i in range(2)]
        qT = [sb(f"q{i}", [C, TOK]) for i in range(2)]
        kT = sb("k", [C, TOK])
        kx = [sb(f"kx{i}", [C, H0, TOK]) for i in range(2)]
        vb = [sb(f"vb{i}", [P, 4, H0 // 2, 2 * D0 + 2]) for i in range(2)]
        S = [sb(f"s{i}", [P, H0, WTOK]) for i in range(2)]
        E = [sb(f"e{i}", [P, H0, WTOK]) for i in range(2)]
        mx = [sb(f"mx{i}", [P, H0, 1]) for i in range(2)]
        PT = sb("pt", [P, 2, 3, P])
        rec = sb("rec", [P, H0 // 2, 2, 1])
        A = [sb(f"a{i}", [P, 2, C]) for i in range(2)]
        AT = sb("at", [C, TOK])
        scale = float(D0) ** -0.5

        with nc.Block() as block:
            @block.gpsimd
            def _(pool):
                for i in range(2):
                    pool.memset(vb[i][:], 0.0).then_inc(s["bq"], 1)
                pool.wait_ge(s["bq"], 2)
                for i in range(2):
                    pool.memset(vb[i][0:WTOK, :, :, 2 * D0:2 * D0 + 1], 1.0).then_inc(s["init"], 1)
                    pool.wait_ge(s["init"], i + 1)
                    pool.memset(vb[i][WTOK:P, :, :, 2 * D0 + 1:2 * D0 + 2], 1.0).then_inc(s["bq"], 1)
                    pool.wait_ge(s["bq"], 3 + i)
                pool.tensor_scalar(bqs[:], k.bq0[:], scale, 0.0, ALU.mult, ALU.add).then_inc(s["bq"], 1)
                pool.wait_ge(s["bq"], 5)

                def body(n, slot, first):
                    normalise(pool, k, s, n, 2, k.Y[slot][:, 0:2, :], k.bp0, k.v, k.r, n - 1)
                    for t in range(2):
                        after(pool, s["mx"], 2 * n + t + 1)
                        pool.tensor_tensor(S[t][:], S[t][:], mx[t][:].broadcast_to([P, H0, WTOK]), ALU.subtract).then_inc(s["sub"], 1)
                pairs(pool, IMAGES, body)

            @block.tensor
            def _(pe):
                def probs(n, t, slot):
                    after(pe, s["exp"], 2 * n + t + 1)
                    after(pe, s["pte"], 2 * n + t)
                    for j in range(H0 // 2):
                        last = pe.transpose(bank[5 + j // 3][:, (j % 3) * P:(j % 3 + 1) * P],
                                            E[t][:, 2 * j:2 * j + 2, :].rearrange("p h k -> p (h k)"), k.ident[:])
                    last.then_inc(s["pt"], 1)
                    after(pe, s["pte"], 2 * n + t + 1)
                    after(pe, s["a"], 2 * n + t)
                    if t == 0:
                        after(pe, s["x"], n)
                    for w in range(2):
                        for j in range(H0 // 2):
                            last = pe.matmul(bank[7][w * WTOK:(w + 1) * WTOK, j * 18:(j + 1) * 18],
                                             PT[:, j // 3, j % 3, w * WTOK:(w + 1) * WTOK], vb[slot][:, 2 * t + w, j, :],
                                             start=True, stop=True)
                    last.then_inc(s["av"], 1)

                def finish(n, slot):
                    after(pe, s["a"], 2 * n + 2)
                    for t in range(2):
                        last = pe.transpose(bank[0][0:C, t * P:(t + 1) * P], A[slot][:, t, :], k.ident[:])
                    last.then_inc(s["oT"], 1)
                    after(pe, s["oTe"], n + 1)
                    for t in range(2):
                        last = pe.matmul(bank[7][:, t * C:(t + 1) * C], AT[:, t * P:(t + 1) * P], k.wp0[:], start=True, stop=True)
                    last.then_inc(s["pj"], 1)

                def body(n, slot, first):
                    after(pe, s["y"], n + 1)
                    after(pe, s["oTe"], n - 1)
                    for t in range(2):
                        last = pe.transpose(bank[0][0:C, t * P:(t + 1) * P], k.Y[slot][:, t, :], k.ident[:])
                    last.then_inc(s["T"], 1)
                    after(pe, s["hT"], n + 1)
                    after(pe, s["q"], n)
                    after(pe, s["kb"], n)
                    h = h2[slot][:, :, 0, :]
                    pe.matmul(bank[1][0:C, 0:TOK], k.wqkv0[:, 0:C], h, start=True, stop=True)
                    pe.matmul(bank[1][0:C, TOK:2 * TOK], k.wqkv0[:, C:2 * C], h, start=True, stop=True).then_inc(s["qk"], 1)
                    after(pe, s["v"], n)
                    for w in range(4):
                        last = pe.matmul(bank[2][:, w * C:(w + 1) * C], h2[slot][:, w, :, :].rearrange("p i k -> p (i k)"), k.wqkv0[:, 2 * C:3 * C], start=True, stop=True)
                    last.then_inc(s["vp"], 1)
                    if not first:
                        probs(n - 1, 1, 1 - slot)
                        finish(n - 1, 1 - slot)
                    after(pe, s["kx"], n + 1)
                    after(pe, s["q"], n + 1)
                    for t in range(2):
                        after(pe, s["add"], 2 * n + t)
                        for w in range(2):
                            for half in range(2):
                                o = (2 * t + w) * WTOK
                                last = pe.matmul(bank[3 + half][w * WTOK:(w + 1) * WTOK, 0:384], qT[slot][:, o:o + WTOK],
                                                 kx[slot][:, half * 6:half * 6 + 6, o:o + WTOK], start=True, stop=True)
                        last.then_inc(s["sc"], 1)
                    probs(n, 0, slot)
                pairs(pe, IMAGES, body)
                probs(IMAGES - 1, 1, 1)
                finish(IMAGES - 1, 1)

            @block.scalar
            def _(act):
                act.wait_ge(s["bq"], 5)

                def pt_out(n, t):
                    after(act, s["pt"], 2 * n + t + 1)
                    after(act, s["av"], 2 * n + t)
                    for b in range(2):
                        last = act.activation(PT[:, b, :, :], bank[5 + b][:, 0:384].rearrange("p (j q) -> p j q", j=3), ACT.Copy)
                    last.then_inc(s["pte"], 1)

                def exps(n, t):
                    after(act, s["sub"], 2 * n + t + 1)
                    after(act, s["pt"], 2 * n + t - 1)
                    act.activation(E[t][:], S[t][:], ACT.Exp).then_inc(s["exp"], 1)

                def out_t(n):
                    after(act, s["oT"], n + 1)
                    after(act, s["pj"], n)
                    act.activation(AT[:], bank[0][0:C, 0:TOK], ACT.Copy).then_inc(s["oTe"], 1)

                def body(n, slot, first):
                    after(act, s["T"], n + 1)
                    after(act, s["vp"], n - 1)
                    act.activation(h2[slot][:], bank[0][0:C, 0:TOK].rearrange("p (v k) -> p v k", v=4)[:, :, None, :].broadcast_to([C, 4, 2, WTOK]),
                                   ACT.Identity, bias=k.b1[:], scale=k.g1[:]).then_inc(s["hT"], 1)
                    after(act, s["qk"], n + 1)
                    after(act, s["sc"], 2 * n - 2)
                    act.activation(qT[slot][:], bank[1][0:C, 0:TOK], ACT.Identity, bias=bqs[:], scale=scale).then_inc(s["q"], 1)
                    if not first:
                        pt_out(n - 1, 1)
                        out_t(n - 1)
                    exps(n, 0)
                    pt_out(n, 0)
                    exps(n, 1)
                pairs(act, IMAGES, body)
                pt_out(IMAGES - 1, 1)
                out_t(IMAGES - 1)

            @block.vector
            def _(dve):
                def heads_out(n, t, slot):
                    after(dve, s["av"], 2 * n + t + 1)
                    after(dve, s["oT"], n - 1)
                    o = bank[7][:, 0:108].rearrange("p (j c) -> p j c", c=18)
                    dve.reciprocal(rec[:], o[:, :, 16:18, None]).then_inc(s["rec"], 1)
                    after(dve, s["rec"], 2 * n + t + 1)
                    dve.tensor_tensor(A[slot][:, t, :].rearrange("p (j i d) -> p j i d", j=H0 // 2, i=2),
                                      o[:, :, 0:16].rearrange("p j (i d) -> p j i d", i=2),
                                      rec[:].broadcast_to([P, H0 // 2, 2, D0]), ALU.mult).then_inc(s["a"], 1)

                def residual(n):
                    after(dve, s["pj"], n + 1)
                    after(dve, s["xb"], n + 1)
                    add_and_stats(dve, k, s, n, 2, bank[7][:, 0:2 * C].rearrange("p (t c) -> p t c", t=2), k.stats, k.aggr)

                def body(n, slot, first):
                    after(dve, s["qk"], n + 1)
                    after(dve, s["q"], n + 1)
                    dve.tensor_scalar(kT[:], bank[1][0:C, TOK:2 * TOK], k.bk0[:], None, ALU.add).then_inc(s["kb"], 1)
                    after(dve, s["kb"], n + 1)
                    after(dve, s["sc"], 2 * n - 2)
                    dve.tensor_tensor(kx[slot][:], kT[:, None, :].broadcast_to([C, H0, TOK]),
                                      k.headmask[:, :, None].broadcast_to([C, H0, TOK]), ALU.mult).then_inc(s["kx"], 1)
                    after(dve, s["vp"], n + 1)
                    after(dve, s["av"], 2 * n - 2)
                    if first:
                        dve.wait_ge(s["bq"], 5)
                    for r in range(2):
                        rows = slice(r * WTOK, (r + 1) * WTOK)
                        src = bank[2][rows, 0:4 * C].rearrange("p (v j i d) -> p v j i d", v=4, i=2, d=D0)
                        b = k.bv0[rows, :].rearrange("p (j i d) -> p j i d", i=2, d=D0)
                        for w in range(4):
                            last = dve.tensor_tensor(vb[slot][rows, w, :, r * D0:(r + 1) * D0], src[:, w, :, r, :], b[:, :, r, :], ALU.add)
                    last.then_inc(s["v"], 1)
                    if not first:
                        heads_out(n - 1, 1, 1 - slot)
                        residual(n - 1)
                    for t in range(2):
                        after(dve, s["sc"], 2 * n + t + 1)
                        after(dve, s["exp"], 2 * n + t - 1)
                        for half in range(2):
                            hs = slice(half * 6, half * 6 + 6)
                            last = dve.tensor_tensor(S[t][:, hs, :], bank[3 + half][:, 0:384].rearrange("p (h k) -> p h k", h=6),
                                                     k.bias0[:, :, hs].rearrange("p k h -> p h k"), ALU.add)
                        last.then_inc(s["add"], 1)
                        after(dve, s["add"], 2 * n + t + 1)
                        dve.tensor_reduce(mx[t][:, :, 0], S[t][:], AX.X, ALU.max).then_inc(s["mx"], 1)
                    heads_out(n, 0, slot)
                pairs(dve, IMAGES, body)
                heads_out(IMAGES - 1, 1, 1)
                residual(IMAGES - 1)


def mlp(k, bank, prefix, w):
    nc = k.nc
    s = k.sems(prefix, LN_SEMS + "T hT up gelu down")
    steps = TILES // 4
    with ExitStack() as ctx:
        G = [k.sb(f"{prefix}_G{i}", [P, KH, 512], F32, ctx) for i in range(2)]
        with nc.Block() as block:
            @block.gpsimd
            def _(pool):
                def body(n, slot, first):
                    normalise(pool, k, s, n, 4, k.Y[slot][:], w["b2"], k.v, k.r, n - 1)
                pairs(pool, steps, body)

            @block.tensor
            def _(pe):
                def down(n, slot):
                    after(pe, s["gelu"], KH * (n + 1))
                    after(pe, s["x"], n)
                    for t in range(4):
                        for j in range(KH):
                            last = pe.matmul(bank[7][:, t * C:(t + 1) * C], G[slot][:, j, t * P:(t + 1) * P], w["w2"][:, j, :],
                                             start=(j == 0), stop=(j == KH - 1))
                    last.then_inc(s["down"], 1)

                def body(n, slot, first):
                    after(pe, s["y"], n + 1)
                    after(pe, s["hT"], n)
                    for t in range(4):
                        last = pe.transpose(bank[6][0:C, t * P:(t + 1) * P], k.Y[slot][:, t, :], k.ident[:])
                    last.then_inc(s["T"], 1)
                    if not first:
                        down(n - 1, 1 - slot)
                    after(pe, s["hT"], n + 1)
                    after(pe, s["gelu"], KH * (n - 1))
                    for j in range(KH):
                        pe.matmul(bank[3 * slot + j][:], w["w1"][:, j * P:(j + 1) * P], k.hT[slot][:], start=True, stop=True).then_inc(s["up"], 1)
                pairs(pe, steps, body)
                down(steps - 1, 1)

            @block.scalar
            def _(act):
                def body(n, slot, first):
                    after(act, s["down"], n - 1)
                    for j in range(KH):
                        after(act, s["up"], KH * n + j + 1)
                        act.activation(G[slot][:, j, :], bank[3 * slot + j][:], ACT.Gelu, bias=w["b1"][:, j:j + 1]).then_inc(s["gelu"], 1)
                pairs(act, steps, body)

            @block.vector
            def _(dve):
                def residual(n):
                    after(dve, s["down"], n + 1)
                    after(dve, s["xb"], n + 1)
                    add_and_stats(dve, k, s, n, 4, bank[7][:, 0:4 * C].rearrange("p (t c) -> p t c", t=4), k.stats, k.aggr)

                def body(n, slot, first):
                    after(dve, s["T"], n + 1)
                    after(dve, s["up"], KH * (n - 1))
                    dve.tensor_scalar(k.hT[slot][:], bank[6][0:C, :], w["g"][:], w["b"][:], ALU.mult, ALU.add).then_inc(s["hT"], 1)
                    if not first:
                        residual(n - 1)
                pairs(dve, steps, body)
                residual(steps - 1)


def raster(t, y):
    return t.rearrange("p (y i v c) -> p y v i c", y=2, i=WS, v=2)[:, y]


def conv_mixer(k, bank):
    nc = k.nc
    s = k.sems("cm", LN_SEMS + "z T hT in p taps acc1 conv ct loc mix bn2 ag2 va2 rs2 z2 zT zTe out diag init")
    with ExitStack() as ctx:
        def sb(name, shape, dt=F32):
            return k.sb("cm_" + name, shape, dt, ctx)

        grid = [sb(f"g{i}", [C, 2, GRID, GRID]) for i in range(2)]
        acc = [sb(f"acc{i}", [C, TOK]) for i in range(2)]
        acc1 = sb("accb", [C, TOK])
        diag = sb("diag", [C, 9, C])
        loc = sb("loc", [P, 2, CI])
        st2, ag2 = sb("st2", [P, 2, 6]), sb("ag2", [P, 2, 2])
        v2, r2 = sb("v2", [P, 2, 1]), sb("r2", [P, 2, 1])
        Z = sb("z", [P, 2, CI])
        ZT = sb("zT", [C, 2, 2, P])

        with nc.Block() as block:
            @block.gpsimd
            def _(pool):
                for i in range(2):
                    last = pool.memset(grid[i][:], 0.0)
                last.then_inc(s["init"], 1)
                for tap in range(9):
                    last = pool.tensor_scalar(diag[:, tap, :], k.ident[0:C, 0:C], k.kconv[:, 1, tap:tap + 1], 0.0, ALU.mult, ALU.add)
                last.then_inc(s["diag"], 1)

                def rstd2(n):
                    after(pool, s["ag2"], n + 1)
                    after(pool, s["z2"], n)
                    pool.tensor_tensor(v2[:], ag2[:, :, 1:2], k.eps[:, 0:2, :], ALU.add).then_inc(s["va2"], 1)
                    after(pool, s["va2"], n + 1)
                    pool.tensor_tensor(r2[:], v2[:], k.minus_half[:, 0:2, :], ALU.pow).then_inc(s["rs2"], 1)

                def body(n, slot, first):
                    normalise(pool, k, s, n, 2, k.Y[slot][:, 0:2, :], k.bout, k.v, k.r, n - 1)
                    if not first:
                        rstd2(n - 1)
                pairs(pool, IMAGES, body)
                rstd2(IMAGES - 1)

            @block.tensor
            def _(pe):
                def mix(n):
                    after(pe, s["loc"], n + 1)
                    after(pe, s["z2"], n)
                    for t in range(2):
                        for j in range(2):
                            last = pe.matmul(bank[4][:, t * CI:(t + 1) * CI], k.mixer[:, j, t * P:(t + 1) * P], loc[:, j, :],
                                             start=(j == 0), stop=(j == 1))
                    last.then_inc(s["mix"], 1)

                def back(n):
                    after(pe, s["z2"], n + 1)
                    after(pe, s["zTe"], n)
                    for j in range(2):
                        for t in range(2):
                            last = pe.transpose(bank[5][0:C, (2 * j + t) * P:(2 * j + t + 1) * P], Z[:, t, j * C:(j + 1) * C], k.ident[:])
                    last.then_inc(s["zT"], 1)

                def out(n):
                    after(pe, s["zTe"], n + 1)
                    after(pe, s["x"], n)
                    after(pe, s["xb"], n + 1)
                    for t in range(2):
                        o = bank[6][:, t * C:(t + 1) * C]
                        pe.matmul(o, k.perm[:], k.X[:, bass.ds(n * 2 + t, 1), :], start=True, stop=False)
                        for j in range(2):
                            last = pe.matmul(o, ZT[:, j, t, :], k.wout[:, j, :], start=False, stop=(j == 1))
                    last.then_inc(s["out"], 1)

                def body(n, slot, first):
                    after(pe, s["y"], n + 1)
                    after(pe, s["hT"], n)
                    for t in range(2):
                        last = pe.transpose(bank[0][0:C, t * P:(t + 1) * P], k.Y[slot][:, t, :], k.ident[:])
                    last.then_inc(s["T"], 1)
                    if not first:
                        mix(n - 1)
                    after(pe, s["hT"], n + 1)
                    after(pe, s["p"], n)
                    for j in range(2):
                        last = pe.matmul(bank[1][0:C, j * TOK:(j + 1) * TOK], k.win[:, j * C:(j + 1) * C], k.hT[slot][:, 0:TOK], start=True, stop=True)
                    last.then_inc(s["in"], 1)
                    if not first:
                        back(n - 1)
                    if first:
                        pe.wait_ge(s["diag"], 1)
                    after(pe, s["p"], n + 1)
                    after(pe, s["acc1"], n)
                    for tap in range(9):
                        y, x = divmod(tap, 3)
                        last = pe.matmul(bank[3][0:C, 0:TOK], diag[:, tap, :], grid[slot][:, 1, y:y + SIDE, x:x + SIDE],
                                         start=(tap == 0), stop=(tap == 8))
                    last.then_inc(s["taps"], 1)
                    if not first:
                        out(n - 1)
                    after(pe, s["conv"], 9 * (n + 1))
                    after(pe, s["acc1"], n + 1)
                    after(pe, s["loc"], n)
                    for half, src in ((0, acc[slot]), (1, acc1)):
                        for j in range(2):
                            last = pe.transpose(bank[2][:, (2 * j + half) * C:(2 * j + half + 1) * C], src[:, j * P:(j + 1) * P], k.ident[0:C, 0:C])
                    last.then_inc(s["ct"], 1)
                pairs(pe, IMAGES, body)
                mix(IMAGES - 1)
                back(IMAGES - 1)
                out(IMAGES - 1)

            @block.scalar
            def _(act):
                act.wait_ge(s["init"], 1)

                def zt(n):
                    after(act, s["zT"], n + 1)
                    after(act, s["out"], n)
                    for j in range(2):
                        last = act.activation(ZT[:, j, :, :], bank[5][0:C, j * 2 * P:(j + 1) * 2 * P].rearrange("p (t q) -> p t q", t=2),
                                              ACT.Identity, bias=k.onb[:, j:j + 1], scale=k.ong[:, j:j + 1])
                    last.then_inc(s["zTe"], 1)

                def body(n, slot, first):
                    after(act, s["T"], n + 1)
                    after(act, s["in"], n - 1)
                    for y in range(2):
                        last = act.activation(raster(k.hT[slot][:, 0:TOK], y), bank[0][0:C, y * P:(y + 1) * P].rearrange("p (v i c) -> p v i c", v=2, i=WS),
                                              ACT.Identity, bias=k.b3[:], scale=k.g3[:])
                    last.then_inc(s["hT"], 1)
                    after(act, s["in"], n + 1)
                    after(act, s["taps"], n - 1)
                    after(act, s["conv"], 9 * (n - 1))
                    for j in range(2):
                        last = act.activation(grid[slot][:, j, 1:1 + SIDE, 1:1 + SIDE],
                                              bank[1][0:C, j * TOK:(j + 1) * TOK].rearrange("p (i c) -> p i c", c=SIDE),
                                              ACT.Identity, bias=k.bin[:, j:j + 1])
                    last.then_inc(s["p"], 1)
                    if not first:
                        zt(n - 1)
                    after(act, s["taps"], n + 1)
                    after(act, s["ct"], n)
                    act.activation(acc1[:], bank[3][0:C, 0:TOK], ACT.Copy).then_inc(s["acc1"], 1)
                    after(act, s["ct"], n + 1)
                    after(act, s["mix"], n)
                    act.activation(loc[:], bank[2][:, 0:2 * CI].rearrange("p (t c) -> p t c", t=2), ACT.Copy).then_inc(s["loc"], 1)
                pairs(act, IMAGES, body)
                zt(IMAGES - 1)

            @block.vector
            def _(dve):
                def norm2(n):
                    after(dve, s["mix"], n + 1)
                    after(dve, s["va2"], n)
                    for t in range(2):
                        last = dve.bn_stats(st2[:, t, :], bank[4][:, t * CI:(t + 1) * CI])
                    last.then_inc(s["bn2"], 1)
                    alone(dve, k)
                    after(dve, s["bn2"], n + 1)
                    for t in range(2):
                        last = dve.bn_aggr(ag2[:, t, :], st2[:, t, :])
                    last.then_inc(s["ag2"], 1)

                def norm2b(n):
                    after(dve, s["rs2"], n + 1)
                    after(dve, s["zT"], n)
                    for t in range(2):
                        last = dve.tensor_scalar(Z[:, t, :], bank[4][:, t * CI:(t + 1) * CI], ag2[:, t, 0:1], r2[:, t, :], ALU.subtract, ALU.mult)
                    last.then_inc(s["z2"], 1)

                def residual(n):
                    after(dve, s["out"], n + 1)
                    after(dve, s["xb"], n + 1)
                    add_and_stats(dve, k, s, n, 2, bank[6][:, 0:2 * C].rearrange("p (t c) -> p t c", t=2), k.stats, k.aggr, replace=True)

                def body(n, slot, first):
                    if not first:
                        norm2(n - 1)
                        norm2b(n - 1)
                    after(dve, s["p"], n + 1)
                    after(dve, s["ct"], n - 1)
                    o = acc[slot][:].rearrange("p (i c) -> p i c", c=SIDE)
                    for tap in range(9):
                        y, x = divmod(tap, 3)
                        src = grid[slot][:, 0, y:y + SIDE, x:x + SIDE]
                        kk = k.kconv[:, 0, tap:tap + 1]
                        if tap == 0:
                            dve.tensor_scalar(o, src, kk, None, ALU.mult).then_inc(s["conv"], 1)
                        else:
                            after(dve, s["conv"], 9 * n + tap)
                            dve.scalar_tensor_tensor(out=o, in0=src, scalar=kk, in1=o, op0=ALU.mult, op1=ALU.add).then_inc(s["conv"], 1)
                    if not first:
                        residual(n - 1)
                pairs(dve, IMAGES, body)
                norm2(IMAGES - 1)
                norm2b(IMAGES - 1)
                residual(IMAGES - 1)


def full_attention(k, bank):
    nc = k.nc
    s = k.sems("fa", LN_SEMS + "init T hT pj e1 e2 sc nm exp rec nrm pt pte av ote out")
    with ExitStack() as ctx:
        def sb(name, shape, dt=F32):
            return k.sb("fa_" + name, shape, dt, ctx)

        qT = [sb(f"q{i}", [P, PAIRS2, TOK]) for i in range(2)]
        kz = [sb(f"kz{i}", [P, H2, TOK]) for i in range(2)]
        V = [sb(f"v{i}", [P, 2, H2, 64]) for i in range(2)]
        nm = [sb(f"nm{i}", [P, 2]) for i in range(2)]
        sm = [sb(f"sm{i}", [P, 2]) for i in range(2)]
        rc = [sb(f"rc{i}", [P, 2]) for i in range(2)]
        E = [sb(f"e{i}", [P, 2, TOK]) for i in range(2)]
        PT = [sb(f"pt{i}", [P, 2, TOK]) for i in range(2)]
        OT = [sb(f"ot{i}", [P, PAIRS2, TOK]) for i in range(2)]
        scale = float(D2) ** -0.5
        U = H2

        with nc.Block() as block:
            @block.gpsimd
            def _(pool):
                for t in kz + V:
                    last = pool.memset(t[:], 0.0)
                last.then_inc(s["init"], 1)

                def body(n, slot, first):
                    normalise(pool, k, s, n, 2, k.Y[slot][:, 0:2, :], k.bp2, k.v, k.r, n - 1)
                pairs(pool, IMAGES, body)

            @block.tensor
            def _(pe):
                def score(n, h, slot):
                    u = U * n + h
                    after(pe, s["exp"], u - 1)
                    for c in range(2):
                        last = pe.matmul(bank[3 + h % 2][:, c * TOK:(c + 1) * TOK], qT[slot][:, h // 2, c * P:(c + 1) * P],
                                         kz[slot][:, h, :], start=True, stop=True)
                    last.then_inc(s["sc"], 1)

                def probs(n, h, slot):
                    u = U * n + h
                    after(pe, s["nrm"], u + 1)
                    after(pe, s["pte"], u - 1)
                    for kc in range(2):
                        for c in range(2):
                            last = pe.transpose(bank[5 + h % 2][:, kc * TOK + c * P:kc * TOK + (c + 1) * P],
                                                E[h % 2][:, c, kc * P:(kc + 1) * P], k.ident[:])
                    last.then_inc(s["pt"], 1)

                def values(n, h, slot):
                    u = U * n + h
                    after(pe, s["pte"], u + 1)
                    if h % 2 == 0:
                        after(pe, s["ote"], PAIRS2 * n + h // 2)
                    for kc in range(2):
                        last = pe.matmul(bank[7][64 * (h % 2):64 * (h % 2) + 64, 0:TOK], V[slot][:, kc, h, :], PT[h % 2][:, kc, :],
                                         start=(kc == 0), stop=(kc == 1))
                    last.then_inc(s["av"], 1)

                def out(n, slot):
                    after(pe, s["ote"], PAIRS2 * (n + 1))
                    for t in range(2):
                        for p in range(PAIRS2):
                            last = pe.matmul(bank[0][:, t * C:(t + 1) * C], OT[slot][:, p, t * P:(t + 1) * P], k.wp2[:, p, :],
                                             start=(p == 0), stop=(p == PAIRS2 - 1))
                    last.then_inc(s["out"], 1)

                def body(n, slot, first):
                    after(pe, s["y"], n + 1)
                    after(pe, s["x"], n - 1)
                    for t in range(2):
                        last = pe.transpose(bank[0][0:C, t * P:(t + 1) * P], k.Y[slot][:, t, :], k.ident[:])
                    last.then_inc(s["T"], 1)
                    after(pe, s["hT"], n + 1)
                    for j in range(6):
                        b = bank[1 + j % 2]
                        after(pe, s["e1"] if j % 2 == 0 else s["e2"], 3 * n + j // 2)
                        for i in range(2):
                            if j < 4:
                                w = (k.wq2 if j < 2 else k.wk2)[:, 2 * (j % 2) + i, :, :].rearrange("c h d -> c (h d)")
                                last = pe.matmul(b[:, i * TOK:(i + 1) * TOK], w, k.hT[slot][:, 0:TOK], start=True, stop=True)
                            elif i == 0:
                                last = pe.matmul(b[:, 0:H2 * D2], k.hT[slot][:, (j - 4) * P:(j - 3) * P], k.wv2[:], start=True, stop=True)
                        last.then_inc(s["pj"], 1)
                    after(pe, s["e1"], 3 * n + 2)
                    after(pe, s["e2"], 3 * n + 2)
                    score(n, 0, slot)
                    if not first:
                        probs(n - 1, 6, 1 - slot)
                        values(n - 1, 6, 1 - slot)
                    score(n, 1, slot)
                    if not first:
                        probs(n - 1, 7, 1 - slot)
                        values(n - 1, 7, 1 - slot)
                    for h in range(2, H2):
                        score(n, h, slot)
                        probs(n, h - 2, slot)
                        if h == 2:
                            after(pe, s["e1"], 3 * n + 3)
                            after(pe, s["e2"], 3 * n + 3)
                            if not first:
                                out(n - 1, 1 - slot)
                        values(n, h - 2, slot)
                pairs(pe, IMAGES, body)
                for h in (6, 7):
                    probs(IMAGES - 1, h, 1)
                    values(IMAGES - 1, h, 1)
                out(IMAGES - 1, 1)

            @block.scalar
            def _(act):
                def exps(n, h):
                    u = U * n + h
                    after(act, s["nm"], u + 1)
                    after(act, s["pt"], u - 1)
                    after(act, s["rec"], u - 1)
                    for c in range(2):
                        last = act.activation(E[h % 2][:, c, :], bank[3 + h % 2][:, c * TOK:(c + 1) * TOK], ACT.Exp,
                                              bias=nm[h % 2][:, c:c + 1], accum_out=sm[h % 2][:, c:c + 1])
                    last.then_inc(s["exp"], 1)

                def pt_out(n, h):
                    u = U * n + h
                    after(act, s["pt"], u + 1)
                    after(act, s["av"], u - 1)
                    act.activation(PT[h % 2][:], bank[5 + h % 2][:].rearrange("p (a b) -> p a b", a=2), ACT.Copy).then_inc(s["pte"], 1)

                def body(n, slot, first):
                    after(act, s["T"], n + 1)
                    after(act, s["pj"], 6 * (n - 1))
                    act.activation(k.hT[slot][:, 0:TOK], bank[0][0:C, 0:TOK], ACT.Copy).then_inc(s["hT"], 1)
                    after(act, s["pj"], 6 * n + 1)
                    after(act, s["sc"], U * (n - 1))
                    act.activation(qT[slot][:, 0:2, :], bank[1][:].rearrange("p (a b) -> p a b", a=2), ACT.Copy, scale=scale).then_inc(s["e1"], 1)
                    if first:
                        act.wait_ge(s["init"], 1)
                    after(act, s["pj"], 6 * n + 3)
                    for r in range(2):
                        last = act.activation(kz[slot][64 * r:64 * r + 64, r:4:2, :],
                                              bank[1][64 * r:64 * r + 64, :].rearrange("p (a b) -> p a b", a=2), ACT.Copy)
                    last.then_inc(s["e1"], 1)
                    after(act, s["pj"], 6 * n + 5)
                    after(act, s["av"], U * (n - 1))
                    act.activation(V[slot][:, 0, :, 0:D2], bank[1][:, 0:H2 * D2].rearrange("p (h d) -> p h d", d=D2), ACT.Copy).then_inc(s["e1"], 1)
                    if not first:
                        pt_out(n - 1, 6)
                    exps(n, 0)
                    if not first:
                        pt_out(n - 1, 7)
                    exps(n, 1)
                    for h in range(2, H2):
                        pt_out(n, h - 2)
                        exps(n, h)
                pairs(act, IMAGES, body)
                pt_out(IMAGES - 1, 6)
                pt_out(IMAGES - 1, 7)

            @block.vector
            def _(dve):
                def maxima(n, h):
                    u = U * n + h
                    after(dve, s["sc"], u + 1)
                    after(dve, s["exp"], u - 1)
                    dve.tensor_reduce(nm[h % 2][:], bank[3 + h % 2][:].rearrange("p (a b) -> p a b", a=2), AX.X, ALU.max, negate=True).then_inc(s["nm"], 1)

                def norm(n, h):
                    u = U * n + h
                    after(dve, s["exp"], u + 1)
                    after(dve, s["nrm"], u - 1)
                    dve.reciprocal(rc[h % 2][:], sm[h % 2][:]).then_inc(s["rec"], 1)
                    after(dve, s["rec"], u + 1)
                    for c in range(2):
                        last = dve.tensor_scalar(E[h % 2][:, c, :], E[h % 2][:, c, :], rc[h % 2][:, c:c + 1], None, ALU.mult)
                    last.then_inc(s["nrm"], 1)

                def head_out(n, h, slot):
                    if h % 2:
                        after(dve, s["av"], U * n + h + 1)
                        after(dve, s["out"], n - 1)
                        dve.tensor_copy(OT[slot][:, h // 2, :], bank[7][:, 0:TOK]).then_inc(s["ote"], 1)

                def residual(n):
                    after(dve, s["out"], n + 1)
                    after(dve, s["xb"], n + 1)
                    add_and_stats(dve, k, s, n, 2, bank[0][:, 0:2 * C].rearrange("p (t c) -> p t c", t=2), k.stats, k.aggr)

                def body(n, slot, first):
                    after(dve, s["pj"], 6 * n + 2)
                    after(dve, s["sc"], U * (n - 1))
                    dve.tensor_scalar(qT[slot][:, 2:4, :], bank[2][:].rearrange("p (a b) -> p a b", a=2), scale, None, ALU.mult).then_inc(s["e2"], 1)
                    if first:
                        dve.wait_ge(s["init"], 1)
                    after(dve, s["pj"], 6 * n + 4)
                    for r in range(2):
                        last = dve.tensor_copy(kz[slot][64 * r:64 * r + 64, 4 + r:8:2, :],
                                               bank[2][64 * r:64 * r + 64, :].rearrange("p (a b) -> p a b", a=2))
                    last.then_inc(s["e2"], 1)
                    after(dve, s["pj"], 6 * n + 6)
                    after(dve, s["av"], U * (n - 1))
                    dve.tensor_copy(V[slot][:, 1, :, 0:D2], bank[2][:, 0:H2 * D2].rearrange("p (h d) -> p h d", d=D2)).then_inc(s["e2"], 1)
                    if not first:
                        norm(n - 1, 7)
                    maxima(n, 0)
                    if not first:
                        head_out(n - 1, 6, 1 - slot)
                    maxima(n, 1)
                    norm(n, 0)
                    if not first:
                        head_out(n - 1, 7, 1 - slot)
                    for h in range(2, H2):
                        maxima(n, h)
                        norm(n, h - 1)
                        if h == 2 and not first:
                            residual(n - 1)
                        head_out(n, h - 2, slot)
                pairs(dve, IMAGES, body)
                norm(IMAGES - 1, 7)
                head_out(IMAGES - 1, 6, 1)
                head_out(IMAGES - 1, 7, 1)
                residual(IMAGES - 1)


def binary_ffn(k, bank):
    nc = k.nc
    s = k.sems("bf", LN_SEMS + "sum mean gt lt sg tw twe T hT up h am ar1 c1 clip gelu down z am2 ar2 c2 zc q2 tmp")
    with ExitStack() as ctx:
        def sb(name, shape, dt=F32):
            return k.sb("bf_" + name, shape, dt, ctx)

        w1T = sb("w1T", [C, HID])
        w2T = sb("w2T", [P, KH, C])
        part = sb("part", [P, 2, GROUPS])
        mean = sb("mean", [P, 2, GROUPS])
        lt1, lt2 = sb("lt1", [k.g76, GROUPS, C]), sb("lt2", [k.g19, GROUPS, HID])
        gt1, gt2 = sb("gt1", [k.g76, GROUPS, C]), sb("gt2", [k.g19, GROUPS, HID])
        Y = sb("Y", [P, GT, C])
        hT = sb("hT", [C, GT * P])
        Hh = sb("H", [P, KH, GT * P])
        Z = sb("Z", [P, GT, C])
        am, ar, cc = sb("am", [P, 2]), sb("ar", [P, 2]), sb("cc", [P, 2, 4])
        half = GT * P // 2
        MAX = bass.bass_isa.ReduceOp.max
        mats = ((k.g76, k.f1, C, gt1, lt1), (k.g19, k.f2, HID, gt2, lt2))

        def scales(dve, i, g, src, done):
            after(dve, s[src], g + 1)
            dve.tensor_scalar(cc[:, i, 3:4], ar[:, i:i + 1], EPS_Q, None, ALU.add).then_inc(s["tmp"], 1)
            after(dve, s["tmp"], 4 * g + 2 * i + 1)
            dve.reciprocal(cc[:, i, 0:1], cc[:, i, 3:4]).then_inc(s["tmp"], 1)
            dve.tensor_scalar(cc[:, i, 1:2], cc[:, i, 3:4], (QB - EPS_Q) / QB, None, ALU.mult)
            dve.tensor_scalar(cc[:, i, 2:3], cc[:, i, 3:4], -(QB - EPS_Q) / QB, None, ALU.mult)
            after(dve, s["tmp"], 4 * g + 2 * i + 2)
            dve.tensor_scalar(cc[:, i, 0:1], cc[:, i, 0:1], QB, None, ALU.mult).then_inc(s[done], 1)

        with nc.Block() as block:
            @block.gpsimd
            def _(pool):
                pool.memset(w1T[:], 0.0)
                pool.memset(w2T[:], 0.0).then_inc(s["twe"], 1)

                def body(g):
                    normalise(pool, k, s, g, GT, Y[:], None, k.v, k.r, g)
                    alone(pool, k)
                    after(pool, s["am"], g + 1)
                    after(pool, s["c1"], g)
                    pool.partition_all_reduce(ar[:, 0:1], am[:, 0:1], P, MAX).then_inc(s["ar1"], 1)
                    alone(pool, k)
                    after(pool, s["am2"], g + 1)
                    after(pool, s["c2"], g)
                    pool.partition_all_reduce(ar[:, 1:2], am[:, 1:2], P, MAX).then_inc(s["ar2"], 1)
                body(0)
                with pool.Fori(1, GROUPS) as g:
                    body(g)

            @block.tensor
            def _(pe):
                pe.wait_ge(s["sum"], 2)
                for i, (n, w, cols, gt, lt) in enumerate(mats):
                    last = pe.matmul(bank[0][:, i * GROUPS:(i + 1) * GROUPS], k.ones[0:n, :], part[0:n, i, :], start=True, stop=True)
                last.then_inc(s["mean"], 1)
                pe.wait_ge(s["sg"], 2)
                for g in range(GROUPS):
                    last = pe.transpose(bank[1][0:C, g * k.g76:(g + 1) * k.g76], gt1[:, g, :], k.ident[0:k.g76, 0:k.g76])
                    for j in range(KH):
                        last = pe.transpose(bank[2][:, j * P + g * k.g19:j * P + (g + 1) * k.g19], gt2[:, g, j * P:(j + 1) * P], k.ident[0:k.g19, 0:k.g19])
                last.then_inc(s["tw"], 1)
                pe.wait_ge(s["twe"], 3)

                def body(g):
                    after(pe, s["y"], g + 1)
                    after(pe, s["hT"], g)
                    for t in range(GT):
                        last = pe.transpose(bank[t // 3][0:C, (t % 3) * P:(t % 3 + 1) * P], Y[:, t, :], k.ident[:])
                    last.then_inc(s["T"], 1)
                    after(pe, s["hT"], g + 1)
                    for j in range(KH):
                        for i in range(2):
                            u = 2 * j + i
                            after(pe, s["h"], 6 * g + u - 3)
                            pe.matmul(bank[2 + u % 4][:, 0:half], w1T[:, j * P:(j + 1) * P], hT[:, i * half:(i + 1) * half], start=True, stop=True).then_inc(s["up"], 1)
                    after(pe, s["gelu"], KH * (g + 1))
                    after(pe, s["z"], 2 * g)
                    for t in range(GT):
                        for j in range(KH):
                            last = pe.matmul(bank[6 + t // 3][:, (t % 3) * C:(t % 3 + 1) * C], Hh[:, j, t * P:(t + 1) * P], w2T[:, j, :],
                                             start=(j == 0), stop=(j == KH - 1))
                    last.then_inc(s["down"], 1)
                body(0)
                with pe.Fori(1, GROUPS) as g:
                    body(g)

            @block.scalar
            def _(act):
                def body(g):
                    after(act, s["T"], g + 1)
                    after(act, s["up"], 6 * g)
                    for i in range(2):
                        last = act.activation(hT[:, i * half:(i + 1) * half], bank[i][0:C, 0:half], ACT.Copy)
                    last.then_inc(s["hT"], 1)
                    after(act, s["down"], g)
                    for j in range(KH):
                        for i in range(2):
                            u = 2 * j + i
                            after(act, s["up"], 6 * g + u + 1)
                            act.activation(Hh[:, j, i * half:(i + 1) * half], bank[2 + u % 4][:, 0:half], ACT.Identity, bias=k.fb1[:, j:j + 1]).then_inc(s["h"], 1)
                    for j in range(KH):
                        after(act, s["clip"], KH * g + j + 1)
                        act.activation(Hh[:, j, :], Hh[:, j, :], ACT.Gelu, scale=cc[:, 0, 0:1]).then_inc(s["gelu"], 1)
                body(0)
                with act.Fori(1, GROUPS) as g:
                    body(g)

            @block.vector
            def _(dve):
                for i, (n, w, cols, gt, lt) in enumerate(mats):
                    dve.tensor_reduce(part[0:n, i, :], w[:], AX.X, ALU.add).then_inc(s["sum"], 1)
                dve.wait_ge(s["mean"], 1)
                for i, (n, w, cols, gt, lt) in enumerate(mats):
                    dve.tensor_scalar(mean[:, i, :], bank[0][:, i * GROUPS:(i + 1) * GROUPS], 1.0 / (n * cols), None, ALU.mult).then_inc(s["gt"], 1)
                dve.wait_ge(s["gt"], 2)
                for i, (n, w, cols, gt, lt) in enumerate(mats):
                    m = mean[0:n, i, :, None].broadcast_to([n, GROUPS, cols])
                    dve.tensor_tensor(gt[:], w[:], m, ALU.is_gt).then_inc(s["gt"], 1)
                    dve.tensor_tensor(lt[:], w[:], m, ALU.is_lt).then_inc(s["lt"], 1)
                dve.wait_ge(s["gt"], 4)
                dve.wait_ge(s["lt"], 2)
                for i, (n, w, cols, gt, lt) in enumerate(mats):
                    dve.tensor_tensor(gt[:], gt[:], lt[:], ALU.subtract).then_inc(s["sg"], 1)
                dve.wait_ge(s["tw"], 1)
                dve.wait_ge(s["twe"], 1)
                dve.tensor_copy(w1T[:, 0:GROUPS * k.g76], bank[1][0:C, 0:GROUPS * k.g76]).then_inc(s["twe"], 1)
                dve.tensor_copy(w2T[:, :, 0:GROUPS * k.g19], bank[2][:, 0:KH * P].rearrange("p (j c) -> p j c", j=KH)[:, :, 0:GROUPS * k.g19]).then_inc(s["twe"], 1)

                def body(g):
                    after(dve, s["h"], 6 * (g + 1))
                    after(dve, s["ar1"], g)
                    dve.tensor_reduce(am[:, 0:1], Hh[:], AX.XY, ALU.max, apply_absolute_value=True).then_inc(s["am"], 1)
                    after(dve, s["gelu"], KH * g)
                    scales(dve, 0, g, "ar1", "c1")
                    after(dve, s["c1"], g + 1)
                    for j in range(KH):
                        dve.tensor_scalar(Hh[:, j, :], Hh[:, j, :], cc[:, 0, 1:2], cc[:, 0, 2:3], ALU.min, ALU.max).then_inc(s["clip"], 1)
                    after(dve, s["down"], g + 1)
                    for b in range(2):
                        dve.tensor_tensor(Z[:, 3 * b:3 * b + 3, :], bank[6 + b][:, 0:3 * C].rearrange("p (t c) -> p t c", t=3),
                                          k.fb2[:, None, :].broadcast_to([P, 3, C]), ALU.add).then_inc(s["z"], 1)
                    after(dve, s["z"], 2 * (g + 1))
                    after(dve, s["ar2"], g)
                    dve.tensor_reduce(am[:, 1:2], Z[:], AX.XY, ALU.max, apply_absolute_value=True).then_inc(s["am2"], 1)
                    scales(dve, 1, g, "ar2", "c2")
                    after(dve, s["c2"], g + 1)
                    dve.tensor_scalar(Z[:], Z[:], cc[:, 1, 1:2], cc[:, 1, 2:3], ALU.min, ALU.max).then_inc(s["zc"], 1)
                    after(dve, s["zc"], g + 1)
                    dve.tensor_scalar(Z[:], Z[:], cc[:, 1, 0:1], None, ALU.mult).then_inc(s["q2"], 1)
                    after(dve, s["q2"], g + 1)
                    after(dve, s["y"], g + 1)
                    add_and_stats(dve, k, s, g, GT, Z[:], k.stats, k.aggr)
                body(0)
                with dve.Fori(1, GROUPS) as g:
                    body(g)


def causal_attention(k, bank):
    nc = k.nc
    s = k.sems("ca", LN_SEMS + "T hT pj e qx kv vt v sc nm exp rec nrm pt pte av ote out")
    with ExitStack() as ctx:
        def sb(name, shape, dt=F32):
            return k.sb("ca_" + name, shape, dt, ctx)

        ROWS = TOK * H3
        qx = [sb(f"qx{i}", [C, TOK, H3]) for i in range(2)]
        kv = [sb(f"kv{i}", [C + D3, TOK, H3]) for i in range(2)]
        V = [sb(f"v{i}", [P, 2 * H3, H3, D3]) for i in range(2)]
        nm = [sb(f"nm{i}", [P, 2]) for i in range(2)]
        sm = [sb(f"sm{i}", [P, 2]) for i in range(2)]
        rc = [sb(f"rc{i}", [P, 2]) for i in range(2)]
        E = [sb(f"e{i}", [P, 3, P]) for i in range(2)]
        PT = [sb(f"pt{i}", [P, 3, P]) for i in range(2)]
        OT = [sb(f"ot{i}", [C, ROWS]) for i in range(2)]
        parts = ((0, 0, 1), (1, 1, 3))
        U = H3

        with nc.Block() as block:
            @block.gpsimd
            def _(pool):
                def body(n, slot, first):
                    normalise(pool, k, s, n, 2, k.Y[slot][:, 0:2, :], k.bp3, k.v, k.r, n - 1)
                pairs(pool, IMAGES, body)

            @block.tensor
            def _(pe):
                def score(n, h, slot):
                    u = U * n + h
                    b = bank[4 + h % 2]
                    q = qx[slot][:].rearrange("p t g -> p (t g)")
                    kk = kv[slot][:].rearrange("p t g -> p (t g)")
                    after(pe, s["exp"], u - 1)
                    pe.matmul(b[:, 0:P], q[:, h * TOK:h * TOK + P], kk[0:C, h * TOK:h * TOK + P], start=True, stop=False, skip_group_check=True)
                    pe.matmul(b[:, P:3 * P], q[:, h * TOK + P:(h + 1) * TOK], kk[0:C, h * TOK:(h + 1) * TOK], start=False, stop=False, skip_group_check=True)
                    pe.matmul(b[:].rearrange("p (a c) -> p a c", a=2)[:, :, 0:P], k.identb[:], k.causal[:, None, :].broadcast_to([P, 2, P]),
                              start=False, stop=True, skip_group_check=True).then_inc(s["sc"], 1)

                def probs(n, h):
                    u = U * n + h
                    after(pe, s["nrm"], u + 1)
                    after(pe, s["pte"], u - 1)
                    for i in range(3):
                        last = pe.transpose(bank[6 + h % 2][:, i * P:(i + 1) * P], E[h % 2][:, i, :], k.ident[:])
                    last.then_inc(s["pt"], 1)

                def values(n, h, slot):
                    u = U * n + h
                    after(pe, s["pte"], u + 1)
                    after(pe, s["ote"], u)
                    for kc in range(2):
                        w = V[slot][:, 2 * h + kc, :, :].rearrange("p g d -> p (g d)")
                        last = pe.matmul(bank[3][0:C, kc * P:TOK], w, PT[h % 2][:, 2 * kc:2 + kc, :], start=(kc == 0), stop=(kc == 1), skip_group_check=True)
                    last.then_inc(s["av"], 1)

                def out(n, slot):
                    after(pe, s["ote"], U * (n + 1))
                    o = OT[slot][:].rearrange("p (y t g) -> p y g t", y=2, g=H3)
                    for t in range(2):
                        for g in range(H3):
                            last = pe.matmul(bank[0][:, t * C:(t + 1) * C], o[:, t, g], k.wp3[:, g, :], start=(g == 0), stop=(g == H3 - 1))
                    last.then_inc(s["out"], 1)

                def body(n, slot, first):
                    after(pe, s["y"], n + 1)
                    after(pe, s["x"], n - 1)
                    for t in range(2):
                        last = pe.transpose(bank[0][0:C, t * P:(t + 1) * P], k.Y[slot][:, t, :], k.ident[:])
                    last.then_inc(s["T"], 1)
                    after(pe, s["hT"], n + 1)
                    after(pe, s["e"], 3 * n - 1)
                    pe.matmul(bank[1][0:C, 0:TOK], k.wq3[:], k.hT[slot][:, 0:TOK], start=True, stop=True).then_inc(s["pj"], 1)
                    for j in range(3):
                        b = bank[1 + (j + 1) % 2]
                        if j == 0:
                            after(pe, s["e"], 3 * n)
                        elif j == 1:
                            after(pe, s["qx"], n + 1)
                        else:
                            after(pe, s["e"], 3 * n + 1)
                        for i in range(2):
                            last = pe.matmul(b[0:C + D3, i * TOK:(i + 1) * TOK], k.wkv3[:, 2 * j + i, :], k.hT[slot][:, 0:TOK], start=True, stop=True)
                        last.then_inc(s["pj"], 1)
                    if not first:
                        probs(n - 1, U - 2)
                        values(n - 1, U - 2, 1 - slot)
                    after(pe, s["e"], 3 * (n + 1))
                    score(n, 0, slot)
                    if not first:
                        probs(n - 1, U - 1)
                        values(n - 1, U - 1, 1 - slot)
                    score(n, 1, slot)
                    kk = kv[slot][:].rearrange("p t g -> p (t g)")
                    for j in range(2 * H3):
                        last = pe.transpose(bank[0][:, 256 + j * D3:256 + (j + 1) * D3], kk[C:C + D3, j * P:(j + 1) * P], k.ident[C:C + D3, C:C + D3])
                    last.then_inc(s["vt"], 1)
                    for h in range(2, U):
                        score(n, h, slot)
                        probs(n, h - 2)
                        if h == 2:
                            after(pe, s["v"], n + 1)
                            if not first:
                                out(n - 1, 1 - slot)
                        values(n, h - 2, slot)
                pairs(pe, IMAGES, body)
                for h in (U - 2, U - 1):
                    probs(IMAGES - 1, h)
                    values(IMAGES - 1, h, 1)
                out(IMAGES - 1, 1)

            @block.scalar
            def _(act):
                def exps(n, h):
                    u = U * n + h
                    after(act, s["nm"], u + 1)
                    after(act, s["pt"], u - 1)
                    after(act, s["rec"], u - 1)
                    for c, lo, hi in parts:
                        last = act.activation(E[h % 2][:, lo:hi, :], bank[4 + h % 2][:, lo * P:hi * P].rearrange("p (a b) -> p a b", b=P), ACT.Exp,
                                              bias=nm[h % 2][:, c:c + 1], accum_out=sm[h % 2][:, c:c + 1])
                    last.then_inc(s["exp"], 1)

                def pt_out(n, h):
                    u = U * n + h
                    after(act, s["pt"], u + 1)
                    after(act, s["av"], u - 1)
                    act.activation(PT[h % 2][:], bank[6 + h % 2][:, 0:3 * P].rearrange("p (a b) -> p a b", b=P), ACT.Copy).then_inc(s["pte"], 1)

                def body(n, slot, first):
                    after(act, s["T"], n + 1)
                    after(act, s["pj"], 4 * (n - 1))
                    act.activation(k.hT[slot][:, 0:TOK], bank[0][0:C, 0:TOK], ACT.Copy).then_inc(s["hT"], 1)
                    after(act, s["sc"], U * (n - 1))
                    for j in range(3):
                        after(act, s["pj"], 4 * n + j + 2)
                        act.activation(kv[slot][:].rearrange("p t g -> p g t")[:, 2 * j:2 * j + 2, :],
                                       bank[1 + (j + 1) % 2][0:C + D3, :].rearrange("p (g t) -> p g t", g=2), ACT.Copy).then_inc(s["e"], 1)
                    if not first:
                        pt_out(n - 1, U - 2)
                    exps(n, 0)
                    if not first:
                        pt_out(n - 1, U - 1)
                    exps(n, 1)
                    for h in range(2, U):
                        pt_out(n, h - 2)
                        exps(n, h)
                pairs(act, IMAGES, body)
                pt_out(IMAGES - 1, U - 2)
                pt_out(IMAGES - 1, U - 1)

            @block.vector
            def _(dve):
                def maxima(n, h):
                    u = U * n + h
                    after(dve, s["sc"], u + 1)
                    after(dve, s["exp"], u - 1)
                    for c, lo, hi in parts:
                        last = dve.tensor_reduce(nm[h % 2][:, c:c + 1], bank[4 + h % 2][:, lo * P:hi * P], AX.X, ALU.max, negate=True)
                    last.then_inc(s["nm"], 1)

                def norm(n, h):
                    u = U * n + h
                    after(dve, s["exp"], u + 1)
                    after(dve, s["nrm"], u - 1)
                    dve.reciprocal(rc[h % 2][:], sm[h % 2][:]).then_inc(s["rec"], 1)
                    after(dve, s["rec"], u + 1)
                    for c, lo, hi in parts:
                        last = dve.tensor_scalar(E[h % 2][:, lo:hi, :], E[h % 2][:, lo:hi, :], rc[h % 2][:, c:c + 1], None, ALU.mult)
                    last.then_inc(s["nrm"], 1)

                def head_out(n, h, slot):
                    after(dve, s["av"], U * n + h + 1)
                    after(dve, s["out"], n - 1)
                    dve.tensor_copy(OT[slot][:, h * TOK:(h + 1) * TOK], bank[3][0:C, 0:TOK]).then_inc(s["ote"], 1)

                def residual(n):
                    after(dve, s["out"], n + 1)
                    after(dve, s["xb"], n + 1)
                    add_and_stats(dve, k, s, n, 2, bank[0][:, 0:2 * C].rearrange("p (t c) -> p t c", t=2), k.stats, k.aggr)

                def body(n, slot, first):
                    after(dve, s["pj"], 4 * n + 1)
                    after(dve, s["sc"], U * (n - 1))
                    dve.tensor_tensor(qx[slot][:], bank[1][0:C, 0:TOK, None].broadcast_to([C, TOK, H3]),
                                      k.groupmask[:, None, :].broadcast_to([C, TOK, H3]), ALU.mult).then_inc(s["qx"], 1)
                    if not first:
                        norm(n - 1, U - 1)
                        head_out(n - 1, U - 2, 1 - slot)
                    maxima(n, 0)
                    if not first:
                        head_out(n - 1, U - 1, 1 - slot)
                    maxima(n, 1)
                    norm(n, 0)
                    after(dve, s["vt"], n + 1)
                    after(dve, s["av"], U * (n - 1))
                    dve.tensor_copy(V[slot][:], bank[0][:, 256:256 + 2 * H3 * D3].rearrange("p (j d) -> p j d", d=D3)[:, :, None, :]
                                    .broadcast_to([P, 2 * H3, H3, D3])).then_inc(s["v"], 1)
                    for h in range(2, U):
                        maxima(n, h)
                        norm(n, h - 1)
                        if h == 2 and not first:
                            residual(n - 1)
                        head_out(n, h - 2, slot)
                pairs(dve, IMAGES, body)
                norm(IMAGES - 1, U - 1)
                head_out(IMAGES - 1, U - 2, 1)
                head_out(IMAGES - 1, U - 1, 1)
                residual(IMAGES - 1)


def experts(k, bank, out):
    nc = k.nc
    s = k.sems("ex", LN_SEMS + "T hT keep gl lb mx sub exp sum rec pr cmp rank m rd up gelu down acc b2 xo st g1 g2 gd g3 g4 g5")
    steps = TILES // 4
    with ExitStack() as ctx:
        def sb(name, shape, dt=F32):
            return k.sb("ex_" + name, shape, dt, ctx)

        HT = sb("HT", [C, steps, 512])
        L = sb("L", [P, TILES, EXPERTS])
        one = sb("one", [P, TILES, 1])
        ge = sb("ge", [P, TILES, EXPERTS, EXPERTS])
        gt = sb("gt", [P, TILES, EXPERTS, EXPERTS])
        rank = sb("rank", [P, TILES, EXPERTS])
        tmp = [sb(f"tmp{i}", [P, 4, C]) for i in range(2)]
        G = [sb(f"G{i}", [P, KH, 512]) for i in range(2)]
        full = [P, TILES, EXPERTS]

        with nc.Block() as block:
            @block.gpsimd
            def _(pool):
                def body(n, slot, first):
                    normalise(pool, k, s, n, 4, k.Y[slot][:], None, k.v, k.r, n - 1)
                    after(pool, s["hT"], n + 1)
                    pool.tensor_copy(HT[:, bass.ds(n, 1), :], k.hT[slot][:, None, :]).then_inc(s["keep"], 1)
                pairs(pool, steps, body)

            @block.tensor
            def _(pe):
                def body(n, slot, first):
                    after(pe, s["y"], n + 1)
                    after(pe, s["hT"], n - 1)
                    for t in range(4):
                        last = pe.transpose(bank[slot][0:C, t * P:(t + 1) * P], k.Y[slot][:, t, :], k.ident[:])
                    last.then_inc(s["T"], 1)
                    after(pe, s["hT"], n + 1)
                    after(pe, s["lb"], n - 1)
                    for t in range(4):
                        last = pe.matmul(bank[2 + slot][:, t * EXPERTS:(t + 1) * EXPERTS], k.hT[slot][:, t * P:(t + 1) * P], k.gw[:], start=True, stop=True)
                    last.then_inc(s["gl"], 1)
                pairs(pe, steps, body)

            @block.scalar
            def _(act):
                def body(n, slot, first):
                    after(act, s["T"], n + 1)
                    after(act, s["gl"], n - 1)
                    after(act, s["keep"], n - 1)
                    act.activation(k.hT[slot][:], bank[slot][0:C, :], ACT.Copy).then_inc(s["hT"], 1)
                pairs(act, steps, body)
                act.wait_ge(s["sub"], 1)
                act.activation(L[:], L[:], ACT.Exp).then_inc(s["exp"], 1)

            @block.vector
            def _(dve):
                def body(n, slot, first):
                    after(dve, s["gl"], n + 1)
                    dve.tensor_tensor(tiles_of(L, n * 4, 4), bank[2 + slot][:, 0:4 * EXPERTS].rearrange("p (t e) -> p t e", e=EXPERTS),
                                      k.gb[:, None, :].broadcast_to([P, 4, EXPERTS]), ALU.add).then_inc(s["lb"], 1)
                pairs(dve, steps, body)
                dve.wait_ge(s["lb"], steps)
                dve.tensor_reduce(one[:, :, 0], L[:], AX.X, ALU.max).then_inc(s["mx"], 1)
                dve.wait_ge(s["mx"], 1)
                dve.tensor_tensor(L[:], L[:], one[:].broadcast_to(full), ALU.subtract).then_inc(s["sub"], 1)
                dve.wait_ge(s["exp"], 1)
                dve.tensor_reduce(one[:, :, 0], L[:], AX.X, ALU.add).then_inc(s["sum"], 1)
                dve.wait_ge(s["sum"], 1)
                dve.reciprocal(one[:], one[:]).then_inc(s["rec"], 1)
                dve.wait_ge(s["rec"], 1)
                dve.tensor_tensor(L[:], L[:], one[:].broadcast_to(full), ALU.mult).then_inc(s["pr"], 1)
                dve.wait_ge(s["pr"], 1)
                square = [P, TILES, EXPERTS, EXPERTS]
                other, own = L[:, :, None, :].broadcast_to(square), L[:, :, :, None].broadcast_to(square)
                dve.tensor_tensor(ge[:], other, own, ALU.is_ge).then_inc(s["cmp"], 1)
                dve.tensor_tensor(gt[:], other, own, ALU.is_gt).then_inc(s["cmp"], 1)
                dve.wait_ge(s["cmp"], 2)
                dve.tensor_tensor(ge[:], ge[:], k.lower[:, None, :, :].broadcast_to(square), ALU.mult).then_inc(s["cmp"], 1)
                dve.wait_ge(s["cmp"], 3)
                dve.tensor_tensor(gt[:], gt[:], ge[:], ALU.max).then_inc(s["cmp"], 1)
                dve.wait_ge(s["cmp"], 4)
                dve.tensor_reduce(rank[:], gt[:], AX.X, ALU.add).then_inc(s["rank"], 1)
                dve.wait_ge(s["rank"], 1)
                dve.tensor_scalar(rank[:], rank[:], 2.0, None, ALU.is_lt).then_inc(s["rank"], 1)
                dve.wait_ge(s["rank"], 2)
                dve.tensor_tensor(L[:], L[:], rank[:], ALU.mult).then_inc(s["m"], 1)
                dve.wait_ge(s["m"], 1)
                dve.tensor_reduce(one[:, :, 0], L[:], AX.X, ALU.add).then_inc(s["g1"], 1)
                dve.wait_ge(s["g1"], 1)
                dve.tensor_scalar(one[:], one[:], 1e-9, None, ALU.add).then_inc(s["g2"], 1)
                dve.wait_ge(s["g2"], 1)
                dve.reciprocal(one[:], one[:]).then_inc(s["gd"], 1)
                dve.wait_ge(s["gd"], 1)
                dve.tensor_tensor(L[:], L[:], one[:].broadcast_to(full), ALU.mult).then_inc(s["m"], 1)

        with nc.Block() as block:
            @block.gpsimd
            def _(pool):
                def body(n, slot, first):
                    own = tiles_of(L, n * 4, 4)
                    b = k.eb2[:, :, None, :]
                    wide = [P, 4, C]
                    after(pool, s["xb"], n)
                    pool.tensor_tensor(tmp[0][:], b[:, 0].broadcast_to(wide), own[:, :, 0:1].broadcast_to(wide), ALU.mult).then_inc(s["g4"], 1)
                    for e in range(1, EXPERTS):
                        u = (EXPERTS - 1) * n + e
                        after(pool, s["g5"], u - 1)
                        pool.tensor_tensor(tmp[1][:], b[:, e].broadcast_to(wide), own[:, :, e:e + 1].broadcast_to(wide), ALU.mult).then_inc(s["g3"], 1)
                        after(pool, s["g4"], n + 1)
                        after(pool, s["g3"], u)
                        pool.tensor_tensor(tmp[0][:], tmp[0][:], tmp[1][:], ALU.add).then_inc(s["g5"], 1)
                    x = tiles_of(k.X, n * 4, 4)
                    alone(pool, k)
                    after(pool, s["g5"], (EXPERTS - 1) * (n + 1))
                    pool.tensor_tensor(x, x, tmp[0][:], ALU.add).then_inc(s["xb"], 1)
                pairs(pool, steps, body)

            @block.tensor
            def _(pe):
                def down(n, e):
                    u = EXPERTS * n + e
                    after(pe, s["gelu"], KH * (u + 1))
                    after(pe, s["acc"], 4 * (u - 1))
                    for t in range(4):
                        for j in range(KH):
                            last = pe.matmul(bank[6 + e % 2][:, t * C:(t + 1) * C], G[e % 2][:, j, t * P:(t + 1) * P], k.ew2[:, e, j, :],
                                             start=(j == 0), stop=(j == KH - 1))
                    last.then_inc(s["down"], 1)

                def body(n, first):
                    for e in range(EXPERTS):
                        u = EXPERTS * n + e
                        after(pe, s["gelu"], KH * (u - 1))
                        for j in range(KH):
                            pe.matmul(bank[3 * (e % 2) + j][:], k.ew1[:, e, j * P:(j + 1) * P], HT[:, bass.ds(n, 1), :], start=True, stop=True).then_inc(s["up"], 1)
                        if e:
                            down(n, e - 1)
                        elif not first:
                            down(n - 1, EXPERTS - 1)
                body(0, True)
                with pe.Fori(1, steps) as n:
                    body(n, False)
                down(steps - 1, EXPERTS - 1)

            @block.scalar
            def _(act):
                def body(n):
                    for e in range(EXPERTS):
                        u = EXPERTS * n + e
                        after(act, s["down"], u - 1)
                        for j in range(KH):
                            after(act, s["up"], KH * u + j + 1)
                            act.activation(G[e % 2][:, j, :], bank[3 * (e % 2) + j][:], ACT.Gelu, bias=k.eb1[:, e, j:j + 1]).then_inc(s["gelu"], 1)
                body(0)
                with act.Fori(1, steps) as n:
                    body(n)

            @block.vector
            def _(dve):
                def body(n):
                    after(dve, s["xb"], n + 1)
                    for e in range(EXPERTS):
                        u = EXPERTS * n + e
                        after(dve, s["down"], u + 1)
                        after(dve, s["acc"], 4 * u)
                        for t in range(4):
                            x = k.X[:, bass.ds(n * 4 + t, 1), :]
                            dve.scalar_tensor_tensor(out=x, in0=bank[6 + e % 2][:, None, t * C:(t + 1) * C], scalar=L[:, bass.ds(n * 4 + t, 1), e],
                                                     in1=x, op0=ALU.mult, op1=ALU.add).then_inc(s["acc"], 1)
                body(0)
                with dve.Fori(1, steps) as n:
                    body(n)

            @block.sync
            def _(sp):
                sp.wait_ge(s["acc"], 4 * EXPERTS * steps)
                sp.dma_start(out.rearrange("b (y i) c d -> (i c) (b y) d", y=2), k.X[:]).then_inc(s["st"], 16)
                sp.wait_ge(s["st"], 16)


def build(nc, a, out, upto=99):
    with ExitStack() as ctx:
        k = Core(nc, ctx)
        bank = [ctx.enter_context(nc.psum_tensor(f"bank{i}", [P, 512], F32)) for i in range(8)]
        setup(k, a)
        k.end_phase()
        phases = ((window_attention, ()), (mlp, ("ml0", k.mlp0)), (conv_mixer, ()), (mlp, ("ml1", k.mlp1)),
                  (full_attention, ()), (binary_ffn, ()), (causal_attention, ()), (experts, (out,)))
        for phase, more in phases:
            phase(k, bank, *more)
            k.end_phase()


def constants():
    f = np.float32
    decay, gain = 0.6, 0.4
    d = np.abs(np.arange(SIDE)[:, None] - np.arange(SIDE)[None, :])
    scan = gain * decay ** d * (1 + (d == 0))
    eye = np.eye(SIDE)
    mixer = np.eye(TOK) + 0.25 * (np.kron(eye, scan) + np.kron(scan, eye))
    tok = np.arange(TOK).reshape(2, WS, 2, WS).transpose(0, 2, 1, 3).reshape(-1)
    return {
        "ident": np.eye(P, dtype=f),
        "mixer": mixer.astype(f),
        "perm": (tok[0:P, None] == np.arange(P)[None, :]).astype(f),
        "headmask": (np.arange(C)[:, None] // D0 == np.arange(H0)[None, :]).astype(f),
        "groupmask": ((np.arange(C)[:, None] // D3 == np.arange(H3)[None, :]) * float(C) ** -0.5).astype(f),
        "causal": np.where(np.arange(P)[:, None] >= np.arange(P)[None, :], 0.0, -1e30).astype(f),
        "lower": (np.arange(EXPERTS)[None, :] < np.arange(EXPERTS)[:, None]).astype(f),
    }


def kernel(**inputs):
    import concourse.bacc as bacc
    from concourse.bass_utils import run_bass_kernel_spmd

    nc = bacc.Bacc("TRN2", target_bir_lowering=False, num_devices=1)
    arrays = {name: np.ascontiguousarray(value) for name, value in inputs.items()}
    arrays.update(constants())
    a = {name: nc.dram_tensor(f"in_{name}", v.shape, mybir.dt.from_np(v.dtype), kind="ExternalInput").ap()
         for name, v in arrays.items()}
    out = nc.dram_tensor("out_tokens", (IMAGES, SIDE, SIDE, C), F32, kind="ExternalOutput").ap()
    build(nc, a, out)
    r = run_bass_kernel_spmd(nc, [{f"in_{name}": v for name, v in arrays.items()}], core_ids=[0])
    return r.results[0]["out_tokens"]
```

```python
from contextlib import ExitStack

import numpy as np

import concourse.bass as bass
from concourse import mybir

F32 = mybir.dt.float32
BF16 = mybir.dt.bfloat16
ALU = mybir.AluOpType
ACT = mybir.ActivationFunctionType
AX = mybir.AxisListType

P = 128
IMAGES = 16
SIDE = 16
TOK = SIDE * SIDE
C = 96
TILES = IMAGES * TOK // P
HID = 4 * C
KH = HID // P
LN_EPS = 1e-5
WS = 8
WTOK = WS * WS
H0 = 12
D0 = C // H0
CI = 2 * C
H2, D2 = 8, 48
PAIRS2 = H2 // 2
H3 = 6
D3 = C // H3
GRID = SIDE + 2
GROUPS = 5
GIMG = IMAGES // GROUPS
GT = 2 * GIMG
EXPERTS = 4
EPS_Q = 1e-5
QB = 128.0


def after(eng, sem, count):
    if not isinstance(count, int) or count > 0:
        eng.wait_ge(sem, count)


def alone(eng, k):
    eng.wait_ge(k.started, 1)


def pairs(eng, steps, body):
    for s in range(2):
        body(s, s, s == 0)
    with eng.Fori(1, steps // 2) as g:
        for s in range(2):
            body(g * 2 + s, s, False)


class Core:

    def __init__(self, nc, ctx):
        self.nc, self.ctx = nc, ctx
        self.started = nc.alloc_semaphore(name="started")

    def sb(self, name, shape, dt=F32, ctx=None):
        return (ctx or self.ctx).enter_context(self.nc.sbuf_tensor(name, shape, dt))

    def sems(self, prefix, names):
        self.live = {n: self.nc.alloc_semaphore(name=f"{prefix}_{n}") for n in names.split()}
        return self.live

    def end_phase(self):
        self.nc.clear_and_free_semaphores(list(self.live.values()))
        self.nc.all_engine_barrier()


def pipeline(eng, steps, body):
    for q in range(2):
        body(q, q, q == 0, False)
    with eng.Fori(1, steps // 2 - 1) as g:
        for q in range(2):
            body(g * 2 + q, q, False, False)
    for q in range(2):
        body(steps - 2 + q, q, False, q == 1)


def tiles_of(t, first, count):
    return t[:, bass.ds(first, count), :]


def normalise(pool, k, s, n, count, y, bias, v, r, free):
    x = tiles_of(k.X, n * count, count)
    mean = tiles_of(k.MV, n * count, count)[:, :, 0:1]
    var = tiles_of(k.MV, n * count, count)[:, :, 1:2]
    alone(pool, k)
    after(pool, s["T"], free)
    pool.tensor_tensor(v[:, 0:count, :], var, k.eps[:, 0:count, :], ALU.add).then_inc(s["var"], 1)
    pool.tensor_tensor(y, x, mean.broadcast_to([P, count, C]), ALU.subtract).then_inc(s["centred"], 1)
    after(pool, s["var"], n + 1)
    pool.tensor_tensor(r[:, 0:count, :], v[:, 0:count, :], k.minus_half[:, 0:count, :], ALU.pow).then_inc(s["rstd"], 1)
    alone(pool, k)
    after(pool, s["rstd"], n + 1)
    after(pool, s["centred"], n + 1)
    pool.tensor_tensor(y, y, r[:, 0:count, :].broadcast_to([P, count, C]), ALU.mult).then_inc(s["y"], 1)
    if bias is not None:
        pool.tensor_tensor(x, x, bias[:, None, :].broadcast_to([P, count, C]), ALU.add).then_inc(s["xb"], 1)


def add_and_stats(dve, k, s, n, count, new, stats, aggr, replace=False):
    x = tiles_of(k.X, n * count, count)
    (dve.tensor_copy(x, new) if replace else dve.tensor_tensor(x, x, new, ALU.add)).then_inc(s["x"], 1)
    alone(dve, k)
    after(dve, s["x"], n + 1)
    after(dve, s["mv"], n)
    for t in range(count):
        last = dve.bn_stats(stats[:, t, :], k.X[:, bass.ds(n * count + t, 1), :])
    last.then_inc(s["bn"], 1)
    alone(dve, k)
    after(dve, s["bn"], n + 1)
    for t in range(count):
        last = dve.bn_aggr(aggr[:, t, :], stats[:, t, :])
    last.then_inc(s["ag"], 1)
    after(dve, s["ag"], n + 1)
    dve.tensor_copy(tiles_of(k.MV, n * count, count), aggr[:, 0:count, :]).then_inc(s["mv"], 1)


LN_SEMS = "var centred rstd y xb x bn ag mv "


def setup(k, a):
    nc = k.nc
    s = k.sems("set", "x w cst bn ag mv zero")
    sb = k.sb
    k.X = sb("X", [P, TILES, C])
    k.MV = sb("MV", [P, TILES, 2])
    k.ident = sb("ident", [P, P])
    k.identb = sb("identb", [P, P], BF16)
    k.causal = sb("causal", [P, P], BF16)
    k.eps = sb("eps", [P, 8, 1])
    k.minus_half = sb("minus_half", [P, 8, 1])
    k.ones = sb("ones", [P, P])
    k.stats = sb("stats", [P, 8, 6])
    k.aggr = sb("aggr", [P, 8, 2])
    k.v, k.r = sb("ln_v", [P, 8, 1]), sb("ln_r", [P, 8, 1])
    k.Y = [sb(f"Y{i}", [P, 4, C]) for i in range(2)]
    k.hT = [sb(f"hT{i}", [C, 512]) for i in range(2)]
    loads = []

    def weight(name, shape, src, dst=None):
        t = sb(name, shape)
        loads.append((t[:] if dst is None else dst(t), src))
        return t

    def column(name, src):
        return weight(name, [src.shape[0], 1], src[:, None])

    def row(name, src):
        return weight(name, [P, src.shape[0]], src[None, :].broadcast_to([P, src.shape[0]]))

    k.g1, k.b1 = column("w_g1", a["L0_conv_ln1_w"]), column("w_b1", a["L0_conv_ln1_b"])
    k.wqkv0 = weight("w_qkv0", [C, 3 * C], a["L0_conv_qkv_w"])
    k.bq0 = column("w_bq0", a["L0_conv_qkv_b"][0:C])
    k.bk0 = column("w_bk0", a["L0_conv_qkv_b"][C:2 * C])
    k.bv0 = row("w_bv0", a["L0_conv_qkv_b"][2 * C:3 * C])
    k.wp0 = weight("w_p0", [C, C], a["L0_conv_proj_w"])
    k.bp0 = row("w_bp0", a["L0_conv_proj_b"])
    k.headmask = weight("headmask", [C, H0], a["headmask"])
    k.bias0 = sb("bias0", [P, WTOK, H0])
    bias0r = sb("bias0r", [P, WTOK, H0])
    table = a["L0_conv_rpb_table"]
    span = 2 * WS - 1
    for wx in range(2):
        for qy in range(WS):
            src = bass.AP(tensor=table.tensor, offset=qy * span * H0, ap=[[H0, WS], [span * H0, WS], [1, WS * H0]])
            p0 = wx * WTOK + qy * WS
            loads.append((bias0r[p0:p0 + WS].rearrange("q (y x) h -> q y (x h)", y=WS), src))

    def mlp(p, g, b, w1, b1, w2, b2):
        return dict(g=column(p + "g", g), b=column(p + "b", b), w1=weight(p + "w1", [C, HID], w1),
                    b1=weight(p + "b1", [P, KH], b1.rearrange("(k p) -> p k", p=P)),
                    w2=weight(p + "w2", [P, KH, C], w2.rearrange("(k p) c -> p k c", p=P)), b2=row(p + "b2", b2))

    k.mlp0 = mlp("m0", a["L0_conv_ln2_w"], a["L0_conv_ln2_b"], a["L0_conv_mlp_w1"], a["L0_conv_mlp_b1"],
                 a["L0_conv_mlp_w2"], a["L0_conv_mlp_b2"])
    k.g3, k.b3 = column("w_g3", a["L1_conv_n1_g"]), column("w_b3", a["L1_conv_n1_b"])
    k.win = weight("w_in", [C, CI], a["L1_conv_w_in"])
    k.bin = weight("b_in", [C, 2], a["L1_conv_b_in"].rearrange("(j p) -> p j", p=C))
    k.kconv = sb("k_conv", [C, 2, 9])
    for j in range(2):
        loads.append((k.kconv[:, j, :], a["L1_conv_k_conv"].rearrange("a b o (j p) -> j p (a b o)", p=C)[j]))
    k.ong = weight("on_g", [C, 2], a["L1_conv_on_g"].rearrange("(j p) -> p j", p=C))
    k.onb = weight("on_b", [C, 2], a["L1_conv_on_b"].rearrange("(j p) -> p j", p=C))
    k.wout = weight("w_out", [C, 2, C], a["L1_conv_w_out"].rearrange("(j p) c -> p j c", p=C))
    k.bout = row("b_out", a["L1_conv_b_out"])
    k.perm = weight("perm", [P, P], a["perm"])
    k.mixer = weight("mixer", [P, 2, TOK], a["mixer"].rearrange("(j p) t -> p j t", p=P))
    k.mlp1 = mlp("m1", a["L1_conv_n2_g"], a["L1_conv_n2_b"], a["L1_conv_w1"], a["L1_conv_b1"],
                 a["L1_conv_w2"], a["L1_conv_b2"])
    wide = [C, PAIRS2, 2, 64]
    k.wq2, k.wk2 = sb("w_q2", wide), sb("w_k2", wide)
    for part, t in enumerate((k.wq2, k.wk2)):
        for p in range(PAIRS2):
            base = part * H2 * D2 + p * 2 * D2
            loads.append((t[:, p, :, 0:D2], a["L2_attn_Wqkv"][:, base:base + 2 * D2].rearrange("c (h d) -> c h d", h=2)))
    k.wv2 = weight("w_v2", [C, H2 * D2], a["L2_attn_Wqkv"][:, 2 * H2 * D2:3 * H2 * D2])
    k.wp2 = sb("w_p2", [P, PAIRS2, C])
    for h in range(2):
        loads.append((k.wp2[64 * h:64 * h + D2, :, :],
                      a["L2_attn_Wproj"].rearrange("(p h d) c -> h d p c", h=2, d=D2)[h]))
    k.bp2 = row("w_bp2", a["L2_attn_bproj"])
    k.fb1 = weight("f_b1", [P, KH], a["L2_ffn_b1"].rearrange("(k p) -> p k", p=P))
    k.fb2 = row("f_b2", a["L2_ffn_b2"])
    k.wq3 = weight("w_q3", [C, C], a["L3_attn_Wq"])
    k.wkv3 = sb("w_kv3", [C, H3, C + D3])
    for g in range(H3):
        loads.append((k.wkv3[:, g, 0:C].rearrange("c (i d) -> c i d", d=D3),
                      a["L3_attn_Wk"][:, None, g * D3:(g + 1) * D3].broadcast_to([C, H3, D3])))
    loads.append((k.wkv3[:, :, C:C + D3], a["L3_attn_Wv"].rearrange("c (g d) -> c g d", d=D3)))
    k.groupmask = weight("groupmask", [C, H3], a["groupmask"])
    k.ingroup = weight("ingroup", [C, H3], a["ingroup"])
    k.wp3 = weight("w_p3", [C, C], a["L3_attn_Wp"])
    k.bp3 = row("w_bp3", a["L3_attn_bp"])
    k.gw = weight("w_gate", [C, EXPERTS], a["L3_ffn_gate_w"])
    k.gb = row("b_gate", a["L3_ffn_gate_b"])
    k.ew1 = weight("e_w1", [C, EXPERTS, HID], a["L3_ffn_w1"].rearrange("e c h -> c e h"))
    k.eb1 = weight("e_b1", [P, EXPERTS, KH], a["L3_ffn_b1"].rearrange("e (k p) -> p e k", p=P))
    k.ew2 = weight("e_w2", [P, EXPERTS, KH, C], a["L3_ffn_w2"].rearrange("e (k p) c -> p e k c", p=P))
    k.eb2 = weight("e_b2", [P, EXPERTS, C], a["L3_ffn_b2"][None, :, :].broadcast_to([P, EXPERTS, C]))
    k.lower = weight("lower", [P, EXPERTS, EXPERTS], a["lower"][None, :, :].broadcast_to([P, EXPERTS, EXPERTS]))
    k.g76, k.g19 = HID // GROUPS, C // GROUPS
    k.f1 = weight("f_w1", [k.g76, GROUPS, C], a["L2_ffn_W1"][0:GROUPS * k.g76, :].rearrange("(g o) c -> o g c", g=GROUPS))
    k.f2 = weight("f_w2", [k.g19, GROUPS, HID], a["L2_ffn_W2"][0:GROUPS * k.g19, :].rearrange("(g o) c -> o g c", g=GROUPS))
    loads.append((k.ident[:], a["ident"]))
    stage = weight("causal_f", [P, P], a["causal"])

    with nc.Block() as block:
        @block.sync
        def _(sp):
            for wx in range(2):
                for r in range(WS):
                    p0 = wx * WTOK + r * WS
                    src = a["x"].rearrange("b (y i) (v c) d -> v i c (b y) d", i=WS, c=WS)[wx, r]
                    sp.dma_start(k.X[p0:p0 + WS, :, :], src).then_inc(s["x"], 16)
            sp.wait_ge(s["x"], 16 * 2 * WS)

        @block.gpsimd
        def _(pool):
            pool.memset(k.eps[:], LN_EPS).then_inc(k.started, 1)
            pool.memset(k.minus_half[:], -0.5)
            for t in (k.wq2, k.wk2, k.wp2, k.ones):
                last = pool.memset(t[:], 1.0 if t is k.ones else 0.0)
            last.then_inc(s["zero"], 1)
            pool.wait_ge(s["w"], 16 * len(loads))
            pool.tensor_copy(k.identb[:], k.ident[:])
            pool.tensor_copy(k.bias0[:], bias0r[:, ::-1, :])
            pool.tensor_copy(k.causal[:], stage[:]).then_inc(s["cst"], 1)

        @block.scalar
        def _(act):
            act.wait_ge(s["zero"], 1)
            for dst, src in loads:
                act.dma_start(dst, src, allow_slow_non_contiguous=True).then_inc(s["w"], 16)
            act.wait_ge(s["w"], 16 * len(loads))

        @block.vector
        def _(dve):
            dve.wait_ge(s["x"], 16 * 2 * WS)
            for n in range(TILES // 4):
                for t in range(4):
                    last = dve.bn_stats(k.stats[:, t, :], k.X[:, bass.ds(n * 4 + t, 1), :])
                last.then_inc(s["bn"], 1)
                after(dve, s["bn"], n + 1)
                for t in range(4):
                    last = dve.bn_aggr(k.aggr[:, t, :], k.stats[:, t, :])
                last.then_inc(s["ag"], 1)
                after(dve, s["ag"], n + 1)
                dve.tensor_copy(tiles_of(k.MV, n * 4, 4), k.aggr[:, 0:4, :]).then_inc(s["mv"], 1)
                after(dve, s["mv"], n + 1)


def window_attention(k, bank):
    nc = k.nc
    s = k.sems("wa", LN_SEMS + "init bq T hT qk q kb kx vp v sc add mx sub exp pt pte av rec a oT oTe pj")
    with ExitStack() as ctx:
        def sb(name, shape, dt=F32):
            return k.sb("wa_" + name, shape, dt, ctx)

        bqs = sb("bqs", [C, 1])
        h2 = [sb(f"h2{i}", [C, 4, 2, WTOK]) for i in range(2)]
        qT = [sb(f"q{i}", [C, TOK]) for i in range(2)]
        kT = sb("k", [C, TOK])
        kx = [sb(f"kx{i}", [C, H0, TOK]) for i in range(2)]
        vb = [sb(f"vb{i}", [P, 4, H0 // 2, 2 * D0 + 2]) for i in range(2)]
        S = [sb(f"s{i}", [P, H0, WTOK]) for i in range(2)]
        E = [sb(f"e{i}", [P, H0, WTOK]) for i in range(2)]
        mx = [sb(f"mx{i}", [P, H0, 1]) for i in range(2)]
        PT = sb("pt", [P, 2, 3, P])
        rec = sb("rec", [P, H0 // 2, 2, 1])
        A = [sb(f"a{i}", [P, 2, C]) for i in range(2)]
        AT = sb("at", [C, TOK])
        scale = float(D0) ** -0.5

        with nc.Block() as block:
            @block.gpsimd
            def _(pool):
                for i in range(2):
                    pool.memset(vb[i][:], 0.0).then_inc(s["bq"], 1)
                pool.wait_ge(s["bq"], 2)
                for i in range(2):
                    pool.memset(vb[i][0:WTOK, :, :, 2 * D0:2 * D0 + 1], 1.0).then_inc(s["init"], 1)
                    pool.wait_ge(s["init"], i + 1)
                    pool.memset(vb[i][WTOK:P, :, :, 2 * D0 + 1:2 * D0 + 2], 1.0).then_inc(s["bq"], 1)
                    pool.wait_ge(s["bq"], 3 + i)
                pool.tensor_scalar(bqs[:], k.bq0[:], scale, 0.0, ALU.mult, ALU.add).then_inc(s["bq"], 1)
                pool.wait_ge(s["bq"], 5)

                def norm(n, slot):
                    normalise(pool, k, s, n, 2, k.Y[slot][:, 0:2, :], k.bp0, k.v, k.r, n - 1)
                norm(0, 0)

                def body(n, slot, first, last):
                    if not last:
                        norm(n + 1, 1 - slot)
                    for t in range(2):
                        after(pool, s["mx"], 2 * n + t + 1)
                        pool.tensor_tensor(S[t][:], S[t][:], mx[t][:].broadcast_to([P, H0, WTOK]), ALU.subtract).then_inc(s["sub"], 1)
                pipeline(pool, IMAGES, body)

            @block.tensor
            def _(pe):
                def tokens_t(n, slot):
                    after(pe, s["y"], n + 1)
                    after(pe, s["hT"], n)
                    after(pe, s["oTe"], n - 2)
                    for t in range(2):
                        last = pe.transpose(bank[0][0:C, t * P:(t + 1) * P], k.Y[slot][:, t, :], k.ident[:])
                    last.then_inc(s["T"], 1)

                def queries_keys(n, slot):
                    after(pe, s["hT"], n + 1)
                    after(pe, s["q"], n)
                    after(pe, s["kb"], n)
                    h = h2[slot][:, :, 0, :]
                    pe.matmul(bank[1][0:C, 0:TOK], k.wqkv0[:, 0:C], h, start=True, stop=True)
                    pe.matmul(bank[1][0:C, TOK:2 * TOK], k.wqkv0[:, C:2 * C], h, start=True, stop=True).then_inc(s["qk"], 1)

                def values(n, slot):
                    after(pe, s["v"], n)
                    for w in range(4):
                        last = pe.matmul(bank[2][:, w * C:(w + 1) * C], h2[slot][:, w, :, :].rearrange("p i k -> p (i k)"), k.wqkv0[:, 2 * C:3 * C], start=True, stop=True)
                    last.then_inc(s["vp"], 1)

                def scores(n, t, slot):
                    after(pe, s["add"], 2 * n + t)
                    for half in range(2):
                        for w in range(2):
                            o = (2 * t + w) * WTOK
                            last = pe.matmul(bank[3 + half][w * WTOK:(w + 1) * WTOK, 0:384], qT[slot][:, o:o + WTOK],
                                             kx[slot][:, half * 6:half * 6 + 6, o:o + WTOK], start=True, stop=True)
                    last.then_inc(s["sc"], 1)

                def probs_t(n, t):
                    after(pe, s["exp"], 2 * n + t + 1)
                    after(pe, s["pte"], 2 * n + t)
                    for j in range(H0 // 2):
                        last = pe.transpose(bank[5 + j // 3][:, (j % 3) * P:(j % 3 + 1) * P],
                                            E[t][:, 2 * j:2 * j + 2, :].rearrange("p h k -> p (h k)"), k.ident[:])
                    last.then_inc(s["pt"], 1)

                def attend(n, t, slot):
                    after(pe, s["pte"], 2 * n + t + 1)
                    after(pe, s["a"], 2 * n + t)
                    after(pe, s["v"], n + 1)
                    if t == 0:
                        after(pe, s["x"], n)
                    for j in range(H0 // 2):
                        for w in range(2):
                            last = pe.matmul(bank[7][w * WTOK:(w + 1) * WTOK, j * 18:(j + 1) * 18],
                                             PT[:, j // 3, j % 3, w * WTOK:(w + 1) * WTOK], vb[slot][:, 2 * t + w, j, :],
                                             start=True, stop=True)
                    last.then_inc(s["av"], 1)

                def outputs_t(n, slot, tokens):
                    after(pe, s["a"], 2 * n + 2)
                    after(pe, s["hT"], tokens)
                    for t in range(2):
                        last = pe.transpose(bank[0][0:C, t * P:(t + 1) * P], A[slot][:, t, :], k.ident[:])
                    last.then_inc(s["oT"], 1)

                def project(n):
                    after(pe, s["oTe"], n + 1)
                    for t in range(2):
                        last = pe.matmul(bank[7][:, t * C:(t + 1) * C], AT[:, t * P:(t + 1) * P], k.wp0[:], start=True, stop=True)
                    last.then_inc(s["pj"], 1)

                tokens_t(0, 0)
                queries_keys(0, 0)
                values(0, 0)

                def body(n, slot, first, last):
                    after(pe, s["kx"], n + 1)
                    after(pe, s["q"], n + 1)
                    scores(n, 0, slot)
                    if not last:
                        tokens_t(n + 1, 1 - slot)
                    if not first:
                        probs_t(n - 1, 1)
                    if not last:
                        queries_keys(n + 1, 1 - slot)
                    if not first:
                        attend(n - 1, 1, 1 - slot)
                    if not last:
                        values(n + 1, 1 - slot)
                    if not first:
                        outputs_t(n - 1, 1 - slot, n + 1 if last else n + 2)
                    scores(n, 1, slot)
                    if not first:
                        project(n - 1)
                    probs_t(n, 0)
                    attend(n, 0, slot)
                pipeline(pe, IMAGES, body)
                probs_t(IMAGES - 1, 1)
                attend(IMAGES - 1, 1, 1)
                outputs_t(IMAGES - 1, 1, IMAGES)
                project(IMAGES - 1)

            @block.scalar
            def _(act):
                act.wait_ge(s["bq"], 5)

                def pt_out(n, t):
                    after(act, s["pt"], 2 * n + t + 1)
                    after(act, s["av"], 2 * n + t)
                    for b in range(2):
                        last = act.activation(PT[:, b, :, :], bank[5 + b][:, 0:384].rearrange("p (j q) -> p j q", j=3), ACT.Copy)
                    last.then_inc(s["pte"], 1)

                def exps(n, t):
                    after(act, s["sub"], 2 * n + t + 1)
                    after(act, s["pt"], 2 * n + t - 1)
                    act.activation(E[t][:], S[t][:], ACT.Exp).then_inc(s["exp"], 1)

                def out_t(n):
                    after(act, s["oT"], n + 1)
                    after(act, s["pj"], n)
                    act.activation(AT[:], bank[0][0:C, 0:TOK], ACT.Copy).then_inc(s["oTe"], 1)

                def tokens(n, slot):
                    after(act, s["T"], n + 1)
                    after(act, s["vp"], n - 1)
                    act.activation(h2[slot][:], bank[0][0:C, 0:TOK].rearrange("p (v k) -> p v k", v=4)[:, :, None, :].broadcast_to([C, 4, 2, WTOK]),
                                   ACT.Identity, bias=k.b1[:], scale=k.g1[:]).then_inc(s["hT"], 1)

                def queries(n, slot):
                    after(act, s["kb"], n + 1)
                    after(act, s["sc"], 2 * n - 2)
                    act.activation(qT[slot][:], bank[1][0:C, 0:TOK], ACT.Identity, bias=bqs[:], scale=scale).then_inc(s["q"], 1)

                tokens(0, 0)
                queries(0, 0)

                def body(n, slot, first, last):
                    if not last:
                        tokens(n + 1, 1 - slot)
                    if not first:
                        pt_out(n - 1, 1)
                    exps(n, 0)
                    if not last:
                        queries(n + 1, 1 - slot)
                    if not first:
                        out_t(n - 1)
                    pt_out(n, 0)
                    exps(n, 1)
                pipeline(act, IMAGES, body)
                pt_out(IMAGES - 1, 1)
                out_t(IMAGES - 1)

            @block.vector
            def _(dve):
                def heads_out(n, t, slot):
                    after(dve, s["av"], 2 * n + t + 1)
                    after(dve, s["oT"], n - 1)
                    o = bank[7][:, 0:108].rearrange("p (j c) -> p j c", c=18)
                    dve.reciprocal(rec[:], o[:, :, 16:18, None]).then_inc(s["rec"], 1)
                    after(dve, s["rec"], 2 * n + t + 1)
                    dve.tensor_tensor(A[slot][:, t, :].rearrange("p (j i d) -> p j i d", j=H0 // 2, i=2),
                                      o[:, :, 0:16].rearrange("p j (i d) -> p j i d", i=2),
                                      rec[:].broadcast_to([P, H0 // 2, 2, D0]), ALU.mult).then_inc(s["a"], 1)

                def residual(n):
                    after(dve, s["pj"], n + 1)
                    after(dve, s["xb"], n + 1)
                    add_and_stats(dve, k, s, n, 2, bank[7][:, 0:2 * C].rearrange("p (t c) -> p t c", t=2), k.stats, k.aggr)

                def keys(n):
                    after(dve, s["qk"], n + 1)
                    after(dve, s["kx"], n)
                    dve.tensor_scalar(kT[:], bank[1][0:C, TOK:2 * TOK], k.bk0[:], None, ALU.add).then_inc(s["kb"], 1)

                def keys_by_head(n, slot):
                    after(dve, s["kb"], n + 1)
                    after(dve, s["sc"], 2 * n - 2)
                    dve.tensor_tensor(kx[slot][:], kT[:, None, :].broadcast_to([C, H0, TOK]),
                                      k.headmask[:, :, None].broadcast_to([C, H0, TOK]), ALU.mult).then_inc(s["kx"], 1)

                def values(n, slot):
                    after(dve, s["vp"], n + 1)
                    after(dve, s["av"], 2 * n - 2)
                    for half in range(2):
                        rows = slice(half * WTOK, (half + 1) * WTOK)
                        src = bank[2][rows, 0:4 * C].rearrange("p (v j i d) -> p v j i d", v=4, i=2, d=D0)
                        b = k.bv0[rows, :].rearrange("p (j i d) -> p j i d", i=2, d=D0)
                        for w in range(4):
                            last = dve.tensor_tensor(vb[slot][rows, w, :, half * D0:(half + 1) * D0], src[:, w, :, half, :], b[:, :, half, :], ALU.add)
                    last.then_inc(s["v"], 1)

                def biased_scores(n, t):
                    after(dve, s["sc"], 2 * n + t + 1)
                    after(dve, s["exp"], 2 * n + t - 1)
                    for half in range(2):
                        hs = slice(half * 6, half * 6 + 6)
                        last = dve.tensor_tensor(S[t][:, hs, :], bank[3 + half][:, 0:384].rearrange("p (h k) -> p h k", h=6),
                                                 k.bias0[:, :, hs].rearrange("p k h -> p h k"), ALU.add)
                    last.then_inc(s["add"], 1)
                    after(dve, s["add"], 2 * n + t + 1)
                    dve.tensor_reduce(mx[t][:, :, 0], S[t][:], AX.X, ALU.max).then_inc(s["mx"], 1)

                dve.wait_ge(s["bq"], 5)
                keys(0)
                keys_by_head(0, 0)
                values(0, 0)

                def body(n, slot, first, last):
                    biased_scores(n, 0)
                    if not last:
                        keys(n + 1)
                    if not first:
                        heads_out(n - 1, 1, 1 - slot)
                    if not last:
                        keys_by_head(n + 1, 1 - slot)
                        values(n + 1, 1 - slot)
                    biased_scores(n, 1)
                    if not first:
                        residual(n - 1)
                    heads_out(n, 0, slot)
                pipeline(dve, IMAGES, body)
                heads_out(IMAGES - 1, 1, 1)
                residual(IMAGES - 1)


def mlp(k, bank, prefix, w):
    nc = k.nc
    s = k.sems(prefix, LN_SEMS + "T hT up gelu down")
    steps = TILES // 4
    with ExitStack() as ctx:
        G = [k.sb(f"{prefix}_G{i}", [P, KH, 512], F32, ctx) for i in range(2)]
        with nc.Block() as block:
            @block.gpsimd
            def _(pool):
                def body(n, slot, first):
                    normalise(pool, k, s, n, 4, k.Y[slot][:], w["b2"], k.v, k.r, n - 1)
                pairs(pool, steps, body)

            @block.tensor
            def _(pe):
                def down(n, slot):
                    after(pe, s["gelu"], KH * (n + 1))
                    after(pe, s["x"], n)
                    for t in range(4):
                        for j in range(KH):
                            last = pe.matmul(bank[7][:, t * C:(t + 1) * C], G[slot][:, j, t * P:(t + 1) * P], w["w2"][:, j, :],
                                             start=(j == 0), stop=(j == KH - 1))
                    last.then_inc(s["down"], 1)

                def body(n, slot, first):
                    after(pe, s["y"], n + 1)
                    after(pe, s["hT"], n)
                    for t in range(4):
                        last = pe.transpose(bank[6][0:C, t * P:(t + 1) * P], k.Y[slot][:, t, :], k.ident[:])
                    last.then_inc(s["T"], 1)
                    if not first:
                        down(n - 1, 1 - slot)
                    after(pe, s["hT"], n + 1)
                    after(pe, s["gelu"], KH * (n - 1))
                    for j in range(KH):
                        pe.matmul(bank[3 * slot + j][:], w["w1"][:, j * P:(j + 1) * P], k.hT[slot][:], start=True, stop=True).then_inc(s["up"], 1)
                pairs(pe, steps, body)
                down(steps - 1, 1)

            @block.scalar
            def _(act):
                def body(n, slot, first):
                    after(act, s["down"], n - 1)
                    for j in range(KH):
                        after(act, s["up"], KH * n + j + 1)
                        act.activation(G[slot][:, j, :], bank[3 * slot + j][:], ACT.Gelu, bias=w["b1"][:, j:j + 1]).then_inc(s["gelu"], 1)
                pairs(act, steps, body)

            @block.vector
            def _(dve):
                def residual(n):
                    after(dve, s["down"], n + 1)
                    after(dve, s["xb"], n + 1)
                    add_and_stats(dve, k, s, n, 4, bank[7][:, 0:4 * C].rearrange("p (t c) -> p t c", t=4), k.stats, k.aggr)

                def body(n, slot, first):
                    after(dve, s["T"], n + 1)
                    after(dve, s["up"], KH * (n - 1))
                    dve.tensor_scalar(k.hT[slot][:], bank[6][0:C, :], w["g"][:], w["b"][:], ALU.mult, ALU.add).then_inc(s["hT"], 1)
                    if not first:
                        residual(n - 1)
                pairs(dve, steps, body)
                residual(steps - 1)


def raster(t, y):
    return t.rearrange("p (y i v c) -> p y v i c", y=2, i=WS, v=2)[:, y]


def conv_mixer(k, bank):
    nc = k.nc
    s = k.sems("cm", LN_SEMS + "z T hT in p taps acc1 conv ct loc mix bn2 ag2 va2 rs2 z2 zT zTe out diag init")
    with ExitStack() as ctx:
        def sb(name, shape, dt=F32):
            return k.sb("cm_" + name, shape, dt, ctx)

        grid = [sb(f"g{i}", [C, 2, GRID, GRID]) for i in range(2)]
        acc = [sb(f"acc{i}", [C, TOK]) for i in range(2)]
        acc1 = sb("accb", [C, TOK])
        diag = sb("diag", [C, 9, C])
        loc = sb("loc", [P, 2, CI])
        st2, ag2 = sb("st2", [P, 2, 6]), sb("ag2", [P, 2, 2])
        v2, r2 = sb("v2", [P, 2, 1]), sb("r2", [P, 2, 1])
        Z = sb("z", [P, 2, CI])
        ZT = sb("zT", [C, 2, 2, P])

        with nc.Block() as block:
            @block.gpsimd
            def _(pool):
                for i in range(2):
                    last = pool.memset(grid[i][:], 0.0)
                last.then_inc(s["init"], 1)
                for tap in range(9):
                    last = pool.tensor_scalar(diag[:, tap, :], k.ident[0:C, 0:C], k.kconv[:, 1, tap:tap + 1], 0.0, ALU.mult, ALU.add)
                last.then_inc(s["diag"], 1)

                def rstd2(n):
                    after(pool, s["ag2"], n + 1)
                    after(pool, s["z2"], n)
                    pool.tensor_tensor(v2[:], ag2[:, :, 1:2], k.eps[:, 0:2, :], ALU.add).then_inc(s["va2"], 1)
                    after(pool, s["va2"], n + 1)
                    pool.tensor_tensor(r2[:], v2[:], k.minus_half[:, 0:2, :], ALU.pow).then_inc(s["rs2"], 1)

                def body(n, slot, first):
                    normalise(pool, k, s, n, 2, k.Y[slot][:, 0:2, :], k.bout, k.v, k.r, n - 1)
                    if not first:
                        rstd2(n - 1)
                pairs(pool, IMAGES, body)
                rstd2(IMAGES - 1)

            @block.tensor
            def _(pe):
                def mix(n):
                    after(pe, s["loc"], n + 1)
                    after(pe, s["z2"], n)
                    for t in range(2):
                        for j in range(2):
                            last = pe.matmul(bank[4][:, t * CI:(t + 1) * CI], k.mixer[:, j, t * P:(t + 1) * P], loc[:, j, :],
                                             start=(j == 0), stop=(j == 1))
                    last.then_inc(s["mix"], 1)

                def back(n):
                    after(pe, s["z2"], n + 1)
                    after(pe, s["zTe"], n)
                    for j in range(2):
                        for t in range(2):
                            last = pe.transpose(bank[5][0:C, (2 * j + t) * P:(2 * j + t + 1) * P], Z[:, t, j * C:(j + 1) * C], k.ident[:])
                    last.then_inc(s["zT"], 1)

                def out(n):
                    after(pe, s["zTe"], n + 1)
                    after(pe, s["x"], n)
                    after(pe, s["xb"], n + 1)
                    for t in range(2):
                        o = bank[6][:, t * C:(t + 1) * C]
                        pe.matmul(o, k.perm[:], k.X[:, bass.ds(n * 2 + t, 1), :], start=True, stop=False)
                        for j in range(2):
                            last = pe.matmul(o, ZT[:, j, t, :], k.wout[:, j, :], start=False, stop=(j == 1))
                    last.then_inc(s["out"], 1)

                def body(n, slot, first):
                    after(pe, s["y"], n + 1)
                    after(pe, s["hT"], n)
                    for t in range(2):
                        last = pe.transpose(bank[0][0:C, t * P:(t + 1) * P], k.Y[slot][:, t, :], k.ident[:])
                    last.then_inc(s["T"], 1)
                    if not first:
                        mix(n - 1)
                    after(pe, s["hT"], n + 1)
                    after(pe, s["p"], n)
                    for j in range(2):
                        last = pe.matmul(bank[1][0:C, j * TOK:(j + 1) * TOK], k.win[:, j * C:(j + 1) * C], k.hT[slot][:, 0:TOK], start=True, stop=True)
                    last.then_inc(s["in"], 1)
                    if not first:
                        back(n - 1)
                    if first:
                        pe.wait_ge(s["diag"], 1)
                    after(pe, s["p"], n + 1)
                    after(pe, s["acc1"], n)
                    for tap in range(9):
                        y, x = divmod(tap, 3)
                        last = pe.matmul(bank[3][0:C, 0:TOK], diag[:, tap, :], grid[slot][:, 1, y:y + SIDE, x:x + SIDE],
                                         start=(tap == 0), stop=(tap == 8))
                    last.then_inc(s["taps"], 1)
                    if not first:
                        out(n - 1)
                    after(pe, s["conv"], 9 * (n + 1))
                    after(pe, s["acc1"], n + 1)
                    after(pe, s["loc"], n)
                    for half, src in ((0, acc[slot]), (1, acc1)):
                        for j in range(2):
                            last = pe.transpose(bank[2][:, (2 * j + half) * C:(2 * j + half + 1) * C], src[:, j * P:(j + 1) * P], k.ident[0:C, 0:C])
                    last.then_inc(s["ct"], 1)
                pairs(pe, IMAGES, body)
                mix(IMAGES - 1)
                back(IMAGES - 1)
                out(IMAGES - 1)

            @block.scalar
            def _(act):
                act.wait_ge(s["init"], 1)

                def zt(n):
                    after(act, s["zT"], n + 1)
                    after(act, s["out"], n)
                    for j in range(2):
                        last = act.activation(ZT[:, j, :, :], bank[5][0:C, j * 2 * P:(j + 1) * 2 * P].rearrange("p (t q) -> p t q", t=2),
                                              ACT.Identity, bias=k.onb[:, j:j + 1], scale=k.ong[:, j:j + 1])
                    last.then_inc(s["zTe"], 1)

                def body(n, slot, first):
                    after(act, s["T"], n + 1)
                    after(act, s["in"], n - 1)
                    for y in range(2):
                        last = act.activation(raster(k.hT[slot][:, 0:TOK], y), bank[0][0:C, y * P:(y + 1) * P].rearrange("p (v i c) -> p v i c", v=2, i=WS),
                                              ACT.Identity, bias=k.b3[:], scale=k.g3[:])
                    last.then_inc(s["hT"], 1)
                    after(act, s["in"], n + 1)
                    after(act, s["taps"], n - 1)
                    after(act, s["conv"], 9 * (n - 1))
                    for j in range(2):
                        last = act.activation(grid[slot][:, j, 1:1 + SIDE, 1:1 + SIDE],
                                              bank[1][0:C, j * TOK:(j + 1) * TOK].rearrange("p (i c) -> p i c", c=SIDE),
                                              ACT.Identity, bias=k.bin[:, j:j + 1])
                    last.then_inc(s["p"], 1)
                    if not first:
                        zt(n - 1)
                    after(act, s["taps"], n + 1)
                    after(act, s["ct"], n)
                    act.activation(acc1[:], bank[3][0:C, 0:TOK], ACT.Copy).then_inc(s["acc1"], 1)
                    after(act, s["ct"], n + 1)
                    after(act, s["mix"], n)
                    act.activation(loc[:], bank[2][:, 0:2 * CI].rearrange("p (t c) -> p t c", t=2), ACT.Copy).then_inc(s["loc"], 1)
                pairs(act, IMAGES, body)
                zt(IMAGES - 1)

            @block.vector
            def _(dve):
                def norm2(n):
                    after(dve, s["mix"], n + 1)
                    after(dve, s["va2"], n)
                    for t in range(2):
                        last = dve.bn_stats(st2[:, t, :], bank[4][:, t * CI:(t + 1) * CI])
                    last.then_inc(s["bn2"], 1)
                    alone(dve, k)
                    after(dve, s["bn2"], n + 1)
                    for t in range(2):
                        last = dve.bn_aggr(ag2[:, t, :], st2[:, t, :])
                    last.then_inc(s["ag2"], 1)

                def norm2b(n):
                    after(dve, s["rs2"], n + 1)
                    after(dve, s["zT"], n)
                    for t in range(2):
                        last = dve.tensor_scalar(Z[:, t, :], bank[4][:, t * CI:(t + 1) * CI], ag2[:, t, 0:1], r2[:, t, :], ALU.subtract, ALU.mult)
                    last.then_inc(s["z2"], 1)

                def residual(n):
                    after(dve, s["out"], n + 1)
                    after(dve, s["xb"], n + 1)
                    add_and_stats(dve, k, s, n, 2, bank[6][:, 0:2 * C].rearrange("p (t c) -> p t c", t=2), k.stats, k.aggr, replace=True)

                def body(n, slot, first):
                    if not first:
                        norm2(n - 1)
                        norm2b(n - 1)
                    after(dve, s["p"], n + 1)
                    after(dve, s["ct"], n - 1)
                    o = acc[slot][:].rearrange("p (i c) -> p i c", c=SIDE)
                    for tap in range(9):
                        y, x = divmod(tap, 3)
                        src = grid[slot][:, 0, y:y + SIDE, x:x + SIDE]
                        kk = k.kconv[:, 0, tap:tap + 1]
                        if tap == 0:
                            dve.tensor_scalar(o, src, kk, None, ALU.mult).then_inc(s["conv"], 1)
                        else:
                            after(dve, s["conv"], 9 * n + tap)
                            dve.scalar_tensor_tensor(out=o, in0=src, scalar=kk, in1=o, op0=ALU.mult, op1=ALU.add).then_inc(s["conv"], 1)
                    if not first:
                        residual(n - 1)
                pairs(dve, IMAGES, body)
                norm2(IMAGES - 1)
                norm2b(IMAGES - 1)
                residual(IMAGES - 1)


def full_attention(k, bank):
    nc = k.nc
    s = k.sems("fa", LN_SEMS + "init T hT pj e1 e2 sc nm exp rec nrm pt pte av ote out")
    with ExitStack() as ctx:
        def sb(name, shape, dt=F32):
            return k.sb("fa_" + name, shape, dt, ctx)

        qT = [sb(f"q{i}", [P, PAIRS2, TOK]) for i in range(2)]
        kz = [sb(f"kz{i}", [P, H2, TOK]) for i in range(2)]
        V = [sb(f"v{i}", [P, 2, H2, 64]) for i in range(2)]
        nm = [sb(f"nm{i}", [P, 2]) for i in range(2)]
        sm = [sb(f"sm{i}", [P, 2]) for i in range(2)]
        rc = [sb(f"rc{i}", [P, 2]) for i in range(2)]
        E = [sb(f"e{i}", [P, 2, TOK]) for i in range(2)]
        PT = [sb(f"pt{i}", [P, 2, TOK]) for i in range(4)]
        OT = [sb(f"ot{i}", [P, PAIRS2, TOK]) for i in range(2)]
        scale = float(D2) ** -0.5
        U = H2

        with nc.Block() as block:
            @block.gpsimd
            def _(pool):
                for t in kz + V:
                    last = pool.memset(t[:], 0.0)
                last.then_inc(s["init"], 1)

                def body(n, slot, first):
                    normalise(pool, k, s, n, 2, k.Y[slot][:, 0:2, :], k.bp2, k.v, k.r, n - 1)
                pairs(pool, IMAGES, body)

            @block.tensor
            def _(pe):
                def score(n, h, slot):
                    u = U * n + h
                    after(pe, s["exp"], u - 1)
                    for c in range(2):
                        last = pe.matmul(bank[3 + h % 2][:, c * TOK:(c + 1) * TOK], qT[slot][:, h // 2, c * P:(c + 1) * P],
                                         kz[slot][:, h, :], start=True, stop=True)
                    last.then_inc(s["sc"], 1)

                def probs(n, h):
                    u = U * n + h
                    after(pe, s["nrm"], u + 1)
                    after(pe, s["pte"], u - 1)
                    for kc in range(2):
                        for c in range(2):
                            last = pe.transpose(bank[5 + h % 2][:, kc * TOK + c * P:kc * TOK + (c + 1) * P],
                                                E[h % 2][:, c, kc * P:(kc + 1) * P], k.ident[:])
                    last.then_inc(s["pt"], 1)

                def values(n, p, slot):
                    after(pe, s["pte"], U * n + 2 * p + 2)
                    after(pe, s["ote"], PAIRS2 * n + p)
                    for kc in range(2):
                        for h in (2 * p, 2 * p + 1):
                            last = pe.matmul(bank[7][64 * (h % 2):64 * (h % 2) + 64, 0:TOK], V[slot][:, kc, h, :], PT[h % 4][:, kc, :],
                                             start=(kc == 0), stop=(kc == 1), skip_group_check=True)
                    last.then_inc(s["av"], 1)

                def out(n, slot):
                    after(pe, s["ote"], PAIRS2 * (n + 1))
                    for t in range(2):
                        for p in range(PAIRS2):
                            last = pe.matmul(bank[0][:, t * C:(t + 1) * C], OT[slot][:, p, t * P:(t + 1) * P], k.wp2[:, p, :],
                                             start=(p == 0), stop=(p == PAIRS2 - 1))
                    last.then_inc(s["out"], 1)

                def tokens(m, slot):
                    after(pe, s["y"], m + 1)
                    after(pe, s["x"], m - 2)
                    for t in range(2):
                        last = pe.transpose(bank[0][0:C, t * P:(t + 1) * P], k.Y[slot][:, t, :], k.ident[:])
                    last.then_inc(s["T"], 1)

                def project(m, j, slot):
                    if j == 0:
                        after(pe, s["hT"], m + 1)
                    b = bank[1 + j % 2]
                    after(pe, s["e1"] if j % 2 == 0 else s["e2"], 3 * m + j // 2)
                    if j < 4:
                        for i in range(2):
                            w = (k.wq2 if j < 2 else k.wk2)[:, 2 * (j % 2) + i, :, :].rearrange("c h d -> c (h d)")
                            last = pe.matmul(b[:, i * TOK:(i + 1) * TOK], w, k.hT[slot][:, 0:TOK], start=True, stop=True)
                    else:
                        last = pe.matmul(b[:, 0:H2 * D2], k.hT[slot][:, (j - 4) * P:(j - 3) * P], k.wv2[:], start=True, stop=True)
                    last.then_inc(s["pj"], 1)

                def step(n, h, slot, start, end):
                    if not end or h < U:
                        if h == 0:
                            after(pe, s["e1"], 3 * n + 2)
                            after(pe, s["e2"], 3 * n + 2)
                        if h < U:
                            score(n, h, slot)
                    if h >= 2 and h < U + 2:
                        probs(n, h - 2)
                    elif h < 2 and not start:
                        probs(n - 1, U + h - 2)
                    if h == 4:
                        after(pe, s["e1"], 3 * n + 3)
                        after(pe, s["e2"], 3 * n + 3)
                    if h % 2 == 0:
                        if h >= 4:
                            values(n, h // 2 - 2, slot)
                        elif not start:
                            values(n - 1, PAIRS2 + h // 2 - 2, 1 - slot)
                    if h == 3 and not start:
                        out(n - 1, 1 - slot)
                    if not end:
                        if h == 0:
                            tokens(n + 1, 1 - slot)
                        elif h < 7:
                            project(n + 1, h - 1, 1 - slot)

                tokens(0, 0)
                for j in range(6):
                    project(0, j, 0)

                def body(n, slot, first, last):
                    for h in range(U):
                        step(n, h, slot, first, last)
                pipeline(pe, IMAGES, body)
                for h in range(U, U + 3):
                    step(IMAGES - 1, h, 1, False, True)
                out(IMAGES - 1, 1)

            @block.scalar
            def _(act):
                def exps(n, h):
                    u = U * n + h
                    after(act, s["nm"], u + 1)
                    after(act, s["pt"], u - 1)
                    after(act, s["rec"], u - 1)
                    for c in range(2):
                        last = act.activation(E[h % 2][:, c, :], bank[3 + h % 2][:, c * TOK:(c + 1) * TOK], ACT.Exp,
                                              bias=nm[h % 2][:, c:c + 1], accum_out=sm[h % 2][:, c:c + 1])
                    last.then_inc(s["exp"], 1)

                def pt_out(n, h):
                    after(act, s["pt"], U * n + h + 1)
                    after(act, s["av"], PAIRS2 * n + h // 2 - 1)
                    act.activation(PT[h % 4][:], bank[5 + h % 2][:].rearrange("p (a b) -> p a b", a=2), ACT.Copy).then_inc(s["pte"], 1)

                def tokens(m, slot):
                    after(act, s["T"], m + 1)
                    after(act, s["pj"], 6 * (m - 1))
                    act.activation(k.hT[slot][:, 0:TOK], bank[0][0:C, 0:TOK], ACT.Copy).then_inc(s["hT"], 1)

                def project(m, j, slot):
                    after(act, s["pj"], 6 * m + 2 * j + 1)
                    if j == 0:
                        after(act, s["sc"], U * (m - 1))
                        act.activation(qT[slot][:, 0:2, :], bank[1][:].rearrange("p (a b) -> p a b", a=2), ACT.Copy, scale=scale).then_inc(s["e1"], 1)
                    elif j == 1:
                        for i in range(2):
                            last = act.activation(kz[slot][64 * i:64 * i + 64, i:4:2, :],
                                                  bank[1][64 * i:64 * i + 64, :].rearrange("p (a b) -> p a b", a=2), ACT.Copy)
                        last.then_inc(s["e1"], 1)
                    else:
                        after(act, s["av"], PAIRS2 * (m - 1))
                        act.activation(V[slot][:, 0, :, 0:D2], bank[1][:, 0:H2 * D2].rearrange("p (h d) -> p h d", d=D2), ACT.Copy).then_inc(s["e1"], 1)

                act.wait_ge(s["init"], 1)
                tokens(0, 0)
                for j in range(3):
                    project(0, j, 0)

                def body(n, slot, first, last):
                    for h in range(U):
                        if h >= 2:
                            pt_out(n, h - 2)
                        elif not first:
                            pt_out(n - 1, U + h - 2)
                        exps(n, h)
                        if not last:
                            if h == 0:
                                tokens(n + 1, 1 - slot)
                            elif h % 2 == 0:
                                project(n + 1, h // 2 - 1, 1 - slot)
                pipeline(act, IMAGES, body)
                pt_out(IMAGES - 1, 6)
                pt_out(IMAGES - 1, 7)

            @block.vector
            def _(dve):
                def maxima(n, h):
                    u = U * n + h
                    after(dve, s["sc"], u + 1)
                    after(dve, s["exp"], u - 1)
                    dve.tensor_reduce(nm[h % 2][:], bank[3 + h % 2][:].rearrange("p (a b) -> p a b", a=2), AX.X, ALU.max, negate=True).then_inc(s["nm"], 1)

                def norm(n, h):
                    u = U * n + h
                    after(dve, s["exp"], u + 1)
                    after(dve, s["nrm"], u - 1)
                    dve.reciprocal(rc[h % 2][:], sm[h % 2][:]).then_inc(s["rec"], 1)
                    after(dve, s["rec"], u + 1)
                    for c in range(2):
                        last = dve.tensor_scalar(E[h % 2][:, c, :], E[h % 2][:, c, :], rc[h % 2][:, c:c + 1], None, ALU.mult)
                    last.then_inc(s["nrm"], 1)

                def pair_out(n, p, slot):
                    after(dve, s["av"], PAIRS2 * n + p + 1)
                    after(dve, s["out"], n - 1)
                    dve.tensor_copy(OT[slot][:, p, :], bank[7][:, 0:TOK]).then_inc(s["ote"], 1)

                def residual(n):
                    after(dve, s["out"], n + 1)
                    after(dve, s["xb"], n + 1)
                    add_and_stats(dve, k, s, n, 2, bank[0][:, 0:2 * C].rearrange("p (t c) -> p t c", t=2), k.stats, k.aggr)

                def project(m, j, slot):
                    after(dve, s["pj"], 6 * m + 2 * j + 2)
                    if j == 0:
                        after(dve, s["sc"], U * (m - 1))
                        dve.tensor_scalar(qT[slot][:, 2:4, :], bank[2][:].rearrange("p (a b) -> p a b", a=2), scale, None, ALU.mult).then_inc(s["e2"], 1)
                    elif j == 1:
                        for i in range(2):
                            last = dve.tensor_copy(kz[slot][64 * i:64 * i + 64, 4 + i:8:2, :],
                                                   bank[2][64 * i:64 * i + 64, :].rearrange("p (a b) -> p a b", a=2))
                        last.then_inc(s["e2"], 1)
                    else:
                        after(dve, s["av"], PAIRS2 * (m - 1))
                        dve.tensor_copy(V[slot][:, 1, :, 0:D2], bank[2][:, 0:H2 * D2].rearrange("p (h d) -> p h d", d=D2)).then_inc(s["e2"], 1)

                dve.wait_ge(s["init"], 1)
                for j in range(3):
                    project(0, j, 0)

                def body(n, slot, first, last):
                    for h in range(U):
                        maxima(n, h)
                        if h >= 1:
                            norm(n, h - 1)
                        elif not first:
                            norm(n - 1, U - 1)
                        if h % 2 == 0:
                            if h >= 4:
                                pair_out(n, h // 2 - 2, slot)
                            elif not first:
                                pair_out(n - 1, PAIRS2 + h // 2 - 2, 1 - slot)
                        if h == 4 and not first:
                            residual(n - 1)
                        if not last and h % 2 == 1 and h >= 3:
                            project(n + 1, (h - 3) // 2, 1 - slot)
                pipeline(dve, IMAGES, body)
                norm(IMAGES - 1, U - 1)
                pair_out(IMAGES - 1, 2, 1)
                pair_out(IMAGES - 1, 3, 1)
                residual(IMAGES - 1)


def binary_ffn(k, bank):
    nc = k.nc
    s = k.sems("bf", LN_SEMS + "sum mean gt lt sg tw twe T hT up h am ar1 c1 clip gelu down z am2 ar2 c2 zc q2 top0 inv0 top1 inv1")
    with ExitStack() as ctx:
        def sb(name, shape, dt=F32):
            return k.sb("bf_" + name, shape, dt, ctx)

        w1T = sb("w1T", [C, HID])
        w2T = sb("w2T", [P, KH, C])
        part = sb("part", [P, 2, GROUPS])
        mean = sb("mean", [P, 2, GROUPS])
        lt1, lt2 = sb("lt1", [k.g76, GROUPS, C]), sb("lt2", [k.g19, GROUPS, HID])
        gt1, gt2 = sb("gt1", [k.g76, GROUPS, C]), sb("gt2", [k.g19, GROUPS, HID])
        Y = [sb(f"Y{i}", [P, GT, C]) for i in range(2)]
        hT = sb("hT", [C, GT * P])
        H = [sb(f"H{i}", [P, KH, GT * P]) for i in range(2)]
        Z = sb("Z", [P, GT, C])
        am, ar, cc = sb("am", [P, 2]), sb("ar", [P, 2]), sb("cc", [P, 2, 4])
        half = GT * P // 2
        MAX = bass.bass_isa.ReduceOp.max
        mats = ((k.g76, k.f1, C, gt1, lt1), (k.g19, k.f2, HID, gt2, lt2))

        def scales(dve, i, g, src, done):
            after(dve, s[src], g + 1)
            dve.tensor_scalar(cc[:, i, 3:4], ar[:, i:i + 1], EPS_Q, None, ALU.add).then_inc(s[f"top{i}"], 1)
            after(dve, s[f"top{i}"], g + 1)
            dve.reciprocal(cc[:, i, 0:1], cc[:, i, 3:4]).then_inc(s[f"inv{i}"], 1)
            dve.tensor_scalar(cc[:, i, 1:2], cc[:, i, 3:4], (QB - EPS_Q) / QB, None, ALU.mult)
            dve.tensor_scalar(cc[:, i, 2:3], cc[:, i, 3:4], -(QB - EPS_Q) / QB, None, ALU.mult)
            after(dve, s[f"inv{i}"], g + 1)
            dve.tensor_scalar(cc[:, i, 0:1], cc[:, i, 0:1], QB, None, ALU.mult).then_inc(s[done], 1)

        def groups(eng, body):
            body(0, 0, True)
            with eng.Fori(0, GROUPS // 2) as q:
                for i in range(2):
                    body(q * 2 + 1 + i, 1 - i, False)

        LAST, LAST_SLOT = GROUPS - 1, (GROUPS - 1) % 2
        with nc.Block() as block:
            @block.gpsimd
            def _(pool):
                pool.memset(w1T[:], 0.0)
                pool.memset(w2T[:], 0.0).then_inc(s["twe"], 1)

                def output_max(g):
                    alone(pool, k)
                    after(pool, s["am2"], g + 1)
                    after(pool, s["c2"], g)
                    pool.partition_all_reduce(ar[:, 1:2], am[:, 1:2], P, MAX).then_inc(s["ar2"], 1)

                def body(g, slot, first):
                    normalise(pool, k, s, g, GT, Y[slot][:], None, k.v, k.r, g - 1)
                    alone(pool, k)
                    after(pool, s["am"], g + 1)
                    after(pool, s["c1"], g)
                    pool.partition_all_reduce(ar[:, 0:1], am[:, 0:1], P, MAX).then_inc(s["ar1"], 1)
                    if not first:
                        output_max(g - 1)
                groups(pool, body)
                output_max(LAST)

            @block.tensor
            def _(pe):
                pe.wait_ge(s["sum"], 2)
                for i, (n, w, cols, gt, lt) in enumerate(mats):
                    last = pe.matmul(bank[0][:, i * GROUPS:(i + 1) * GROUPS], k.ones[0:n, :], part[0:n, i, :], start=True, stop=True)
                last.then_inc(s["mean"], 1)
                pe.wait_ge(s["sg"], 2)
                for g in range(GROUPS):
                    last = pe.transpose(bank[1][0:C, g * k.g76:(g + 1) * k.g76], gt1[:, g, :], k.ident[0:k.g76, 0:k.g76])
                    for j in range(KH):
                        last = pe.transpose(bank[2][:, j * P + g * k.g19:j * P + (g + 1) * k.g19], gt2[:, g, j * P:(j + 1) * P], k.ident[0:k.g19, 0:k.g19])
                last.then_inc(s["tw"], 1)
                pe.wait_ge(s["twe"], 3)

                def down(g, slot):
                    after(pe, s["gelu"], KH * (g + 1))
                    after(pe, s["z"], 2 * g)
                    for t in range(GT):
                        for j in range(KH):
                            last = pe.matmul(bank[6 + t // 3][:, (t % 3) * C:(t % 3 + 1) * C], H[slot][:, j, t * P:(t + 1) * P], w2T[:, j, :],
                                             start=(j == 0), stop=(j == KH - 1))
                    last.then_inc(s["down"], 1)

                def body(g, slot, first):
                    after(pe, s["y"], g + 1)
                    after(pe, s["hT"], g)
                    for t in range(GT):
                        last = pe.transpose(bank[t // 3][0:C, (t % 3) * P:(t % 3 + 1) * P], Y[slot][:, t, :], k.ident[:])
                    last.then_inc(s["T"], 1)
                    after(pe, s["hT"], g + 1)
                    for j in range(KH):
                        for i in range(2):
                            u = 2 * j + i
                            after(pe, s["h"], 6 * g + u - 3)
                            pe.matmul(bank[2 + u % 4][:, 0:half], w1T[:, j * P:(j + 1) * P], hT[:, i * half:(i + 1) * half], start=True, stop=True).then_inc(s["up"], 1)
                    if not first:
                        down(g - 1, 1 - slot)
                groups(pe, body)
                down(LAST, LAST_SLOT)

            @block.scalar
            def _(act):
                def body(g, slot, first):
                    after(act, s["T"], g + 1)
                    after(act, s["up"], 6 * g)
                    for i in range(2):
                        last = act.activation(hT[:, i * half:(i + 1) * half], bank[i][0:C, 0:half], ACT.Copy)
                    last.then_inc(s["hT"], 1)
                    after(act, s["down"], g - 1)
                    for j in range(KH):
                        for i in range(2):
                            u = 2 * j + i
                            after(act, s["up"], 6 * g + u + 1)
                            act.activation(H[slot][:, j, i * half:(i + 1) * half], bank[2 + u % 4][:, 0:half], ACT.Identity, bias=k.fb1[:, j:j + 1]).then_inc(s["h"], 1)
                    for j in range(KH):
                        after(act, s["clip"], KH * g + j + 1)
                        act.activation(H[slot][:, j, :], H[slot][:, j, :], ACT.Gelu, scale=cc[:, 0, 0:1]).then_inc(s["gelu"], 1)
                groups(act, body)

            @block.vector
            def _(dve):
                for i, (n, w, cols, gt, lt) in enumerate(mats):
                    dve.tensor_reduce(part[0:n, i, :], w[:], AX.X, ALU.add).then_inc(s["sum"], 1)
                dve.wait_ge(s["mean"], 1)
                for i, (n, w, cols, gt, lt) in enumerate(mats):
                    dve.tensor_scalar(mean[:, i, :], bank[0][:, i * GROUPS:(i + 1) * GROUPS], 1.0 / (n * cols), None, ALU.mult).then_inc(s["gt"], 1)
                dve.wait_ge(s["gt"], 2)
                for i, (n, w, cols, gt, lt) in enumerate(mats):
                    m = mean[0:n, i, :, None].broadcast_to([n, GROUPS, cols])
                    dve.tensor_tensor(gt[:], w[:], m, ALU.is_gt).then_inc(s["gt"], 1)
                    dve.tensor_tensor(lt[:], w[:], m, ALU.is_lt).then_inc(s["lt"], 1)
                dve.wait_ge(s["gt"], 4)
                dve.wait_ge(s["lt"], 2)
                for i, (n, w, cols, gt, lt) in enumerate(mats):
                    dve.tensor_tensor(gt[:], gt[:], lt[:], ALU.subtract).then_inc(s["sg"], 1)
                dve.wait_ge(s["tw"], 1)
                dve.wait_ge(s["twe"], 1)
                dve.tensor_copy(w1T[:, 0:GROUPS * k.g76], bank[1][0:C, 0:GROUPS * k.g76]).then_inc(s["twe"], 1)
                dve.tensor_copy(w2T[:, :, 0:GROUPS * k.g19], bank[2][:, 0:KH * P].rearrange("p (j c) -> p j c", j=KH)[:, :, 0:GROUPS * k.g19]).then_inc(s["twe"], 1)

                def output(g):
                    after(dve, s["down"], g + 1)
                    after(dve, s["mv"], g)
                    for b in range(2):
                        dve.tensor_tensor(Z[:, 3 * b:3 * b + 3, :], bank[6 + b][:, 0:3 * C].rearrange("p (t c) -> p t c", t=3),
                                          k.fb2[:, None, :].broadcast_to([P, 3, C]), ALU.add).then_inc(s["z"], 1)
                    after(dve, s["z"], 2 * (g + 1))
                    after(dve, s["ar2"], g)
                    dve.tensor_reduce(am[:, 1:2], Z[:], AX.XY, ALU.max, apply_absolute_value=True).then_inc(s["am2"], 1)

                def quantised_output(g):
                    scales(dve, 1, g, "ar2", "c2")
                    after(dve, s["c2"], g + 1)
                    dve.tensor_scalar(Z[:], Z[:], cc[:, 1, 1:2], cc[:, 1, 2:3], ALU.min, ALU.max).then_inc(s["zc"], 1)
                    after(dve, s["zc"], g + 1)
                    dve.tensor_scalar(Z[:], Z[:], cc[:, 1, 0:1], None, ALU.mult).then_inc(s["q2"], 1)
                    after(dve, s["q2"], g + 1)
                    after(dve, s["y"], g + 1)
                    add_and_stats(dve, k, s, g, GT, Z[:], k.stats, k.aggr)

                def body(g, slot, first):
                    after(dve, s["h"], 6 * (g + 1))
                    after(dve, s["ar1"], g)
                    dve.tensor_reduce(am[:, 0:1], H[slot][:], AX.XY, ALU.max, apply_absolute_value=True).then_inc(s["am"], 1)
                    if not first:
                        output(g - 1)
                    after(dve, s["gelu"], KH * g)
                    scales(dve, 0, g, "ar1", "c1")
                    after(dve, s["c1"], g + 1)
                    for j in range(KH):
                        dve.tensor_scalar(H[slot][:, j, :], H[slot][:, j, :], cc[:, 0, 1:2], cc[:, 0, 2:3], ALU.min, ALU.max).then_inc(s["clip"], 1)
                    if not first:
                        quantised_output(g - 1)
                groups(dve, body)
                output(LAST)
                quantised_output(LAST)


def causal_attention(k, bank):
    nc = k.nc
    s = k.sems("ca", LN_SEMS + "T hT pj e qx kv vt v sc nm exp rec nrm pt pte av ote out red own")
    with ExitStack() as ctx:
        def sb(name, shape, dt=F32):
            return k.sb("ca_" + name, shape, dt, ctx)

        qx = [sb(f"qx{i}", [C, TOK, H3]) for i in range(2)]
        kv = [sb(f"kv{i}", [C + D3, TOK, H3]) for i in range(2)]
        V = [sb(f"v{i}", [P, 2 * H3, H3, D3]) for i in range(2)]
        nm = [sb(f"nm{i}", [P, 2]) for i in range(2)]
        sm = [sb(f"sm{i}", [P, 2]) for i in range(2)]
        rc = [sb(f"rc{i}", [P, 2]) for i in range(2)]
        E = [sb(f"e{i}", [P, 3, P]) for i in range(2)]
        PT = [sb(f"pt{i}", [P, 3, P]) for i in range(2)]
        own = sb("own", [C, TOK, H3])
        OT = sb("ot", [C, TOK, H3])
        OR = [sb(f"or{i}", [C, TOK]) for i in range(2)]
        parts = ((0, 0, 1), (1, 1, 3))
        U = H3

        with nc.Block() as block:
            @block.gpsimd
            def _(pool):
                pool.tensor_copy(own[:], k.ingroup[:, None, :].broadcast_to([C, TOK, H3])).then_inc(s["own"], 1)

                def body(n, slot, first):
                    normalise(pool, k, s, n, 2, k.Y[slot][:, 0:2, :], k.bp3, k.v, k.r, n - 1)
                pairs(pool, IMAGES, body)

            @block.tensor
            def _(pe):
                def score(n, h, slot):
                    u = U * n + h
                    b = bank[4 + h % 2]
                    q = qx[slot][:].rearrange("p t g -> p (t g)")
                    kk = kv[slot][:].rearrange("p t g -> p (t g)")
                    if h == 0:
                        after(pe, s["qx"], n + 1)
                        after(pe, s["e"], 3 * (n + 1))
                    after(pe, s["exp"], u - 1)
                    pe.matmul(b[:, 0:P], q[:, h * TOK:h * TOK + P], kk[0:C, h * TOK:h * TOK + P], start=True, stop=False, skip_group_check=True)
                    pe.matmul(b[:, P:3 * P], q[:, h * TOK + P:(h + 1) * TOK], kk[0:C, h * TOK:(h + 1) * TOK], start=False, stop=False, skip_group_check=True)
                    pe.matmul(b[:].rearrange("p (a c) -> p a c", a=2)[:, :, 0:P], k.identb[:], k.causal[:, None, :].broadcast_to([P, 2, P]),
                              start=False, stop=True, skip_group_check=True).then_inc(s["sc"], 1)

                def probs(n, h):
                    u = U * n + h
                    after(pe, s["nrm"], u + 1)
                    after(pe, s["pte"], u - 1)
                    for i in range(3):
                        last = pe.transpose(bank[6 + h % 2][:, i * P:(i + 1) * P], E[h % 2][:, i, :], k.ident[:])
                    last.then_inc(s["pt"], 1)

                def values(n, h, slot):
                    u = U * n + h
                    after(pe, s["pte"], u + 1)
                    after(pe, s["ote"], u)
                    if h == 0:
                        after(pe, s["v"], n + 1)
                    for kc in range(2):
                        w = V[slot][:, 2 * h + kc, :, :].rearrange("p g d -> p (g d)")
                        last = pe.matmul(bank[3][0:C, kc * P:TOK], w, PT[h % 2][:, 2 * kc:2 + kc, :], start=(kc == 0), stop=(kc == 1), skip_group_check=True)
                    last.then_inc(s["av"], 1)

                def out(n, slot):
                    after(pe, s["red"], n + 1)
                    for t in range(2):
                        last = pe.matmul(bank[0][:, t * C:(t + 1) * C], OR[slot][:, t * P:(t + 1) * P], k.wp3[:], start=True, stop=True)
                    last.then_inc(s["out"], 1)

                def tokens(m, slot):
                    after(pe, s["y"], m + 1)
                    after(pe, s["x"], m - 2)
                    for t in range(2):
                        last = pe.transpose(bank[0][0:C, t * P:(t + 1) * P], k.Y[slot][:, t, :], k.ident[:])
                    last.then_inc(s["T"], 1)

                def project(m, j, slot):
                    if j == 0:
                        after(pe, s["hT"], m + 1)
                        after(pe, s["e"], 3 * m - 1)
                        pe.matmul(bank[1][0:C, 0:TOK], k.wq3[:], k.hT[slot][:, 0:TOK], start=True, stop=True).then_inc(s["pj"], 1)
                        return
                    after(pe, s["qx"] if j == 2 else s["e"], m + 1 if j == 2 else 3 * m + j // 2)
                    for i in range(2):
                        last = pe.matmul(bank[1 + j % 2][0:C + D3, i * TOK:(i + 1) * TOK], k.wkv3[:, 2 * j - 2 + i, :], k.hT[slot][:, 0:TOK], start=True, stop=True)
                    last.then_inc(s["pj"], 1)

                def value_rows(n, slot):
                    kk = kv[slot][:].rearrange("p t g -> p (t g)")
                    for j in range(2 * H3):
                        last = pe.transpose(bank[0][:, 256 + j * D3:256 + (j + 1) * D3], kk[C:C + D3, j * P:(j + 1) * P], k.ident[C:C + D3, C:C + D3])
                    last.then_inc(s["vt"], 1)

                def step(n, h, slot, start, end):
                    if h < U:
                        score(n, h, slot)
                    if h < 2:
                        if not start:
                            probs(n - 1, U + h - 2)
                    elif h < U + 2:
                        probs(n, h - 2)
                    if h < 3:
                        if not start:
                            values(n - 1, U + h - 3, 1 - slot)
                    else:
                        values(n, h - 3, slot)
                    if h == 0 and not end:
                        tokens(n + 1, 1 - slot)
                    elif h < 5 and not end:
                        project(n + 1, h - 1, 1 - slot)
                    if h == 1:
                        value_rows(n, slot)
                    if h == 4 and not start:
                        after(pe, s["v"], n + 1)
                        out(n - 1, 1 - slot)

                tokens(0, 0)
                for j in range(4):
                    project(0, j, 0)

                def body(n, slot, first, last):
                    for h in range(U):
                        step(n, h, slot, first, last)
                pipeline(pe, IMAGES, body)
                for h in range(U, U + 3):
                    step(IMAGES - 1, h, 1, False, True)
                out(IMAGES - 1, 1)

            @block.scalar
            def _(act):
                def exps(n, h):
                    u = U * n + h
                    after(act, s["nm"], u + 1)
                    after(act, s["pt"], u - 1)
                    after(act, s["rec"], u - 1)
                    for c, lo, hi in parts:
                        last = act.activation(E[h % 2][:, lo:hi, :], bank[4 + h % 2][:, lo * P:hi * P].rearrange("p (a b) -> p a b", b=P), ACT.Exp,
                                              bias=nm[h % 2][:, c:c + 1], accum_out=sm[h % 2][:, c:c + 1])
                    last.then_inc(s["exp"], 1)

                def pt_out(n, h):
                    u = U * n + h
                    after(act, s["pt"], u + 1)
                    after(act, s["av"], u - 1)
                    act.activation(PT[h % 2][:], bank[6 + h % 2][:, 0:3 * P].rearrange("p (a b) -> p a b", b=P), ACT.Copy).then_inc(s["pte"], 1)

                def tokens(m, slot):
                    after(act, s["T"], m + 1)
                    after(act, s["pj"], 4 * (m - 1))
                    act.activation(k.hT[slot][:, 0:TOK], bank[0][0:C, 0:TOK], ACT.Copy).then_inc(s["hT"], 1)

                def project(m, j, slot):
                    after(act, s["pj"], 4 * m + j + 1)
                    after(act, s["sc"], U * (m - 1))
                    after(act, s["vt"], m - 1)
                    act.activation(kv[slot][:].rearrange("p t g -> p g t")[:, 2 * j - 2:2 * j, :],
                                   bank[1 + j % 2][0:C + D3, :].rearrange("p (g t) -> p g t", g=2), ACT.Copy).then_inc(s["e"], 1)

                tokens(0, 0)
                for j in range(1, 4):
                    project(0, j, 0)

                def body(n, slot, first, last):
                    for h in range(U):
                        if h >= 2:
                            pt_out(n, h - 2)
                        elif not first:
                            pt_out(n - 1, U + h - 2)
                        exps(n, h)
                        if not last:
                            if h == 0:
                                tokens(n + 1, 1 - slot)
                            elif h >= 3:
                                project(n + 1, h - 2, 1 - slot)
                pipeline(act, IMAGES, body)
                pt_out(IMAGES - 1, U - 2)
                pt_out(IMAGES - 1, U - 1)

            @block.vector
            def _(dve):
                def maxima(n, h):
                    u = U * n + h
                    after(dve, s["sc"], u + 1)
                    after(dve, s["exp"], u - 1)
                    for c, lo, hi in parts:
                        last = dve.tensor_reduce(nm[h % 2][:, c:c + 1], bank[4 + h % 2][:, lo * P:hi * P], AX.X, ALU.max, negate=True)
                    last.then_inc(s["nm"], 1)

                def norm(n, h):
                    u = U * n + h
                    after(dve, s["exp"], u + 1)
                    after(dve, s["nrm"], u - 1)
                    dve.reciprocal(rc[h % 2][:], sm[h % 2][:]).then_inc(s["rec"], 1)
                    after(dve, s["rec"], u + 1)
                    for c, lo, hi in parts:
                        last = dve.tensor_scalar(E[h % 2][:, lo:hi, :], E[h % 2][:, lo:hi, :], rc[h % 2][:, c:c + 1], None, ALU.mult)
                    last.then_inc(s["nrm"], 1)

                def head_out(n, h, slot):
                    after(dve, s["av"], U * n + h + 1)
                    rows = slice(h * TOK, (h + 1) * TOK)
                    dve.tensor_tensor(OT[:].rearrange("p t g -> p (t g)")[:, rows], bank[3][0:C, 0:TOK],
                                      own[:].rearrange("p t g -> p (t g)")[:, rows], ALU.mult).then_inc(s["ote"], 1)
                    if h == U - 1:
                        after(dve, s["ote"], U * (n + 1))
                        after(dve, s["out"], n - 1)
                        dve.tensor_reduce(OR[slot][:], OT[:], AX.X, ALU.add).then_inc(s["red"], 1)

                def residual(n):
                    after(dve, s["out"], n + 1)
                    after(dve, s["xb"], n + 1)
                    add_and_stats(dve, k, s, n, 2, bank[0][:, 0:2 * C].rearrange("p (t c) -> p t c", t=2), k.stats, k.aggr)

                def queries(m, slot):
                    after(dve, s["pj"], 4 * m + 1)
                    after(dve, s["sc"], U * (m - 1))
                    dve.tensor_tensor(qx[slot][:], bank[1][0:C, 0:TOK, None].broadcast_to([C, TOK, H3]),
                                      k.groupmask[:, None, :].broadcast_to([C, TOK, H3]), ALU.mult).then_inc(s["qx"], 1)

                def value_rows(n, slot):
                    after(dve, s["vt"], n + 1)
                    after(dve, s["av"], U * (n - 1))
                    dve.tensor_copy(V[slot][:], bank[0][:, 256:256 + 2 * H3 * D3].rearrange("p (j d) -> p j d", d=D3)[:, :, None, :]
                                    .broadcast_to([P, 2 * H3, H3, D3])).then_inc(s["v"], 1)

                dve.wait_ge(s["own"], 1)
                queries(0, 0)

                def body(n, slot, first, last):
                    for h in range(U):
                        maxima(n, h)
                        if h >= 1:
                            norm(n, h - 1)
                        elif not first:
                            norm(n - 1, U - 1)
                        if h >= 3:
                            head_out(n, h - 3, slot)
                        elif not first:
                            head_out(n - 1, U + h - 3, 1 - slot)
                        if h == 1:
                            value_rows(n, slot)
                        if h == 2 and not last:
                            queries(n + 1, 1 - slot)
                        if h == 5 and not first:
                            residual(n - 1)
                pipeline(dve, IMAGES, body)
                norm(IMAGES - 1, U - 1)
                for h in range(U - 3, U):
                    head_out(IMAGES - 1, h, 1)
                residual(IMAGES - 1)


def experts(k, bank, out):
    nc = k.nc
    s = k.sems("ex", LN_SEMS + "T hT keep gl lb mx sub exp sum rec pr cmp rank m rd up gelu down acc b2 xo st g1 g2 gd g3 g4 g5")
    steps = TILES // 4
    with ExitStack() as ctx:
        def sb(name, shape, dt=F32):
            return k.sb("ex_" + name, shape, dt, ctx)

        HT = sb("HT", [C, steps, 512])
        L = sb("L", [P, TILES, EXPERTS])
        one = sb("one", [P, TILES, 1])
        ge = sb("ge", [P, TILES, EXPERTS, EXPERTS])
        gt = sb("gt", [P, TILES, EXPERTS, EXPERTS])
        rank = sb("rank", [P, TILES, EXPERTS])
        tmp = [sb(f"tmp{i}", [P, 4, C]) for i in range(2)]
        G = [sb(f"G{i}", [P, KH, 512]) for i in range(2)]
        full = [P, TILES, EXPERTS]

        with nc.Block() as block:
            @block.gpsimd
            def _(pool):
                def body(n, slot, first):
                    normalise(pool, k, s, n, 4, k.Y[slot][:], None, k.v, k.r, n - 1)
                    after(pool, s["hT"], n + 1)
                    pool.tensor_copy(HT[:, bass.ds(n, 1), :], k.hT[slot][:, None, :]).then_inc(s["keep"], 1)
                pairs(pool, steps, body)

            @block.tensor
            def _(pe):
                def body(n, slot, first):
                    after(pe, s["y"], n + 1)
                    after(pe, s["hT"], n - 1)
                    for t in range(4):
                        last = pe.transpose(bank[slot][0:C, t * P:(t + 1) * P], k.Y[slot][:, t, :], k.ident[:])
                    last.then_inc(s["T"], 1)
                    after(pe, s["hT"], n + 1)
                    after(pe, s["lb"], n - 1)
                    for t in range(4):
                        last = pe.matmul(bank[2 + slot][:, t * EXPERTS:(t + 1) * EXPERTS], k.hT[slot][:, t * P:(t + 1) * P], k.gw[:], start=True, stop=True)
                    last.then_inc(s["gl"], 1)
                pairs(pe, steps, body)

            @block.scalar
            def _(act):
                def body(n, slot, first):
                    after(act, s["T"], n + 1)
                    after(act, s["gl"], n - 1)
                    after(act, s["keep"], n - 1)
                    act.activation(k.hT[slot][:], bank[slot][0:C, :], ACT.Copy).then_inc(s["hT"], 1)
                pairs(act, steps, body)
                act.wait_ge(s["sub"], 1)
                act.activation(L[:], L[:], ACT.Exp).then_inc(s["exp"], 1)

            @block.vector
            def _(dve):
                def body(n, slot, first):
                    after(dve, s["gl"], n + 1)
                    dve.tensor_tensor(tiles_of(L, n * 4, 4), bank[2 + slot][:, 0:4 * EXPERTS].rearrange("p (t e) -> p t e", e=EXPERTS),
                                      k.gb[:, None, :].broadcast_to([P, 4, EXPERTS]), ALU.add).then_inc(s["lb"], 1)
                pairs(dve, steps, body)
                dve.wait_ge(s["lb"], steps)
                dve.tensor_reduce(one[:, :, 0], L[:], AX.X, ALU.max).then_inc(s["mx"], 1)
                dve.wait_ge(s["mx"], 1)
                dve.tensor_tensor(L[:], L[:], one[:].broadcast_to(full), ALU.subtract).then_inc(s["sub"], 1)
                dve.wait_ge(s["exp"], 1)
                dve.tensor_reduce(one[:, :, 0], L[:], AX.X, ALU.add).then_inc(s["sum"], 1)
                dve.wait_ge(s["sum"], 1)
                dve.reciprocal(one[:], one[:]).then_inc(s["rec"], 1)
                dve.wait_ge(s["rec"], 1)
                dve.tensor_tensor(L[:], L[:], one[:].broadcast_to(full), ALU.mult).then_inc(s["pr"], 1)
                dve.wait_ge(s["pr"], 1)
                square = [P, TILES, EXPERTS, EXPERTS]
                other, own = L[:, :, None, :].broadcast_to(square), L[:, :, :, None].broadcast_to(square)
                dve.tensor_tensor(ge[:], other, own, ALU.is_ge).then_inc(s["cmp"], 1)
                dve.tensor_tensor(gt[:], other, own, ALU.is_gt).then_inc(s["cmp"], 1)
                dve.wait_ge(s["cmp"], 2)
                dve.tensor_tensor(ge[:], ge[:], k.lower[:, None, :, :].broadcast_to(square), ALU.mult).then_inc(s["cmp"], 1)
                dve.wait_ge(s["cmp"], 3)
                dve.tensor_tensor(gt[:], gt[:], ge[:], ALU.max).then_inc(s["cmp"], 1)
                dve.wait_ge(s["cmp"], 4)
                dve.tensor_reduce(rank[:], gt[:], AX.X, ALU.add).then_inc(s["rank"], 1)
                dve.wait_ge(s["rank"], 1)
                dve.tensor_scalar(rank[:], rank[:], 2.0, None, ALU.is_lt).then_inc(s["rank"], 1)
                dve.wait_ge(s["rank"], 2)
                dve.tensor_tensor(L[:], L[:], rank[:], ALU.mult).then_inc(s["m"], 1)
                dve.wait_ge(s["m"], 1)
                dve.tensor_reduce(one[:, :, 0], L[:], AX.X, ALU.add).then_inc(s["g1"], 1)
                dve.wait_ge(s["g1"], 1)
                dve.tensor_scalar(one[:], one[:], 1e-9, None, ALU.add).then_inc(s["g2"], 1)
                dve.wait_ge(s["g2"], 1)
                dve.reciprocal(one[:], one[:]).then_inc(s["gd"], 1)
                dve.wait_ge(s["gd"], 1)
                dve.tensor_tensor(L[:], L[:], one[:].broadcast_to(full), ALU.mult).then_inc(s["m"], 1)

        with nc.Block() as block:
            @block.gpsimd
            def _(pool):
                def body(n, slot, first):
                    own = tiles_of(L, n * 4, 4)
                    b = k.eb2[:, :, None, :]
                    wide = [P, 4, C]
                    after(pool, s["xb"], n)
                    pool.tensor_tensor(tmp[0][:], b[:, 0].broadcast_to(wide), own[:, :, 0:1].broadcast_to(wide), ALU.mult).then_inc(s["g4"], 1)
                    for e in range(1, EXPERTS):
                        u = (EXPERTS - 1) * n + e
                        after(pool, s["g5"], u - 1)
                        pool.tensor_tensor(tmp[1][:], b[:, e].broadcast_to(wide), own[:, :, e:e + 1].broadcast_to(wide), ALU.mult).then_inc(s["g3"], 1)
                        after(pool, s["g4"], n + 1)
                        after(pool, s["g3"], u)
                        pool.tensor_tensor(tmp[0][:], tmp[0][:], tmp[1][:], ALU.add).then_inc(s["g5"], 1)
                    x = tiles_of(k.X, n * 4, 4)
                    alone(pool, k)
                    after(pool, s["g5"], (EXPERTS - 1) * (n + 1))
                    pool.tensor_tensor(x, x, tmp[0][:], ALU.add).then_inc(s["xb"], 1)
                pairs(pool, steps, body)

            @block.tensor
            def _(pe):
                def down(n, e):
                    u = EXPERTS * n + e
                    after(pe, s["gelu"], KH * (u + 1))
                    after(pe, s["acc"], 4 * (u - 1))
                    for t in range(4):
                        for j in range(KH):
                            last = pe.matmul(bank[6 + e % 2][:, t * C:(t + 1) * C], G[e % 2][:, j, t * P:(t + 1) * P], k.ew2[:, e, j, :],
                                             start=(j == 0), stop=(j == KH - 1))
                    last.then_inc(s["down"], 1)

                def body(n, first):
                    for e in range(EXPERTS):
                        u = EXPERTS * n + e
                        after(pe, s["gelu"], KH * (u - 1))
                        for j in range(KH):
                            pe.matmul(bank[3 * (e % 2) + j][:], k.ew1[:, e, j * P:(j + 1) * P], HT[:, bass.ds(n, 1), :], start=True, stop=True).then_inc(s["up"], 1)
                        if e:
                            down(n, e - 1)
                        elif not first:
                            down(n - 1, EXPERTS - 1)
                body(0, True)
                with pe.Fori(1, steps) as n:
                    body(n, False)
                down(steps - 1, EXPERTS - 1)

            @block.scalar
            def _(act):
                def body(n):
                    for e in range(EXPERTS):
                        u = EXPERTS * n + e
                        after(act, s["down"], u - 1)
                        for j in range(KH):
                            after(act, s["up"], KH * u + j + 1)
                            act.activation(G[e % 2][:, j, :], bank[3 * (e % 2) + j][:], ACT.Gelu, bias=k.eb1[:, e, j:j + 1]).then_inc(s["gelu"], 1)
                body(0)
                with act.Fori(1, steps) as n:
                    body(n)

            @block.vector
            def _(dve):
                def body(n):
                    after(dve, s["xb"], n + 1)
                    for e in range(EXPERTS):
                        u = EXPERTS * n + e
                        after(dve, s["down"], u + 1)
                        after(dve, s["acc"], 4 * u)
                        for t in range(4):
                            x = k.X[:, bass.ds(n * 4 + t, 1), :]
                            dve.scalar_tensor_tensor(out=x, in0=bank[6 + e % 2][:, None, t * C:(t + 1) * C], scalar=L[:, bass.ds(n * 4 + t, 1), e],
                                                     in1=x, op0=ALU.mult, op1=ALU.add).then_inc(s["acc"], 1)
                body(0)
                with dve.Fori(1, steps) as n:
                    body(n)

            @block.sync
            def _(sp):
                sp.wait_ge(s["acc"], 4 * EXPERTS * steps)
                sp.dma_start(out.rearrange("b (y i) c d -> (i c) (b y) d", y=2), k.X[:]).then_inc(s["st"], 16)
                sp.wait_ge(s["st"], 16)


def build(nc, a, out, upto=99):
    with ExitStack() as ctx:
        k = Core(nc, ctx)
        bank = [ctx.enter_context(nc.psum_tensor(f"bank{i}", [P, 512], F32)) for i in range(8)]
        setup(k, a)
        k.end_phase()
        phases = ((window_attention, ()), (mlp, ("ml0", k.mlp0)), (conv_mixer, ()), (mlp, ("ml1", k.mlp1)),
                  (full_attention, ()), (binary_ffn, ()), (causal_attention, ()), (experts, (out,)))
        for phase, more in phases:
            phase(k, bank, *more)
            k.end_phase()


def constants():
    f = np.float32
    decay, gain = 0.6, 0.4
    d = np.abs(np.arange(SIDE)[:, None] - np.arange(SIDE)[None, :])
    scan = gain * decay ** d * (1 + (d == 0))
    eye = np.eye(SIDE)
    mixer = np.eye(TOK) + 0.25 * (np.kron(eye, scan) + np.kron(scan, eye))
    tok = np.arange(TOK).reshape(2, WS, 2, WS).transpose(0, 2, 1, 3).reshape(-1)
    return {
        "ident": np.eye(P, dtype=f),
        "mixer": mixer.astype(f),
        "perm": (tok[0:P, None] == np.arange(P)[None, :]).astype(f),
        "headmask": (np.arange(C)[:, None] // D0 == np.arange(H0)[None, :]).astype(f),
        "ingroup": (np.arange(C)[:, None] // D3 == np.arange(H3)[None, :]).astype(f),
        "groupmask": ((np.arange(C)[:, None] // D3 == np.arange(H3)[None, :]) * float(C) ** -0.5).astype(f),
        "causal": np.where(np.arange(P)[:, None] >= np.arange(P)[None, :], 0.0, -1e30).astype(f),
        "lower": (np.arange(EXPERTS)[None, :] < np.arange(EXPERTS)[:, None]).astype(f),
    }


def kernel(**inputs):
    import concourse.bacc as bacc
    from concourse.bass_utils import run_bass_kernel_spmd

    nc = bacc.Bacc("TRN2", target_bir_lowering=False, num_devices=1)
    arrays = {name: np.ascontiguousarray(value) for name, value in inputs.items()}
    arrays.update(constants())
    a = {name: nc.dram_tensor(f"in_{name}", v.shape, mybir.dt.from_np(v.dtype), kind="ExternalInput").ap()
         for name, v in arrays.items()}
    out = nc.dram_tensor("out_tokens", (IMAGES, SIDE, SIDE, C), F32, kind="ExternalOutput").ap()
    build(nc, a, out)
    r = run_bass_kernel_spmd(nc, [{f"in_{name}": v for name, v in arrays.items()}], core_ids=[0])
    return r.results[0]["out_tokens"]
```

```python
from contextlib import ExitStack

import numpy as np

import concourse.bass as bass
from concourse import mybir

F32 = mybir.dt.float32
BF16 = mybir.dt.bfloat16
ALU = mybir.AluOpType
ACT = mybir.ActivationFunctionType
AX = mybir.AxisListType

P = 128
IMAGES = 16
SIDE = 16
TOK = SIDE * SIDE
C = 96
TILES = IMAGES * TOK // P
HID = 4 * C
KH = HID // P
LN_EPS = 1e-5
WS = 8
WTOK = WS * WS
H0 = 12
D0 = C // H0
CI = 2 * C
H2, D2 = 8, 48
PAIRS2 = H2 // 2
H3 = 6
D3 = C // H3
GRID = SIDE + 2
GROUPS = 5
GIMG = IMAGES // GROUPS
GT = 2 * GIMG
EXPERTS = 4
EPS_Q = 1e-5
QB = 128.0


def after(eng, sem, count):
    if not isinstance(count, int) or count > 0:
        eng.wait_ge(sem, count)


def alone(eng, k):
    eng.wait_ge(k.started, 1)


def pairs(eng, steps, body):
    for s in range(2):
        body(s, s, s == 0)
    with eng.Fori(1, steps // 2) as g:
        for s in range(2):
            body(g * 2 + s, s, False)


class Core:

    def __init__(self, nc, ctx):
        self.nc, self.ctx = nc, ctx
        self.retired = []
        self.started = nc.alloc_semaphore(name="started")

    def sb(self, name, shape, dt=F32, ctx=None):
        return (ctx or self.ctx).enter_context(self.nc.sbuf_tensor(name, shape, dt))

    def sems(self, prefix, names):
        self.live = {n: self.nc.alloc_semaphore(name=f"{prefix}_{n}") for n in names.split()}
        return self.live

    def end_phase(self):
        self.retired = list(self.live.values())

    def clear_retired(self):
        self.nc.clear_and_free_semaphores(self.retired)


def pipeline(eng, steps, body):
    for q in range(2):
        body(q, q, q == 0, False)
    with eng.Fori(1, steps // 2 - 1) as g:
        for q in range(2):
            body(g * 2 + q, q, False, False)
    for q in range(2):
        body(steps - 2 + q, q, False, q == 1)


def exists(n, steps):
    return not isinstance(n, int) or 0 <= n < steps


def tiles_of(t, first, count):
    return t[:, bass.ds(first, count), :]


def normalise(pool, k, s, n, count, y, bias, free, tiles=None):
    if tiles is None and isinstance(n, int) and n == 0:
        for i, name in enumerate(("var", "centred", "rstd", "y") + (() if bias is None else ("xb",))):
            pool.memset(k.flags[:, i:i + 1], 0.0).then_inc(s[name], 1)
        return
    tiles = n * count if tiles is None else tiles
    x = tiles_of(k.X, tiles, count)
    mean = tiles_of(k.MV, tiles, count)[:, :, 0:1]
    var = tiles_of(k.MV, tiles, count)[:, :, 1:2]
    v, r = k.v[:, 0:count, :], k.r[:, 0:count, :]
    alone(pool, k)
    after(pool, s["T"], free)
    pool.tensor_tensor(v, var, k.eps[:, 0:count, :], ALU.add).then_inc(s["var"], 1)
    pool.tensor_tensor(y, x, mean.broadcast_to([P, count, C]), ALU.subtract).then_inc(s["centred"], 1)
    pool.wait_ge(s["var"], n + 1)
    pool.tensor_tensor(r, v, k.minus_half[:, 0:count, :], ALU.pow).then_inc(s["rstd"], 1)
    alone(pool, k)
    pool.wait_ge(s["rstd"], n + 1)
    pool.wait_ge(s["centred"], n + 1)
    pool.tensor_tensor(y, y, r.broadcast_to([P, count, C]), ALU.mult).then_inc(s["y"], 1)
    if bias is not None:
        pool.tensor_tensor(x, x, bias[:, None, :].broadcast_to([P, count, C]), ALU.add).then_inc(s["xb"], 1)


def next_first_step(pool, k, s, steps):
    count, bias = k.next_norm
    pool.wait_ge(s["mv"], 4)
    normalise(pool, k, s, steps, count, k.Y[0][:, 0:count, :], bias, steps, 0)


def add_new(dve, k, s, n, count, new, replace=False):
    x = tiles_of(k.X, n * count, count)
    (dve.tensor_copy(x, new) if replace else dve.tensor_tensor(x, x, new, ALU.add)).then_inc(s["x"], 1)


def statistics(dve, k, s, n, count):
    alone(dve, k)
    dve.wait_ge(s["x"], n + 1)
    after(dve, s["mv"], n)
    for t in range(count):
        last = dve.bn_stats(k.stats[:, t, :], k.X[:, bass.ds(n * count + t, 1), :])
    last.then_inc(s["bn"], 1)
    alone(dve, k)
    dve.wait_ge(s["bn"], n + 1)
    for t in range(count):
        last = dve.bn_aggr(k.aggr[:, t, :], k.stats[:, t, :])
    last.then_inc(s["ag"], 1)
    dve.wait_ge(s["ag"], n + 1)
    dve.tensor_copy(tiles_of(k.MV, n * count, count), k.aggr[:, 0:count, :]).then_inc(s["mv"], 1)


def add_and_stats(dve, k, s, n, count, new, replace=False):
    add_new(dve, k, s, n, count, new, replace)
    statistics(dve, k, s, n, count)


LN_SEMS = "var centred rstd y xb x bn ag mv "


def setup(k, bank, a):
    nc = k.nc
    s = k.sems("set", "x w ones bv bvwp cst bn ag mv")
    sb = k.sb
    k.X = sb("X", [P, TILES, C])
    k.MV = sb("MV", [P, TILES, 2])
    k.ident = sb("ident", [P, P])
    k.identb = sb("identb", [P, P], BF16)
    k.causal = sb("causal", [P, P], BF16)
    k.eps = sb("eps", [P, 8, 1])
    k.minus_half = sb("minus_half", [P, 8, 1])
    k.ones = sb("ones", [P, P])
    k.stats = sb("stats", [P, 8, 6])
    k.aggr = sb("aggr", [P, 8, 2])
    k.v, k.r = sb("ln_v", [P, 8, 1]), sb("ln_r", [P, 8, 1])
    k.Y = [sb(f"Y{i}", [P, 2 * GIMG, C]) for i in range(2)]
    k.flags = sb("flags", [P, 5])
    k.hT = [sb(f"hT{i}", [C, 512]) for i in range(2)]
    loads = []

    def weight(name, shape, src, dst=None):
        t = sb(name, shape)
        loads.append((t[:] if dst is None else dst(t), src))
        return t

    def column(name, src):
        return weight(name, [src.shape[0], 1], src[:, None])

    def row(name, src):
        return weight(name, [P, src.shape[0]], src[None, :].broadcast_to([P, src.shape[0]]))

    k.g1, k.b1 = column("w_g1", a["L0_conv_ln1_w"]), column("w_b1", a["L0_conv_ln1_b"])
    k.wqkv0 = weight("w_qkv0", [P, 3 * C], a["L0_conv_qkv_w"], lambda t: t[0:C, :])
    k.bq0 = column("w_bq0", a["L0_conv_qkv_b"][0:C])
    k.bk0 = column("w_bk0", a["L0_conv_qkv_b"][C:2 * C])
    bv0 = column("w_bv0", a["L0_conv_qkv_b"][2 * C:3 * C])
    bv0_wide = sb("bv0_wide", [C, P])
    k.wp0 = weight("w_p0", [C, C], a["L0_conv_proj_w"])
    bp0 = row("w_bp0", a["L0_conv_proj_b"])
    k.bp0 = sb("bp0", [P, C])
    k.headmask = weight("headmask", [C, H0], a["headmask"])
    k.bias0 = sb("bias0", [P, WTOK, H0])
    bias0r = sb("bias0r", [P, WTOK, H0])
    table = a["L0_conv_rpb_table"]
    span = 2 * WS - 1
    for wx in range(2):
        for qy in range(WS):
            src = bass.AP(tensor=table.tensor, offset=qy * span * H0, ap=[[H0, WS], [span * H0, WS], [1, WS * H0]])
            p0 = wx * WTOK + qy * WS
            loads.append((bias0r[p0:p0 + WS].rearrange("q (y x) h -> q y (x h)", y=WS), src))

    def mlp(p, g, b, w1, b1, w2, b2):
        return dict(g=column(p + "g", g), b=column(p + "b", b), w1=weight(p + "w1", [C, HID], w1),
                    b1=weight(p + "b1", [P, KH], b1.rearrange("(k p) -> p k", p=P)),
                    w2=weight(p + "w2", [P, KH, C], w2.rearrange("(k p) c -> p k c", p=P)), b2=row(p + "b2", b2))

    stage = weight("causal_f", [P, P], a["causal"])
    loads.append((k.ident[:], a["ident"]))
    k.late = []
    first, loads = loads, k.late

    k.mlp0 = mlp("m0", a["L0_conv_ln2_w"], a["L0_conv_ln2_b"], a["L0_conv_mlp_w1"], a["L0_conv_mlp_b1"],
                 a["L0_conv_mlp_w2"], a["L0_conv_mlp_b2"])
    k.g3, k.b3 = column("w_g3", a["L1_conv_n1_g"]), column("w_b3", a["L1_conv_n1_b"])
    k.win = weight("w_in", [C, CI], a["L1_conv_w_in"])
    k.bin = weight("b_in", [C, 2], a["L1_conv_b_in"].rearrange("(j p) -> p j", p=C))
    k.kconv = sb("k_conv", [C, 2, 9])
    for j in range(2):
        loads.append((k.kconv[:, j, :], a["L1_conv_k_conv"].rearrange("a b o (j p) -> j p (a b o)", p=C)[j]))
    k.ong = weight("on_g", [C, 2], a["L1_conv_on_g"].rearrange("(j p) -> p j", p=C))
    k.onb = weight("on_b", [C, 2], a["L1_conv_on_b"].rearrange("(j p) -> p j", p=C))
    k.wout = weight("w_out", [C, 2, C], a["L1_conv_w_out"].rearrange("(j p) c -> p j c", p=C))
    k.bout = row("b_out", a["L1_conv_b_out"])
    k.perm = weight("perm", [P, P], a["perm"])
    k.mixer = weight("mixer", [P, 2, TOK], a["mixer"].rearrange("(j p) t -> p j t", p=P))
    k.mlp1 = mlp("m1", a["L1_conv_n2_g"], a["L1_conv_n2_b"], a["L1_conv_w1"], a["L1_conv_b1"],
                 a["L1_conv_w2"], a["L1_conv_b2"])
    wide = [C, PAIRS2, 2, 64]
    k.wq2, k.wk2 = sb("w_q2", wide), sb("w_k2", wide)
    for part, t in enumerate((k.wq2, k.wk2)):
        for p in range(PAIRS2):
            base = part * H2 * D2 + p * 2 * D2
            loads.append((t[:, p, :, 0:D2], a["L2_attn_Wqkv"][:, base:base + 2 * D2].rearrange("c (h d) -> c h d", h=2)))
    k.wv2 = weight("w_v2", [C, H2 * D2], a["L2_attn_Wqkv"][:, 2 * H2 * D2:3 * H2 * D2])
    k.wp2 = sb("w_p2", [P, PAIRS2, C])
    for h in range(2):
        loads.append((k.wp2[64 * h:64 * h + D2, :, :],
                      a["L2_attn_Wproj"].rearrange("(p h d) c -> h d p c", h=2, d=D2)[h]))
    k.bp2 = row("w_bp2", a["L2_attn_bproj"])
    k.fb1 = weight("f_b1", [P, KH], a["L2_ffn_b1"].rearrange("(k p) -> p k", p=P))
    k.fb2 = row("f_b2", a["L2_ffn_b2"])
    k.wq3 = weight("w_q3", [C, C], a["L3_attn_Wq"])
    k.wkv3 = sb("w_kv3", [C, H3, C + D3])
    for g in range(H3):
        loads.append((k.wkv3[:, g, 0:C].rearrange("c (i d) -> c i d", d=D3),
                      a["L3_attn_Wk"][:, None, g * D3:(g + 1) * D3].broadcast_to([C, H3, D3])))
    loads.append((k.wkv3[:, :, C:C + D3], a["L3_attn_Wv"].rearrange("c (g d) -> c g d", d=D3)))
    k.groupmask = weight("groupmask", [C, H3], a["groupmask"])
    k.ingroup = weight("ingroup", [C, H3], a["ingroup"])
    k.wp3 = weight("w_p3", [C, C], a["L3_attn_Wp"])
    k.bp3 = row("w_bp3", a["L3_attn_bp"])
    k.gw = weight("w_gate", [C, EXPERTS], a["L3_ffn_gate_w"])
    k.gb = row("b_gate", a["L3_ffn_gate_b"])
    k.ew1 = weight("e_w1", [C, EXPERTS, HID], a["L3_ffn_w1"].rearrange("e c h -> c e h"))
    k.eb1 = weight("e_b1", [P, EXPERTS, KH], a["L3_ffn_b1"].rearrange("e (k p) -> p e k", p=P))
    k.ew2 = weight("e_w2", [P, EXPERTS, KH, C], a["L3_ffn_w2"].rearrange("e (k p) c -> p e k c", p=P))
    k.eb2 = weight("e_b2", [P, EXPERTS, C], a["L3_ffn_b2"][None, :, :].broadcast_to([P, EXPERTS, C]))
    k.lower = weight("lower", [P, EXPERTS, EXPERTS], a["lower"][None, :, :].broadcast_to([P, EXPERTS, EXPERTS]))
    k.g76, k.g19 = HID // GROUPS, C // GROUPS
    k.less1, k.less2 = sb("f_less1", [k.g76, GROUPS, C]), sb("f_less2", [k.g19, GROUPS, HID])
    k.part = sb("f_part", [P, 2, GROUPS])
    k.mean = sb("f_mean", [P, 2, GROUPS])
    k.f1 = weight("f_w1", [k.g76, GROUPS, C], a["L2_ffn_W1"][0:GROUPS * k.g76, :].rearrange("(g o) c -> o g c", g=GROUPS))
    k.f2 = weight("f_w2", [k.g19, GROUPS, HID], a["L2_ffn_W2"][0:GROUPS * k.g19, :].rearrange("(g o) c -> o g c", g=GROUPS))

    with nc.Block() as block:
        @block.sync
        def _(sp):
            for wx in range(2):
                for r in range(WS):
                    p0 = wx * WTOK + r * WS
                    src = a["x"].rearrange("b (y i) (v c) d -> v i c (b y) d", i=WS, c=WS)[wx, r]
                    sp.dma_start(k.X[p0:p0 + WS, :, :], src).then_inc(s["x"], 16)
            sp.wait_ge(s["x"], 16 * 2 * WS)

        @block.gpsimd
        def _(pool):
            pool.memset(k.eps[:], LN_EPS).then_inc(k.started, 1)
            pool.memset(k.minus_half[:], -0.5)
            for t in (k.wq2, k.wk2, k.wp2, k.part, k.ones):
                last = pool.memset(t[:], 1.0 if t is k.ones else 0.0)
            last.then_inc(s["ones"], 1)
            pool.wait_ge(s["w"], 16 * len(first))
            pool.wait_ge(s["ones"], 1)
            pool.tensor_scalar(bv0_wide[:], k.ones[0:C, :], bv0[:], 0.0, ALU.mult, ALU.add).then_inc(s["bv"], 1)
            pool.tensor_copy(k.identb[:], k.ident[:])
            pool.tensor_copy(k.bias0[:], bias0r[:, ::-1, :])
            pool.tensor_copy(k.causal[:], stage[:]).then_inc(s["cst"], 1)

        @block.tensor
        def _(pe):
            pe.wait_ge(s["w"], 16 * len(first))
            pe.wait_ge(s["bv"], 1)
            pe.matmul(bank[0][:, 0:C], bv0_wide[:], k.wp0[:], start=True, stop=True).then_inc(s["bvwp"], 1)

        @block.scalar
        def _(act):
            for dst, src in first:
                act.dma_start(dst, src, allow_slow_non_contiguous=True).then_inc(s["w"], 16)
            act.wait_ge(s["w"], 16 * len(first))

        @block.vector
        def _(dve):
            dve.memset(k.wqkv0[C:P, :], 0.0)
            dve.wait_ge(s["x"], 16 * 2 * WS)
            for n in range(TILES // 4):
                for t in range(4):
                    last = dve.bn_stats(k.stats[:, t, :], k.X[:, bass.ds(n * 4 + t, 1), :])
                last.then_inc(s["bn"], 1)
                dve.wait_ge(s["bn"], n + 1)
                for t in range(4):
                    last = dve.bn_aggr(k.aggr[:, t, :], k.stats[:, t, :])
                last.then_inc(s["ag"], 1)
                dve.wait_ge(s["ag"], n + 1)
                dve.tensor_copy(tiles_of(k.MV, n * 4, 4), k.aggr[:, 0:4, :]).then_inc(s["mv"], 1)
                dve.wait_ge(s["mv"], n + 1)
            dve.wait_ge(s["bvwp"], 1)
            dve.tensor_tensor(k.bp0[:], bank[0][:, 0:C], bp0[:], ALU.add).then_inc(s["cst"], 1)


def window_attention(k, bank):
    nc = k.nc
    s = k.sems("wa", LN_SEMS + "late init pad bq T hT qk q kx vp v sc add mx sub exp pt pte av rec a oT oTe pj")
    with ExitStack() as ctx:
        def sb(name, shape, dt=F32):
            return k.sb("wa_" + name, shape, dt, ctx)

        bqs = sb("bqs", [C, 1])
        h2 = [sb(f"h2{i}", [P, 4, 2, WTOK]) for i in range(2)]
        qT = [sb(f"q{i}", [P, TOK]) for i in range(2)]
        kx = [sb(f"kx{i}", [P, H0, TOK]) for i in range(2)]
        vb = [sb(f"vb{i}", [P, 4, H0 // 2, 2 * D0 + 2]) for i in range(2)]
        S = [sb(f"s{i}", [P, H0, WTOK]) for i in range(2)]
        E = [sb(f"e{i}", [P, H0, WTOK]) for i in range(2)]
        mx = [sb(f"mx{i}", [P, H0, 1]) for i in range(2)]
        PT = sb("pt", [P, 2, 3, P])
        rec = sb("rec", [P, H0 // 2, 2, 1])
        A = [sb(f"a{i}", [P, 2, C]) for i in range(2)]
        AT = sb("at", [C, TOK])
        scale = float(D0) ** -0.5

        with nc.Block() as block:
            @block.sync
            def _(sp):
                for dst, src in k.late:
                    sp.dma_start(dst, src, allow_slow_non_contiguous=True).then_inc(s["late"], 16)
                sp.wait_ge(s["late"], 16 * len(k.late))

            @block.gpsimd
            def _(pool):
                k.clear_retired()
                for i in range(2):
                    pool.memset(vb[i][:], 0.0).then_inc(s["bq"], 1)
                pool.wait_ge(s["bq"], 2)
                for i in range(2):
                    pool.memset(vb[i][0:WTOK, :, :, 2 * D0:2 * D0 + 1], 1.0).then_inc(s["init"], 1)
                    pool.wait_ge(s["init"], i + 1)
                    pool.memset(vb[i][WTOK:P, :, :, 2 * D0 + 1:2 * D0 + 2], 1.0).then_inc(s["bq"], 1)
                    pool.wait_ge(s["bq"], 3 + i)
                pool.tensor_scalar(bqs[:], k.bq0[:], scale, 0.0, ALU.mult, ALU.add).then_inc(s["bq"], 1)
                pool.wait_ge(s["bq"], 5)

                def norm(n, slot):
                    normalise(pool, k, s, n, 2, k.Y[slot][:, 0:2, :], k.bp0, n - 1)
                normalise(pool, k, s, 0, 2, k.Y[0][:, 0:2, :], k.bp0, 0, 0)
                norm(1, 1)

                def body(n, slot, first, last):
                    for t in range(2):
                        pool.wait_ge(s["mx"], 2 * n + t + 1)
                        pool.tensor_tensor(S[t][:], S[t][:], mx[t][:].broadcast_to([P, H0, WTOK]), ALU.subtract).then_inc(s["sub"], 1)
                        if t == 0 and exists(n + 2, IMAGES):
                            norm(n + 2, slot)
                pipeline(pool, IMAGES, body)
                pool.wait_ge(s["late"], 16 * len(k.late))
                next_first_step(pool, k, s, IMAGES)

            @block.tensor
            def _(pe):
                def tokens_t(n, slot):
                    pe.wait_ge(s["y"], n + 1)
                    after(pe, s["hT"], n)
                    after(pe, s["oTe"], n - 2)
                    for t in range(2):
                        last = pe.transpose(bank[0][0:C, t * P:(t + 1) * P], k.Y[slot][:, t, :], k.ident[:])
                    last.then_inc(s["T"], 1)

                def queries_keys(n, slot):
                    pe.wait_ge(s["hT"], n + 1)
                    after(pe, s["q"], n)
                    after(pe, s["kx"], 2 * n)
                    h = h2[slot][:, :, 0, :]
                    pe.matmul(bank[1][0:C, 0:TOK], k.wqkv0[:, 0:C], h, start=True, stop=True)
                    pe.matmul(bank[1][0:C, TOK:2 * TOK], k.wqkv0[:, C:2 * C], h, start=True, stop=True).then_inc(s["qk"], 1)

                def values(n, slot):
                    after(pe, s["v"], n)
                    for w in range(4):
                        last = pe.matmul(bank[2][:, w * C:(w + 1) * C], h2[slot][:, w, :, :].rearrange("p i k -> p (i k)"), k.wqkv0[:, 2 * C:3 * C], start=True, stop=True)
                    last.then_inc(s["vp"], 1)

                def scores(n, t, slot):
                    if t == 0:
                        pe.wait_ge(s["kx"], 2 * n + 2)
                        pe.wait_ge(s["q"], n + 1)
                    after(pe, s["add"], 2 * n + t)
                    for half in range(2):
                        for w in range(2):
                            o = (2 * t + w) * WTOK
                            last = pe.matmul(bank[3 + half][w * WTOK:(w + 1) * WTOK, 0:384], qT[slot][:, o:o + WTOK],
                                             kx[slot][:, half * 6:half * 6 + 6, o:o + WTOK], start=True, stop=True)
                    last.then_inc(s["sc"], 1)

                def probs_t(n, t):
                    pe.wait_ge(s["exp"], 2 * n + t + 1)
                    after(pe, s["pte"], 2 * n + t)
                    for j in range(H0 // 2):
                        last = pe.transpose(bank[5 + j // 3][:, (j % 3) * P:(j % 3 + 1) * P],
                                            E[t][:, 2 * j:2 * j + 2, :].rearrange("p h k -> p (h k)"), k.ident[:])
                    last.then_inc(s["pt"], 1)

                def attend(n, t, slot):
                    pe.wait_ge(s["pte"], 2 * n + t + 1)
                    after(pe, s["a"], 2 * n + t)
                    pe.wait_ge(s["v"], n + 1)
                    if t == 0:
                        after(pe, s["x"], n)
                    for j in range(H0 // 2):
                        for w in range(2):
                            last = pe.matmul(bank[7][w * WTOK:(w + 1) * WTOK, j * 18:(j + 1) * 18],
                                             PT[:, j // 3, j % 3, w * WTOK:(w + 1) * WTOK], vb[slot][:, 2 * t + w, j, :],
                                             start=True, stop=True)
                    last.then_inc(s["av"], 1)

                def outputs_t(n, slot, tokens):
                    pe.wait_ge(s["a"], 2 * n + 2)
                    after(pe, s["hT"], tokens)
                    for t in range(2):
                        last = pe.transpose(bank[0][0:C, t * P:(t + 1) * P], A[slot][:, t, :], k.ident[:])
                    last.then_inc(s["oT"], 1)

                def project(n):
                    pe.wait_ge(s["oTe"], n + 1)
                    for t in range(2):
                        last = pe.matmul(bank[7][:, t * C:(t + 1) * C], AT[:, t * P:(t + 1) * P], k.wp0[:], start=True, stop=True)
                    last.then_inc(s["pj"], 1)

                tokens_t(0, 0)
                pe.wait_ge(s["pad"], 1)
                queries_keys(0, 0)
                values(0, 0)
                tokens_t(1, 1)
                scores(0, 0, 0)

                def body(n, slot, first, last):
                    if not last:
                        queries_keys(n + 1, 1 - slot)
                    if not first:
                        probs_t(n - 1, 1)
                    if not last:
                        values(n + 1, 1 - slot)
                    if not first:
                        attend(n - 1, 1, 1 - slot)
                    scores(n, 1, slot)
                    if not first:
                        outputs_t(n - 1, 1 - slot, n + 1 if last else n + 2)
                        project(n - 1)
                    probs_t(n, 0)
                    if exists(n + 2, IMAGES):
                        tokens_t(n + 2, slot)
                    if not last:
                        scores(n + 1, 0, 1 - slot)
                    attend(n, 0, slot)
                pipeline(pe, IMAGES, body)
                probs_t(IMAGES - 1, 1)
                attend(IMAGES - 1, 1, 1)
                outputs_t(IMAGES - 1, 1, IMAGES)
                project(IMAGES - 1)

            @block.scalar
            def _(act):
                act.wait_ge(s["bq"], 5)

                def pt_out(n, t):
                    act.wait_ge(s["pt"], 2 * n + t + 1)
                    after(act, s["av"], 2 * n + t)
                    for b in range(2):
                        last = act.activation(PT[:, b, :, :], bank[5 + b][:, 0:384].rearrange("p (j q) -> p j q", j=3), ACT.Copy)
                    last.then_inc(s["pte"], 1)

                def exps(n, t):
                    act.wait_ge(s["sub"], 2 * n + t + 1)
                    after(act, s["pt"], 2 * n + t - 1)
                    act.activation(E[t][:], S[t][:], ACT.Exp).then_inc(s["exp"], 1)

                def out_t(n):
                    act.wait_ge(s["oT"], n + 1)
                    after(act, s["pj"], n)
                    act.activation(AT[:], bank[0][0:C, 0:TOK], ACT.Copy).then_inc(s["oTe"], 1)

                def tokens(n, slot):
                    act.wait_ge(s["T"], n + 1)
                    after(act, s["vp"], n - 1)
                    act.activation(h2[slot][0:C], bank[0][0:C, 0:TOK].rearrange("p (v k) -> p v k", v=4)[:, :, None, :].broadcast_to([C, 4, 2, WTOK]),
                                   ACT.Identity, bias=k.b1[:], scale=k.g1[:]).then_inc(s["hT"], 1)

                def queries(n, slot):
                    act.wait_ge(s["kx"], 2 * n + 2)
                    after(act, s["sc"], 2 * n - 2)
                    act.activation(qT[slot][0:C], bank[1][0:C, 0:TOK], ACT.Identity, bias=bqs[:], scale=scale).then_inc(s["q"], 1)

                def values(n, slot):
                    act.wait_ge(s["vp"], n + 1)
                    after(act, s["av"], 2 * n - 2)
                    for half in range(2):
                        rows = slice(half * WTOK, (half + 1) * WTOK)
                        src = bank[2][rows, 0:4 * C].rearrange("p (v j i d) -> p v j i d", v=4, i=2, d=D0)
                        last = act.activation(vb[slot][rows, :, :, half * D0:(half + 1) * D0], src[:, :, :, half, :], ACT.Copy)
                    last.then_inc(s["v"], 1)

                tokens(0, 0)
                queries(0, 0)
                values(0, 0)
                tokens(1, 1)

                def body(n, slot, first, last):
                    if not first:
                        pt_out(n - 1, 1)
                    exps(n, 0)
                    if not first:
                        out_t(n - 1)
                    if not last:
                        queries(n + 1, 1 - slot)
                    pt_out(n, 0)
                    if not last:
                        values(n + 1, 1 - slot)
                    if exists(n + 2, IMAGES):
                        tokens(n + 2, slot)
                    exps(n, 1)
                pipeline(act, IMAGES, body)
                pt_out(IMAGES - 1, 1)
                out_t(IMAGES - 1)

            @block.vector
            def _(dve):
                def heads_out(n, t, slot):
                    dve.wait_ge(s["av"], 2 * n + t + 1)
                    after(dve, s["oT"], n - 1)
                    o = bank[7][:, 0:108].rearrange("p (j c) -> p j c", c=18)
                    dve.reciprocal(rec[:], o[:, :, 16:18, None]).then_inc(s["rec"], 1)
                    dve.wait_ge(s["rec"], 2 * n + t + 1)
                    dve.tensor_tensor(A[slot][:, t, :].rearrange("p (j i d) -> p j i d", j=H0 // 2, i=2),
                                      o[:, :, 0:16].rearrange("p j (i d) -> p j i d", i=2),
                                      rec[:].broadcast_to([P, H0 // 2, 2, D0]), ALU.mult).then_inc(s["a"], 1)

                def residual(n):
                    dve.wait_ge(s["pj"], n + 1)
                    dve.wait_ge(s["xb"], n + 1)
                    add_and_stats(dve, k, s, n, 2, bank[7][:, 0:2 * C].rearrange("p (t c) -> p t c", t=2))

                def keys_by_head(n, slot, part):
                    if part == 0:
                        dve.wait_ge(s["qk"], n + 1)
                        after(dve, s["sc"], 2 * n - 2)
                    hs = slice(part * 6, part * 6 + 6)
                    dve.scalar_tensor_tensor(out=kx[slot][0:C, hs, :], in0=bank[1][0:C, None, TOK:2 * TOK].broadcast_to([C, 6, TOK]),
                                             scalar=k.bk0[:], in1=k.headmask[:, hs, None].broadcast_to([C, 6, TOK]),
                                             op0=ALU.add, op1=ALU.mult).then_inc(s["kx"], 1)

                def biased_scores(n, t):
                    dve.wait_ge(s["sc"], 2 * n + t + 1)
                    after(dve, s["exp"], 2 * n + t - 1)
                    for half in range(2):
                        hs = slice(half * 6, half * 6 + 6)
                        last = dve.tensor_tensor(S[t][:, hs, :], bank[3 + half][:, 0:384].rearrange("p (h k) -> p h k", h=6),
                                                 k.bias0[:, :, hs].rearrange("p k h -> p h k"), ALU.add)
                    last.then_inc(s["add"], 1)
                    dve.wait_ge(s["add"], 2 * n + t + 1)
                    dve.tensor_reduce(mx[t][:, :, 0], S[t][:], AX.X, ALU.max).then_inc(s["mx"], 1)

                for t in h2 + qT + kx:
                    last = dve.memset(t[C:P], 0.0)
                last.then_inc(s["pad"], 1)
                for part in range(2):
                    keys_by_head(0, 0, part)

                def body(n, slot, first, last):
                    biased_scores(n, 0)
                    if not first:
                        heads_out(n - 1, 0, 1 - slot)
                    if not last:
                        keys_by_head(n + 1, 1 - slot, 0)
                        keys_by_head(n + 1, 1 - slot, 1)
                    if not first:
                        heads_out(n - 1, 1, 1 - slot)
                    biased_scores(n, 1)
                    if not first:
                        residual(n - 1)
                pipeline(dve, IMAGES, body)
                heads_out(IMAGES - 1, 0, 1)
                heads_out(IMAGES - 1, 1, 1)
                residual(IMAGES - 1)


def mlp(k, bank, prefix, w):
    nc = k.nc
    s = k.sems(prefix, LN_SEMS + "T hT up gelu down")
    steps = TILES // 4
    with ExitStack() as ctx:
        G = [k.sb(f"{prefix}_G{i}", [P, KH, 512], F32, ctx) for i in range(2)]
        with nc.Block() as block:
            @block.gpsimd
            def _(pool):
                k.clear_retired()
                def body(n, slot, first):
                    normalise(pool, k, s, n, 4, k.Y[slot][:, 0:4, :], w["b2"], n - 1)
                pairs(pool, steps, body)
                next_first_step(pool, k, s, steps)

            @block.tensor
            def _(pe):
                def down(n, slot):
                    pe.wait_ge(s["gelu"], KH * (n + 1))
                    after(pe, s["x"], n)
                    for t in range(4):
                        for j in range(KH):
                            last = pe.matmul(bank[7][:, t * C:(t + 1) * C], G[slot][:, j, t * P:(t + 1) * P], w["w2"][:, j, :],
                                             start=(j == 0), stop=(j == KH - 1))
                    last.then_inc(s["down"], 1)

                def body(n, slot, first):
                    pe.wait_ge(s["y"], n + 1)
                    after(pe, s["hT"], n)
                    for t in range(4):
                        last = pe.transpose(bank[6][0:C, t * P:(t + 1) * P], k.Y[slot][:, t, :], k.ident[:])
                    last.then_inc(s["T"], 1)
                    if not first:
                        down(n - 1, 1 - slot)
                    pe.wait_ge(s["hT"], n + 1)
                    after(pe, s["gelu"], KH * (n - 1))
                    for j in range(KH):
                        pe.matmul(bank[3 * slot + j][:], w["w1"][:, j * P:(j + 1) * P], k.hT[slot][:], start=True, stop=True).then_inc(s["up"], 1)
                pairs(pe, steps, body)
                down(steps - 1, 1)

            @block.scalar
            def _(act):
                def body(n, slot, first):
                    after(act, s["down"], n - 1)
                    for j in range(KH):
                        act.wait_ge(s["up"], KH * n + j + 1)
                        act.activation(G[slot][:, j, :], bank[3 * slot + j][:], ACT.Gelu, bias=w["b1"][:, j:j + 1]).then_inc(s["gelu"], 1)
                pairs(act, steps, body)

            @block.vector
            def _(dve):
                def residual(n):
                    dve.wait_ge(s["down"], n + 1)
                    dve.wait_ge(s["xb"], n + 1)
                    add_and_stats(dve, k, s, n, 4, bank[7][:, 0:4 * C].rearrange("p (t c) -> p t c", t=4))

                def body(n, slot, first):
                    dve.wait_ge(s["T"], n + 1)
                    after(dve, s["up"], KH * (n - 1))
                    dve.tensor_scalar(k.hT[slot][:], bank[6][0:C, :], w["g"][:], w["b"][:], ALU.mult, ALU.add).then_inc(s["hT"], 1)
                    if not first:
                        residual(n - 1)
                pairs(dve, steps, body)
                residual(steps - 1)


def raster(t, y):
    return t.rearrange("p (y i v c) -> p y v i c", y=2, i=WS, v=2)[:, y]


def conv_mixer(k, bank):
    nc = k.nc
    s = k.sems("cm", LN_SEMS + "z T hT in p taps acc1 conv ct loc mix bn2 ag2 va2 rs2 z2 zT zTe out diag init")
    with ExitStack() as ctx:
        def sb(name, shape, dt=F32):
            return k.sb("cm_" + name, shape, dt, ctx)

        grid = [sb(f"g{i}", [P, 2, GRID, GRID]) for i in range(2)]
        acc = [sb(f"acc{i}", [C, TOK]) for i in range(2)]
        acc1 = sb("accb", [C, TOK])
        diag = sb("diag", [P, 9, C])
        loc = sb("loc", [P, 2, CI])
        st2, ag2 = sb("st2", [P, 2, 6]), sb("ag2", [P, 2, 2])
        v2, r2 = sb("v2", [P, 2, 1]), sb("r2", [P, 2, 1])
        Z = sb("z", [P, 2, CI])
        ZT = sb("zT", [C, 2, 2, P])

        with nc.Block() as block:
            @block.gpsimd
            def _(pool):
                k.clear_retired()
                pool.memset(diag[:], 0.0)
                for i in range(2):
                    last = pool.memset(grid[i][:], 0.0)
                last.then_inc(s["init"], 1)
                pool.wait_ge(s["init"], 1)
                for tap in range(9):
                    last = pool.tensor_scalar(diag[0:C, tap, :], k.ident[0:C, 0:C], k.kconv[:, 1, tap:tap + 1], 0.0, ALU.mult, ALU.add)
                last.then_inc(s["diag"], 1)

                def rstd2(n):
                    pool.wait_ge(s["ag2"], n + 1)
                    after(pool, s["z2"], n)
                    pool.tensor_tensor(v2[:], ag2[:, :, 1:2], k.eps[:, 0:2, :], ALU.add).then_inc(s["va2"], 1)
                    pool.wait_ge(s["va2"], n + 1)
                    pool.tensor_tensor(r2[:], v2[:], k.minus_half[:, 0:2, :], ALU.pow).then_inc(s["rs2"], 1)

                def norm(n, slot):
                    normalise(pool, k, s, n, 2, k.Y[slot][:, 0:2, :], k.bout, n - 1)
                norm(0, 0)

                def body(n, slot, first, last):
                    if not last:
                        norm(n + 1, 1 - slot)
                    if not first:
                        rstd2(n - 1)
                pipeline(pool, IMAGES, body)
                next_first_step(pool, k, s, IMAGES)
                rstd2(IMAGES - 1)

            @block.tensor
            def _(pe):
                def mix(n):
                    pe.wait_ge(s["loc"], n + 1)
                    after(pe, s["z2"], n)
                    for t in range(2):
                        for j in range(2):
                            last = pe.matmul(bank[4][:, t * CI:(t + 1) * CI], k.mixer[:, j, t * P:(t + 1) * P], loc[:, j, :],
                                             start=(j == 0), stop=(j == 1))
                    last.then_inc(s["mix"], 1)

                def back(n):
                    pe.wait_ge(s["z2"], n + 1)
                    after(pe, s["zTe"], n)
                    for j in range(2):
                        for t in range(2):
                            last = pe.transpose(bank[5][0:C, (2 * j + t) * P:(2 * j + t + 1) * P], Z[:, t, j * C:(j + 1) * C], k.ident[:])
                    last.then_inc(s["zT"], 1)

                def out(n):
                    pe.wait_ge(s["zTe"], n + 1)
                    after(pe, s["x"], n)
                    pe.wait_ge(s["xb"], n + 1)
                    for t in range(2):
                        o = bank[6][:, t * C:(t + 1) * C]
                        pe.matmul(o, k.perm[:], k.X[:, bass.ds(n * 2 + t, 1), :], start=True, stop=False)
                        for j in range(2):
                            last = pe.matmul(o, ZT[:, j, t, :], k.wout[:, j, :], start=False, stop=(j == 1))
                    last.then_inc(s["out"], 1)

                def tokens(n, slot):
                    pe.wait_ge(s["y"], n + 1)
                    after(pe, s["hT"], n)
                    for t in range(2):
                        last = pe.transpose(bank[0][0:C, t * P:(t + 1) * P], k.Y[slot][:, t, :], k.ident[:])
                    last.then_inc(s["T"], 1)

                def widen(n, slot):
                    pe.wait_ge(s["hT"], n + 1)
                    after(pe, s["p"], n)
                    for j in range(2):
                        last = pe.matmul(bank[1][0:C, j * TOK:(j + 1) * TOK], k.win[:, j * C:(j + 1) * C], k.hT[slot][:, 0:TOK], start=True, stop=True)
                    last.then_inc(s["in"], 1)

                def taps(n, slot, first):
                    pe.wait_ge(s["p"], n + 1)
                    after(pe, s["acc1"], n)
                    for tap in range(9):
                        if tap == 2 and not first:
                            mix(n - 1)
                        y, x = divmod(tap, 3)
                        last = pe.matmul(bank[3][0:C, 0:TOK], diag[:, tap, :], grid[slot][:, 1, y:y + SIDE, x:x + SIDE],
                                         start=(tap == 0), stop=(tap == 8))
                    last.then_inc(s["taps"], 1)

                def conv_t(n, slot):
                    pe.wait_ge(s["conv"], 9 * (n + 1))
                    pe.wait_ge(s["acc1"], n + 1)
                    after(pe, s["loc"], n)
                    for half, src in ((0, acc[slot]), (1, acc1)):
                        for j in range(2):
                            last = pe.transpose(bank[2][:, (2 * j + half) * C:(2 * j + half + 1) * C], src[:, j * P:(j + 1) * P], k.ident[0:C, 0:C])
                    last.then_inc(s["ct"], 1)

                tokens(0, 0)
                widen(0, 0)
                pe.wait_ge(s["diag"], 1)

                def body(n, slot, first, last):
                    if not last:
                        tokens(n + 1, 1 - slot)
                    taps(n, slot, first)
                    if not first:
                        back(n - 1)
                    if not last:
                        widen(n + 1, 1 - slot)
                    if not first:
                        out(n - 1)
                    conv_t(n, slot)
                pipeline(pe, IMAGES, body)
                mix(IMAGES - 1)
                back(IMAGES - 1)
                out(IMAGES - 1)

            @block.scalar
            def _(act):
                act.wait_ge(s["init"], 1)

                def zt(n):
                    act.wait_ge(s["zT"], n + 1)
                    after(act, s["out"], n)
                    for j in range(2):
                        last = act.activation(ZT[:, j, :, :], bank[5][0:C, j * 2 * P:(j + 1) * 2 * P].rearrange("p (t q) -> p t q", t=2),
                                              ACT.Identity, bias=k.onb[:, j:j + 1], scale=k.ong[:, j:j + 1])
                    last.then_inc(s["zTe"], 1)

                def tokens(n, slot):
                    act.wait_ge(s["T"], n + 1)
                    after(act, s["in"], n - 1)
                    for y in range(2):
                        last = act.activation(raster(k.hT[slot][:, 0:TOK], y), bank[0][0:C, y * P:(y + 1) * P].rearrange("p (v i c) -> p v i c", v=2, i=WS),
                                              ACT.Identity, bias=k.b3[:], scale=k.g3[:])
                    last.then_inc(s["hT"], 1)

                def widened(n, slot):
                    act.wait_ge(s["in"], n + 1)
                    after(act, s["taps"], n - 1)
                    after(act, s["conv"], 9 * (n - 1))
                    for j in range(2):
                        last = act.activation(grid[slot][0:C, j, 1:1 + SIDE, 1:1 + SIDE],
                                              bank[1][0:C, j * TOK:(j + 1) * TOK].rearrange("p (i c) -> p i c", c=SIDE),
                                              ACT.Identity, bias=k.bin[:, j:j + 1])
                    last.then_inc(s["p"], 1)

                tokens(0, 0)
                widened(0, 0)

                def body(n, slot, first, last):
                    if not last:
                        tokens(n + 1, 1 - slot)
                    act.wait_ge(s["taps"], n + 1)
                    after(act, s["ct"], n)
                    act.activation(acc1[:], bank[3][0:C, 0:TOK], ACT.Copy).then_inc(s["acc1"], 1)
                    if not first:
                        zt(n - 1)
                    if not last:
                        widened(n + 1, 1 - slot)
                    act.wait_ge(s["ct"], n + 1)
                    after(act, s["mix"], n)
                    act.activation(loc[:], bank[2][:, 0:2 * CI].rearrange("p (t c) -> p t c", t=2), ACT.Copy).then_inc(s["loc"], 1)
                pipeline(act, IMAGES, body)
                zt(IMAGES - 1)

            @block.vector
            def _(dve):
                def norm2(n):
                    dve.wait_ge(s["mix"], n + 1)
                    after(dve, s["va2"], n)
                    for t in range(2):
                        last = dve.bn_stats(st2[:, t, :], bank[4][:, t * CI:(t + 1) * CI])
                    last.then_inc(s["bn2"], 1)
                    alone(dve, k)
                    dve.wait_ge(s["bn2"], n + 1)
                    for t in range(2):
                        last = dve.bn_aggr(ag2[:, t, :], st2[:, t, :])
                    last.then_inc(s["ag2"], 1)

                def norm2b(n):
                    dve.wait_ge(s["rs2"], n + 1)
                    after(dve, s["zT"], n)
                    for t in range(2):
                        last = dve.tensor_scalar(Z[:, t, :], bank[4][:, t * CI:(t + 1) * CI], ag2[:, t, 0:1], r2[:, t, :], ALU.subtract, ALU.mult)
                    last.then_inc(s["z2"], 1)

                def residual(n):
                    dve.wait_ge(s["out"], n + 1)
                    dve.wait_ge(s["xb"], n + 1)
                    add_and_stats(dve, k, s, n, 2, bank[6][:, 0:2 * C].rearrange("p (t c) -> p t c", t=2), replace=True)

                def body(n, slot, first, last):
                    dve.wait_ge(s["p"], n + 1)
                    after(dve, s["ct"], n - 1)
                    o = acc[slot][:].rearrange("p (i c) -> p i c", c=SIDE)
                    for tap in range(9):
                        if tap == 1 and exists(n - 2, IMAGES):
                            residual(n - 2)
                        if tap == 2 and not first:
                            norm2(n - 1)
                        if tap == 5 and not first:
                            norm2b(n - 1)
                        y, x = divmod(tap, 3)
                        src = grid[slot][0:C, 0, y:y + SIDE, x:x + SIDE]
                        kk = k.kconv[:, 0, tap:tap + 1]
                        if tap == 0:
                            dve.tensor_scalar(o, src, kk, None, ALU.mult).then_inc(s["conv"], 1)
                        else:
                            after(dve, s["conv"], 9 * n + tap)
                            dve.scalar_tensor_tensor(out=o, in0=src, scalar=kk, in1=o, op0=ALU.mult, op1=ALU.add).then_inc(s["conv"], 1)
                pipeline(dve, IMAGES, body)
                residual(IMAGES - 2)
                norm2(IMAGES - 1)
                norm2b(IMAGES - 1)
                residual(IMAGES - 1)


def centre_weights(pool, k, s):
    pool.wait_ge(s["sum"], 2)
    pool.partition_all_reduce(k.mean[:].rearrange("p i g -> p (i g)"), k.part[:].rearrange("p i g -> p (i g)"), P,
                              bass.bass_isa.ReduceOp.add).then_inc(s["total"], 1)
    pool.wait_ge(s["total"], 1)
    for i, (n, w, cols) in enumerate(((k.g76, k.f1, C), (k.g19, k.f2, HID))):
        pool.tensor_scalar(k.mean[:, i, :], k.mean[:, i, :], 1.0 / (n * cols), 0.0, ALU.mult, ALU.add).then_inc(s["mean"], 1)
    pool.wait_ge(s["mean"], 2)
    for i, (n, w, cols) in enumerate(((k.g76, k.f1, C), (k.g19, k.f2, HID))):
        pool.tensor_tensor(w[:], w[:], k.mean[0:n, i, :, None].broadcast_to([n, GROUPS, cols]), ALU.subtract).then_inc(s["centre"], 1)
        pool.wait_ge(s["centre"], i + 1)


def full_attention(k, bank):
    nc = k.nc
    s = k.sems("fa", LN_SEMS + "sum total mean centre less sign init T hT pj e1 e2 sc nm exp rec nrm pt pte av ote out")
    with ExitStack() as ctx:
        def sb(name, shape, dt=F32):
            return k.sb("fa_" + name, shape, dt, ctx)

        qT = [sb(f"q{i}", [P, PAIRS2, TOK]) for i in range(2)]
        kz = [sb(f"kz{i}", [P, H2, TOK]) for i in range(2)]
        V = [sb(f"v{i}", [P, 2, H2, 64]) for i in range(2)]
        nm = [sb(f"nm{i}", [P, 2]) for i in range(2)]
        sm = [sb(f"sm{i}", [P, 2]) for i in range(2)]
        rc = [sb(f"rc{i}", [P, 2]) for i in range(2)]
        E = [sb(f"e{i}", [P, 2, TOK]) for i in range(2)]
        PT = [sb(f"pt{i}", [P, 2, TOK]) for i in range(4)]
        OT = [sb(f"ot{i}", [P, PAIRS2, TOK]) for i in range(2)]
        scale = float(D2) ** -0.5
        U = H2

        with nc.Block() as block:
            @block.gpsimd
            def _(pool):
                k.clear_retired()
                for t in kz + V:
                    last = pool.memset(t[:], 0.0)
                last.then_inc(s["init"], 1)

                def body(n, slot, first):
                    normalise(pool, k, s, n, 2, k.Y[slot][:, 0:2, :], k.bp2, n - 1)
                pairs(pool, IMAGES, body)
                centre_weights(pool, k, s)
                next_first_step(pool, k, s, IMAGES)

            @block.tensor
            def _(pe):
                def score(n, h, slot):
                    u = U * n + h
                    after(pe, s["exp"], u - 1)
                    for c in range(2):
                        last = pe.matmul(bank[3 + h % 2][:, c * TOK:(c + 1) * TOK], qT[slot][:, h // 2, c * P:(c + 1) * P],
                                         kz[slot][:, h, :], start=True, stop=True)
                    last.then_inc(s["sc"], 1)

                def probs(n, h):
                    u = U * n + h
                    pe.wait_ge(s["nrm"], u + 1)
                    after(pe, s["pte"], u - 1)
                    for kc in range(2):
                        for c in range(2):
                            last = pe.transpose(bank[5 + h % 2][:, kc * TOK + c * P:kc * TOK + (c + 1) * P],
                                                E[h % 2][:, c, kc * P:(kc + 1) * P], k.ident[:])
                    last.then_inc(s["pt"], 1)

                def values(n, p, slot):
                    pe.wait_ge(s["pte"], U * n + 2 * p + 2)
                    after(pe, s["ote"], PAIRS2 * n + p)
                    for kc in range(2):
                        for h in (2 * p, 2 * p + 1):
                            last = pe.matmul(bank[7][64 * (h % 2):64 * (h % 2) + 64, 0:TOK], V[slot][:, kc, h, :], PT[h % 4][:, kc, :],
                                             start=(kc == 0), stop=(kc == 1), skip_group_check=True)
                    last.then_inc(s["av"], 1)

                def out(n, slot):
                    pe.wait_ge(s["ote"], PAIRS2 * (n + 1))
                    for t in range(2):
                        for p in range(PAIRS2):
                            last = pe.matmul(bank[0][:, t * C:(t + 1) * C], OT[slot][:, p, t * P:(t + 1) * P], k.wp2[:, p, :],
                                             start=(p == 0), stop=(p == PAIRS2 - 1))
                    last.then_inc(s["out"], 1)

                def tokens(m, slot):
                    pe.wait_ge(s["y"], m + 1)
                    after(pe, s["x"], m - 2)
                    for t in range(2):
                        last = pe.transpose(bank[0][0:C, t * P:(t + 1) * P], k.Y[slot][:, t, :], k.ident[:])
                    last.then_inc(s["T"], 1)

                def project(m, j, slot):
                    if j == 0:
                        pe.wait_ge(s["hT"], m + 1)
                    b = bank[1 + j % 2]
                    after(pe, s["e1"] if j % 2 == 0 else s["e2"], 3 * m + j // 2)
                    if j < 4:
                        for i in range(2):
                            w = (k.wq2 if j < 2 else k.wk2)[:, 2 * (j % 2) + i, :, :].rearrange("c h d -> c (h d)")
                            last = pe.matmul(b[:, i * TOK:(i + 1) * TOK], w, k.hT[slot][:, 0:TOK], start=True, stop=True)
                    else:
                        last = pe.matmul(b[:, 0:H2 * D2], k.hT[slot][:, (j - 4) * P:(j - 3) * P], k.wv2[:], start=True, stop=True)
                    last.then_inc(s["pj"], 1)

                def step(n, h, slot, start, end):
                    if not end or h < U:
                        if h == 0:
                            pe.wait_ge(s["e1"], 3 * n + 2)
                            pe.wait_ge(s["e2"], 3 * n + 2)
                        if h < U:
                            score(n, h, slot)
                    if h >= 2 and h < U + 2:
                        probs(n, h - 2)
                    elif h < 2 and not start:
                        probs(n - 1, U + h - 2)
                    if h == 4:
                        pe.wait_ge(s["e1"], 3 * n + 3)
                        pe.wait_ge(s["e2"], 3 * n + 3)
                    if h % 2 == 0:
                        if h >= 4:
                            values(n, h // 2 - 2, slot)
                        elif not start:
                            values(n - 1, PAIRS2 + h // 2 - 2, 1 - slot)
                    if h == 3 and not start:
                        out(n - 1, 1 - slot)
                    if not end:
                        if h == 0:
                            tokens(n + 1, 1 - slot)
                        elif h < 7:
                            project(n + 1, h - 1, 1 - slot)

                tokens(0, 0)
                for j in range(6):
                    project(0, j, 0)

                def body(n, slot, first, last):
                    for h in range(U):
                        step(n, h, slot, first, last)
                pipeline(pe, IMAGES, body)
                for h in range(U, U + 3):
                    step(IMAGES - 1, h, 1, False, True)
                out(IMAGES - 1, 1)

            @block.scalar
            def _(act):
                def exps(n, h):
                    u = U * n + h
                    act.wait_ge(s["nm"], u + 1)
                    after(act, s["pt"], u - 1)
                    after(act, s["rec"], u - 1)
                    for c in range(2):
                        last = act.activation(E[h % 2][:, c, :], bank[3 + h % 2][:, c * TOK:(c + 1) * TOK], ACT.Exp,
                                              bias=nm[h % 2][:, c:c + 1], accum_out=sm[h % 2][:, c:c + 1])
                    last.then_inc(s["exp"], 1)

                def pt_out(n, h):
                    act.wait_ge(s["pt"], U * n + h + 1)
                    after(act, s["av"], PAIRS2 * n + h // 2 - 1)
                    act.activation(PT[h % 4][:], bank[5 + h % 2][:].rearrange("p (a b) -> p a b", a=2), ACT.Copy).then_inc(s["pte"], 1)

                def tokens(m, slot):
                    act.wait_ge(s["T"], m + 1)
                    after(act, s["pj"], 6 * (m - 1))
                    act.activation(k.hT[slot][:, 0:TOK], bank[0][0:C, 0:TOK], ACT.Copy).then_inc(s["hT"], 1)

                def project(m, j, slot):
                    act.wait_ge(s["pj"], 6 * m + 2 * j + 1)
                    if j == 0:
                        after(act, s["sc"], U * (m - 1))
                        act.activation(qT[slot][:, 0:2, :], bank[1][:].rearrange("p (a b) -> p a b", a=2), ACT.Copy, scale=scale).then_inc(s["e1"], 1)
                    elif j == 1:
                        for i in range(2):
                            last = act.activation(kz[slot][64 * i:64 * i + 64, i:4:2, :],
                                                  bank[1][64 * i:64 * i + 64, :].rearrange("p (a b) -> p a b", a=2), ACT.Copy)
                        last.then_inc(s["e1"], 1)
                    else:
                        after(act, s["av"], PAIRS2 * (m - 1))
                        act.activation(V[slot][:, 0, :, 0:D2], bank[1][:, 0:H2 * D2].rearrange("p (h d) -> p h d", d=D2), ACT.Copy).then_inc(s["e1"], 1)

                act.wait_ge(s["init"], 1)
                tokens(0, 0)
                for j in range(3):
                    project(0, j, 0)

                def body(n, slot, first, last):
                    for h in range(U):
                        if h >= 2:
                            pt_out(n, h - 2)
                        elif not first:
                            pt_out(n - 1, U + h - 2)
                        exps(n, h)
                        if not last:
                            if h == 0:
                                tokens(n + 1, 1 - slot)
                            elif h % 2 == 0:
                                project(n + 1, h // 2 - 1, 1 - slot)
                pipeline(act, IMAGES, body)
                pt_out(IMAGES - 1, 6)
                pt_out(IMAGES - 1, 7)

            @block.vector
            def _(dve):
                def maxima(n, h):
                    u = U * n + h
                    dve.wait_ge(s["sc"], u + 1)
                    after(dve, s["exp"], u - 1)
                    dve.tensor_reduce(nm[h % 2][:], bank[3 + h % 2][:].rearrange("p (a b) -> p a b", a=2), AX.X, ALU.max, negate=True).then_inc(s["nm"], 1)

                def norm(n, h):
                    u = U * n + h
                    dve.wait_ge(s["exp"], u + 1)
                    after(dve, s["nrm"], u - 1)
                    dve.reciprocal(rc[h % 2][:], sm[h % 2][:]).then_inc(s["rec"], 1)
                    dve.wait_ge(s["rec"], u + 1)
                    for c in range(2):
                        last = dve.tensor_scalar(E[h % 2][:, c, :], E[h % 2][:, c, :], rc[h % 2][:, c:c + 1], None, ALU.mult)
                    last.then_inc(s["nrm"], 1)

                def pair_out(n, p, slot):
                    dve.wait_ge(s["av"], PAIRS2 * n + p + 1)
                    after(dve, s["out"], n - 1)
                    dve.tensor_copy(OT[slot][:, p, :], bank[7][:, 0:TOK]).then_inc(s["ote"], 1)

                def residual(n):
                    dve.wait_ge(s["out"], n + 1)
                    dve.wait_ge(s["xb"], n + 1)
                    add_and_stats(dve, k, s, n, 2, bank[0][:, 0:2 * C].rearrange("p (t c) -> p t c", t=2))

                def project(m, j, slot):
                    dve.wait_ge(s["pj"], 6 * m + 2 * j + 2)
                    if j == 0:
                        after(dve, s["sc"], U * (m - 1))
                        dve.tensor_scalar(qT[slot][:, 2:4, :], bank[2][:].rearrange("p (a b) -> p a b", a=2), scale, None, ALU.mult).then_inc(s["e2"], 1)
                    elif j == 1:
                        for i in range(2):
                            last = dve.tensor_copy(kz[slot][64 * i:64 * i + 64, 4 + i:8:2, :],
                                                   bank[2][64 * i:64 * i + 64, :].rearrange("p (a b) -> p a b", a=2))
                        last.then_inc(s["e2"], 1)
                    else:
                        after(dve, s["av"], PAIRS2 * (m - 1))
                        dve.tensor_copy(V[slot][:, 1, :, 0:D2], bank[2][:, 0:H2 * D2].rearrange("p (h d) -> p h d", d=D2)).then_inc(s["e2"], 1)

                def signs(g):
                    dve.wait_ge(s["centre"], 2)
                    for w, less in ((k.f1, k.less1), (k.f2, k.less2)):
                        dve.tensor_scalar(less[:, g, :], w[:, g, :], 0.0, None, ALU.is_lt).then_inc(s["less"], 1)
                    dve.wait_ge(s["less"], 2 * g + 2)
                    for w, less in ((k.f1, k.less1), (k.f2, k.less2)):
                        dve.scalar_tensor_tensor(out=w[:, g, :], in0=w[:, g, :], scalar=0.0, in1=less[:, g, :],
                                                 op0=ALU.is_gt, op1=ALU.subtract).then_inc(s["sign"], 1)

                dve.wait_ge(s["init"], 1)
                for j in range(3):
                    project(0, j, 0)

                def body(n, slot, first, last):
                    for h in range(U):
                        maxima(n, h)
                        if first and h in (1, 2):
                            rows, w = ((k.g76, k.f1), (k.g19, k.f2))[h - 1]
                            dve.tensor_reduce(k.part[0:rows, h - 1, :], w[:], AX.X, ALU.add).then_inc(s["sum"], 1)
                        if last and 1 <= h <= GROUPS:
                            signs(h - 1)
                        if h >= 1:
                            norm(n, h - 1)
                        elif not first:
                            norm(n - 1, U - 1)
                        if h % 2 == 0:
                            if h >= 4:
                                pair_out(n, h // 2 - 2, slot)
                            elif not first:
                                pair_out(n - 1, PAIRS2 + h // 2 - 2, 1 - slot)
                        if h == 4 and not first:
                            residual(n - 1)
                        if not last and h % 2 == 1 and h >= 3:
                            project(n + 1, (h - 3) // 2, 1 - slot)
                pipeline(dve, IMAGES, body)
                norm(IMAGES - 1, U - 1)
                pair_out(IMAGES - 1, 2, 1)
                pair_out(IMAGES - 1, 3, 1)
                residual(IMAGES - 1)


def binary_ffn(k, bank):
    nc = k.nc
    s = k.sems("bf", LN_SEMS + "tw twe T hT up h am ar1 c1 clip gelu down z am2 ar2 c2 zc q2 top0 inv0 top1 inv1")
    with ExitStack() as ctx:
        def sb(name, shape, dt=F32):
            return k.sb("bf_" + name, shape, dt, ctx)

        w1T = sb("w1T", [C, HID])
        w2T = sb("w2T", [P, KH, C])
        hT = sb("hT", [C, GT * P])
        H = [sb(f"H{i}", [P, KH, GT * P]) for i in range(2)]
        Z = sb("Z", [P, GT, C])
        am, ar, cc = sb("am", [P, 2]), sb("ar", [P, 2]), sb("cc", [P, 2, 4])
        half = GT * P // 2
        MAX = bass.bass_isa.ReduceOp.max

        def scales(dve, i, g, src, done):
            dve.wait_ge(s[src], g + 1)
            dve.tensor_scalar(cc[:, i, 3:4], ar[:, i:i + 1], EPS_Q, None, ALU.add).then_inc(s[f"top{i}"], 1)
            dve.wait_ge(s[f"top{i}"], g + 1)
            dve.reciprocal(cc[:, i, 0:1], cc[:, i, 3:4]).then_inc(s[f"inv{i}"], 1)
            dve.tensor_scalar(cc[:, i, 1:2], cc[:, i, 3:4], (QB - EPS_Q) / QB, None, ALU.mult)
            dve.tensor_scalar(cc[:, i, 2:3], cc[:, i, 3:4], -(QB - EPS_Q) / QB, None, ALU.mult)
            dve.wait_ge(s[f"inv{i}"], g + 1)
            dve.tensor_scalar(cc[:, i, 0:1], cc[:, i, 0:1], QB, None, ALU.mult).then_inc(s[done], 1)

        def groups(body):
            for g in range(GROUPS):
                body(g, g % 2, g == 0, g == LAST)

        LAST, LAST_SLOT = GROUPS - 1, (GROUPS - 1) % 2
        with nc.Block() as block:
            @block.gpsimd
            def _(pool):
                k.clear_retired()
                pool.memset(w1T[:], 0.0)
                pool.memset(w2T[:], 0.0).then_inc(s["twe"], 1)

                def output_max(g):
                    alone(pool, k)
                    pool.wait_ge(s["am2"], g + 1)
                    after(pool, s["c2"], g)
                    pool.partition_all_reduce(ar[:, 1:2], am[:, 1:2], P, MAX).then_inc(s["ar2"], 1)

                normalise(pool, k, s, 0, GT, k.Y[0][:], None, 0)

                def body(g, slot, first, last):
                    if not last:
                        normalise(pool, k, s, g + 1, GT, k.Y[1 - slot][:], None, g)
                    alone(pool, k)
                    pool.wait_ge(s["am"], g + 1)
                    after(pool, s["c1"], g)
                    pool.partition_all_reduce(ar[:, 0:1], am[:, 0:1], P, MAX).then_inc(s["ar1"], 1)
                    if not first:
                        output_max(g - 1)
                groups(body)
                output_max(LAST)
                next_first_step(pool, k, s, GROUPS)

            @block.tensor
            def _(pe):
                for g in range(GROUPS):
                    last = pe.transpose(bank[1][0:C, g * k.g76:(g + 1) * k.g76], k.f1[:, g, :], k.ident[0:k.g76, 0:k.g76])
                    for j in range(KH):
                        last = pe.transpose(bank[2][:, j * P + g * k.g19:j * P + (g + 1) * k.g19], k.f2[:, g, j * P:(j + 1) * P], k.ident[0:k.g19, 0:k.g19])
                last.then_inc(s["tw"], 1)
                pe.wait_ge(s["twe"], 3)

                def down(g, slot):
                    pe.wait_ge(s["gelu"], KH * (g + 1))
                    after(pe, s["z"], 2 * g)
                    for t in range(GT):
                        for j in range(KH):
                            last = pe.matmul(bank[6 + t // 3][:, (t % 3) * C:(t % 3 + 1) * C], H[slot][:, j, t * P:(t + 1) * P], w2T[:, j, :],
                                             start=(j == 0), stop=(j == KH - 1))
                    last.then_inc(s["down"], 1)

                def tokens(g, slot):
                    pe.wait_ge(s["y"], g + 1)
                    after(pe, s["hT"], g)
                    for t in range(GT):
                        last = pe.transpose(bank[t // 3][0:C, (t % 3) * P:(t % 3 + 1) * P], k.Y[slot][:, t, :], k.ident[:])
                    last.then_inc(s["T"], 1)

                tokens(0, 0)

                def body(g, slot, first, last):
                    pe.wait_ge(s["hT"], g + 1)
                    for j in range(KH):
                        for i in range(2):
                            u = 2 * j + i
                            after(pe, s["h"], 6 * g + u - 3)
                            pe.matmul(bank[2 + u % 4][:, 0:half], w1T[:, j * P:(j + 1) * P], hT[:, i * half:(i + 1) * half], start=True, stop=True).then_inc(s["up"], 1)
                    if not last:
                        tokens(g + 1, 1 - slot)
                    if not first:
                        down(g - 1, 1 - slot)
                groups(body)
                down(LAST, LAST_SLOT)

            @block.scalar
            def _(act):
                def tokens(g):
                    act.wait_ge(s["T"], g + 1)
                    after(act, s["up"], 6 * g)
                    for i in range(2):
                        last = act.activation(hT[:, i * half:(i + 1) * half], bank[i][0:C, 0:half], ACT.Copy)
                    last.then_inc(s["hT"], 1)

                tokens(0)

                def body(g, slot, first, last):
                    after(act, s["down"], g - 1)
                    for j in range(KH):
                        for i in range(2):
                            u = 2 * j + i
                            act.wait_ge(s["up"], 6 * g + u + 1)
                            act.activation(H[slot][:, j, i * half:(i + 1) * half], bank[2 + u % 4][:, 0:half], ACT.Identity, bias=k.fb1[:, j:j + 1]).then_inc(s["h"], 1)
                    if not last:
                        tokens(g + 1)
                    for j in range(KH):
                        act.wait_ge(s["clip"], KH * g + j + 1)
                        act.activation(H[slot][:, j, :], H[slot][:, j, :], ACT.Gelu, scale=cc[:, 0, 0:1]).then_inc(s["gelu"], 1)
                groups(body)

            @block.vector
            def _(dve):
                dve.wait_ge(s["tw"], 1)
                dve.wait_ge(s["twe"], 1)
                dve.tensor_copy(w1T[:, 0:GROUPS * k.g76], bank[1][0:C, 0:GROUPS * k.g76]).then_inc(s["twe"], 1)
                dve.tensor_copy(w2T[:, :, 0:GROUPS * k.g19], bank[2][:, 0:KH * P].rearrange("p (j c) -> p j c", j=KH)[:, :, 0:GROUPS * k.g19]).then_inc(s["twe"], 1)

                def output(g):
                    dve.wait_ge(s["down"], g + 1)
                    after(dve, s["mv"], g)
                    for b in range(2):
                        dve.tensor_tensor(Z[:, 3 * b:3 * b + 3, :], bank[6 + b][:, 0:3 * C].rearrange("p (t c) -> p t c", t=3),
                                          k.fb2[:, None, :].broadcast_to([P, 3, C]), ALU.add).then_inc(s["z"], 1)
                    dve.wait_ge(s["z"], 2 * (g + 1))
                    after(dve, s["ar2"], g)
                    dve.tensor_reduce(am[:, 1:2], Z[:], AX.XY, ALU.max, apply_absolute_value=True).then_inc(s["am2"], 1)

                def quantised_output(g):
                    scales(dve, 1, g, "ar2", "c2")
                    dve.wait_ge(s["c2"], g + 1)
                    dve.tensor_scalar(Z[:], Z[:], cc[:, 1, 1:2], cc[:, 1, 2:3], ALU.min, ALU.max).then_inc(s["zc"], 1)
                    dve.wait_ge(s["zc"], g + 1)
                    dve.tensor_scalar(Z[:], Z[:], cc[:, 1, 0:1], None, ALU.mult).then_inc(s["q2"], 1)
                    dve.wait_ge(s["q2"], g + 1)
                    dve.wait_ge(s["y"], g + 1)
                    add_and_stats(dve, k, s, g, GT, Z[:])

                def body(g, slot, first, last):
                    dve.wait_ge(s["h"], 6 * (g + 1))
                    after(dve, s["ar1"], g)
                    dve.tensor_reduce(am[:, 0:1], H[slot][:], AX.XY, ALU.max, apply_absolute_value=True).then_inc(s["am"], 1)
                    if not first:
                        output(g - 1)
                    after(dve, s["gelu"], KH * g)
                    scales(dve, 0, g, "ar1", "c1")
                    dve.wait_ge(s["c1"], g + 1)
                    for j in range(KH):
                        dve.tensor_scalar(H[slot][:, j, :], H[slot][:, j, :], cc[:, 0, 1:2], cc[:, 0, 2:3], ALU.min, ALU.max).then_inc(s["clip"], 1)
                    if not first:
                        quantised_output(g - 1)
                groups(body)
                output(LAST)
                quantised_output(LAST)


def causal_attention(k, bank):
    nc = k.nc
    s = k.sems("ca", LN_SEMS + "pad T hT pj e qs qx kv vt v sc nm exp rec nrm pt pte av ote out red own")
    with ExitStack() as ctx:
        def sb(name, shape, dt=F32):
            return k.sb("ca_" + name, shape, dt, ctx)

        qx = [sb(f"qx{i}", [P, TOK, H3]) for i in range(2)]
        qs = sb("qs", [C, TOK])
        kv = [sb(f"kv{i}", [P, TOK, H3]) for i in range(2)]
        V = [sb(f"v{i}", [P, 2 * H3, H3, D3]) for i in range(2)]
        nm = [sb(f"nm{i}", [P, 2]) for i in range(2)]
        sm = [sb(f"sm{i}", [P, 2]) for i in range(2)]
        rc = [sb(f"rc{i}", [P, 2]) for i in range(2)]
        E = [sb(f"e{i}", [P, 3, P]) for i in range(2)]
        PT = [sb(f"pt{i}", [P, 3, P]) for i in range(2)]
        own = sb("own", [C, TOK, H3])
        OT = sb("ot", [C, TOK, H3])
        OR = [sb(f"or{i}", [C, TOK]) for i in range(2)]
        parts = ((0, 0, 1), (1, 1, 3))
        U = H3

        with nc.Block() as block:
            @block.gpsimd
            def _(pool):
                k.clear_retired()
                def norm(n, slot):
                    normalise(pool, k, s, n, 2, k.Y[slot][:, 0:2, :], k.bp3, n - 1)

                def queries(m, slot):
                    pool.wait_ge(s["qs"], m + 1)
                    after(pool, s["sc"], U * (m - 1))
                    pool.tensor_tensor(qx[slot][0:C], qs[:, :, None].broadcast_to([C, TOK, H3]),
                                       k.groupmask[:, None, :].broadcast_to([C, TOK, H3]), ALU.mult).then_inc(s["qx"], 1)

                norm(0, 0)
                queries(0, 0)
                norm(1, 1)
                pool.tensor_copy(own[:], k.ingroup[:, None, :].broadcast_to([C, TOK, H3])).then_inc(s["own"], 1)

                def body(n, slot, first, last):
                    if not last:
                        queries(n + 1, 1 - slot)
                    if exists(n + 2, IMAGES):
                        norm(n + 2, slot)
                pipeline(pool, IMAGES, body)
                next_first_step(pool, k, s, IMAGES)

            @block.tensor
            def _(pe):
                def score(n, h, slot):
                    u = U * n + h
                    b = bank[4 + h % 2]
                    q = qx[slot][:].rearrange("p t g -> p (t g)")
                    kk = kv[slot][:].rearrange("p t g -> p (t g)")
                    if h == 0:
                        pe.wait_ge(s["qx"], n + 1)
                        pe.wait_ge(s["e"], 3 * (n + 1))
                    after(pe, s["exp"], u - 1)
                    pe.matmul(b[:, 0:P], q[:, h * TOK:h * TOK + P], kk[:, h * TOK:h * TOK + P], start=True, stop=False, skip_group_check=True)
                    pe.matmul(b[:, P:3 * P], q[:, h * TOK + P:(h + 1) * TOK], kk[:, h * TOK:(h + 1) * TOK], start=False, stop=False, skip_group_check=True)
                    pe.matmul(b[:].rearrange("p (a c) -> p a c", a=2)[:, :, 0:P], k.identb[:], k.causal[:, None, :].broadcast_to([P, 2, P]),
                              start=False, stop=True, skip_group_check=True).then_inc(s["sc"], 1)

                def probs(n, h):
                    u = U * n + h
                    pe.wait_ge(s["nrm"], u + 1)
                    after(pe, s["pte"], u - 1)
                    for i in range(3):
                        last = pe.transpose(bank[6 + h % 2][:, i * P:(i + 1) * P], E[h % 2][:, i, :], k.ident[:])
                    last.then_inc(s["pt"], 1)

                def values(n, h, slot):
                    u = U * n + h
                    pe.wait_ge(s["pte"], u + 1)
                    after(pe, s["ote"], u)
                    if h == 0:
                        pe.wait_ge(s["v"], n + 1)
                    for kc in range(2):
                        w = V[slot][:, 2 * h + kc, :, :].rearrange("p g d -> p (g d)")
                        last = pe.matmul(bank[3][0:C, kc * P:TOK], w, PT[h % 2][:, 2 * kc:2 + kc, :], start=(kc == 0), stop=(kc == 1), skip_group_check=True)
                    last.then_inc(s["av"], 1)

                def out(n, slot):
                    pe.wait_ge(s["red"], 2 * (n + 1))
                    for t in range(2):
                        last = pe.matmul(bank[0][:, t * C:(t + 1) * C], OR[slot][:, t * P:(t + 1) * P], k.wp3[:], start=True, stop=True)
                    last.then_inc(s["out"], 1)

                def tokens(m, slot):
                    pe.wait_ge(s["y"], m + 1)
                    after(pe, s["x"], m - 2)
                    for t in range(2):
                        last = pe.transpose(bank[0][0:C, t * P:(t + 1) * P], k.Y[slot][:, t, :], k.ident[:])
                    last.then_inc(s["T"], 1)

                def project(m, j, slot):
                    if j == 0:
                        pe.wait_ge(s["hT"], m + 1)
                        after(pe, s["e"], 3 * m - 1)
                        pe.matmul(bank[1][0:C, 0:TOK], k.wq3[:], k.hT[slot][:, 0:TOK], start=True, stop=True).then_inc(s["pj"], 1)
                        return
                    after(pe, s["qs"] if j == 2 else s["e"], m + 1 if j == 2 else 3 * m + j // 2)
                    for i in range(2):
                        last = pe.matmul(bank[1 + j % 2][0:C + D3, i * TOK:(i + 1) * TOK], k.wkv3[:, 2 * j - 2 + i, :], k.hT[slot][:, 0:TOK], start=True, stop=True)
                    last.then_inc(s["pj"], 1)

                def value_rows(n, slot):
                    kk = kv[slot][:].rearrange("p t g -> p (t g)")
                    for j in range(2 * H3):
                        last = pe.transpose(bank[0][:, 256 + j * D3:256 + (j + 1) * D3], kk[C:C + D3, j * P:(j + 1) * P], k.ident[C:C + D3, C:C + D3])
                    last.then_inc(s["vt"], 1)

                def step(n, h, slot, start, end):
                    if h < U:
                        score(n, h, slot)
                    if h < 2:
                        if not start:
                            probs(n - 1, U + h - 2)
                    elif h < U + 2:
                        probs(n, h - 2)
                    if h < 3:
                        if not start:
                            values(n - 1, U + h - 3, 1 - slot)
                    else:
                        values(n, h - 3, slot)
                    if h == 0 and not end:
                        tokens(n + 1, 1 - slot)
                    elif h < 5 and not end:
                        project(n + 1, h - 1, 1 - slot)
                    if h == 1:
                        value_rows(n, slot)
                    if h == 3 and not start:
                        pe.wait_ge(s["v"], n + 1)
                        out(n - 1, 1 - slot)

                tokens(0, 0)
                for j in range(4):
                    project(0, j, 0)
                pe.wait_ge(s["pad"], 1)

                def body(n, slot, first, last):
                    for h in range(U):
                        step(n, h, slot, first, last)
                pipeline(pe, IMAGES, body)
                for h in range(U, U + 3):
                    step(IMAGES - 1, h, 1, False, True)
                out(IMAGES - 1, 1)

            @block.scalar
            def _(act):
                def exps(n, h):
                    u = U * n + h
                    act.wait_ge(s["nm"], u + 1)
                    after(act, s["pt"], u - 1)
                    after(act, s["rec"], u - 1)
                    for c, lo, hi in parts:
                        last = act.activation(E[h % 2][:, lo:hi, :], bank[4 + h % 2][:, lo * P:hi * P].rearrange("p (a b) -> p a b", b=P), ACT.Exp,
                                              bias=nm[h % 2][:, c:c + 1], accum_out=sm[h % 2][:, c:c + 1])
                    last.then_inc(s["exp"], 1)

                def pt_out(n, h):
                    u = U * n + h
                    act.wait_ge(s["pt"], u + 1)
                    after(act, s["av"], u - 1)
                    act.activation(PT[h % 2][:], bank[6 + h % 2][:, 0:3 * P].rearrange("p (a b) -> p a b", b=P), ACT.Copy).then_inc(s["pte"], 1)

                def tokens(m, slot):
                    act.wait_ge(s["T"], m + 1)
                    after(act, s["pj"], 4 * (m - 1))
                    act.activation(k.hT[slot][:, 0:TOK], bank[0][0:C, 0:TOK], ACT.Copy).then_inc(s["hT"], 1)

                def project(m, j, slot):
                    act.wait_ge(s["pj"], 4 * m + j + 1)
                    after(act, s["sc"], U * (m - 1))
                    after(act, s["vt"], m - 1)
                    act.activation(kv[slot][0:C + D3].rearrange("p t g -> p g t")[:, 2 * j - 2:2 * j, :],
                                   bank[1 + j % 2][0:C + D3, :].rearrange("p (g t) -> p g t", g=2), ACT.Copy).then_inc(s["e"], 1)

                def queries(m):
                    act.wait_ge(s["pj"], 4 * m + 1)
                    after(act, s["qx"], m)
                    act.activation(qs[:], bank[1][0:C, 0:TOK], ACT.Copy).then_inc(s["qs"], 1)

                def value_rows(n, slot):
                    act.wait_ge(s["vt"], n + 1)
                    after(act, s["av"], U * (n - 1))
                    act.activation(V[slot][:], bank[0][:, 256:256 + 2 * H3 * D3].rearrange("p (j d) -> p j d", d=D3)[:, :, None, :]
                                   .broadcast_to([P, 2 * H3, H3, D3]), ACT.Copy).then_inc(s["v"], 1)

                tokens(0, 0)
                queries(0)
                act.wait_ge(s["pad"], 1)
                for j in range(1, 4):
                    project(0, j, 0)

                def body(n, slot, first, last):
                    for h in range(U):
                        if h >= 2:
                            pt_out(n, h - 2)
                        elif not first:
                            pt_out(n - 1, U + h - 2)
                        if h == U - 1 and not last:
                            project(n + 1, 3, 1 - slot)
                        exps(n, h)
                        if not last:
                            if h == 0:
                                tokens(n + 1, 1 - slot)
                            elif h == 1:
                                queries(n + 1)
                            elif h in (3, 4):
                                project(n + 1, h - 2, 1 - slot)
                        if h == 1:
                            value_rows(n, slot)
                pipeline(act, IMAGES, body)
                pt_out(IMAGES - 1, U - 2)
                pt_out(IMAGES - 1, U - 1)

            @block.vector
            def _(dve):
                def maxima(n, h):
                    u = U * n + h
                    dve.wait_ge(s["sc"], u + 1)
                    after(dve, s["exp"], u - 1)
                    for c, lo, hi in parts:
                        last = dve.tensor_reduce(nm[h % 2][:, c:c + 1], bank[4 + h % 2][:, lo * P:hi * P], AX.X, ALU.max, negate=True)
                    last.then_inc(s["nm"], 1)

                def norm(n, h):
                    u = U * n + h
                    dve.wait_ge(s["exp"], u + 1)
                    after(dve, s["nrm"], u - 1)
                    dve.reciprocal(rc[h % 2][:], sm[h % 2][:]).then_inc(s["rec"], 1)
                    dve.wait_ge(s["rec"], u + 1)
                    for c, lo, hi in parts:
                        last = dve.tensor_scalar(E[h % 2][:, lo:hi, :], E[h % 2][:, lo:hi, :], rc[h % 2][:, c:c + 1], None, ALU.mult)
                    last.then_inc(s["nrm"], 1)

                def head_out(n, h, slot):
                    dve.wait_ge(s["av"], U * n + h + 1)
                    rows = slice(h * TOK, (h + 1) * TOK)
                    dve.tensor_tensor(OT[:].rearrange("p t g -> p (t g)")[:, rows], bank[3][0:C, 0:TOK],
                                      own[:].rearrange("p t g -> p (t g)")[:, rows], ALU.mult).then_inc(s["ote"], 1)
                    if h in (U // 2 - 1, U - 1):
                        half = slice(h // (U // 2) * P, h // (U // 2) * P + P)
                        dve.wait_ge(s["ote"], U * n + h + 1)
                        after(dve, s["out"], n - 1)
                        dve.tensor_reduce(OR[slot][:, half], OT[:, half, :], AX.X, ALU.add).then_inc(s["red"], 1)

                def residual(n):
                    dve.wait_ge(s["out"], n + 1)
                    dve.wait_ge(s["xb"], n + 1)
                    add_new(dve, k, s, n, 2, bank[0][:, 0:2 * C].rearrange("p (t c) -> p t c", t=2))

                for t in qx + kv:
                    last = dve.memset(t[C:P], 0.0)
                last.then_inc(s["pad"], 1)
                dve.wait_ge(s["own"], 1)

                def body(n, slot, first, last):
                    for h in range(U):
                        maxima(n, h)
                        if h >= 1:
                            norm(n, h - 1)
                        elif not first:
                            norm(n - 1, U - 1)
                        if h >= 3:
                            head_out(n, h - 3, slot)
                        elif not first:
                            head_out(n - 1, U + h - 3, 1 - slot)
                        if h == 4 and not first:
                            residual(n - 1)
                        if h == 1 and exists(n - 2, IMAGES):
                            statistics(dve, k, s, n - 2, 2)
                pipeline(dve, IMAGES, body)
                norm(IMAGES - 1, U - 1)
                for h in range(U - 3, U):
                    head_out(IMAGES - 1, h, 1)
                statistics(dve, k, s, IMAGES - 2, 2)
                residual(IMAGES - 1)
                statistics(dve, k, s, IMAGES - 1, 2)


def experts(k, bank, out):
    nc = k.nc
    s = k.sems("ex", LN_SEMS + "T hT gl gate exp up gelu down acc g3 g4 g5 st")
    steps = TILES // 4
    GATE = 17
    NB = 4
    UP = EXPERTS * KH
    with ExitStack() as ctx:
        def sb(name, shape, dt=F32):
            return k.sb("ex_" + name, shape, dt, ctx)

        L = [sb(f"L{i}", [P, 4, EXPERTS]) for i in range(2)]
        one = sb("one", [P, 4, 1])
        ge = sb("ge", [P, 4, EXPERTS, EXPERTS])
        gt = sb("gt", [P, 4, EXPERTS, EXPERTS])
        rank = sb("rank", [P, 4, EXPERTS])
        tmp = [sb(f"tmp{i}", [P, 4, C]) for i in range(2)]
        G = [sb(f"G{i}", [P, KH, 512]) for i in range(2)]
        full = [P, 4, EXPERTS]
        square = [P, 4, EXPERTS, EXPERTS]

        with nc.Block() as block:
            @block.gpsimd
            def _(pool):
                k.clear_retired()
                def bias(n, slot):
                    own = L[slot]
                    b = k.eb2[:, :, None, :]
                    wide = [P, 4, C]
                    pool.wait_ge(s["gate"], GATE * (n + 1))
                    after(pool, s["xb"], n)
                    pool.tensor_tensor(tmp[0][:], b[:, 0].broadcast_to(wide), own[:, :, 0:1].broadcast_to(wide), ALU.mult).then_inc(s["g4"], 1)
                    for e in range(1, EXPERTS):
                        u = (EXPERTS - 1) * n + e
                        after(pool, s["g5"], u - 1)
                        pool.tensor_tensor(tmp[1][:], b[:, e].broadcast_to(wide), own[:, :, e:e + 1].broadcast_to(wide), ALU.mult).then_inc(s["g3"], 1)
                        pool.wait_ge(s["g4"], n + 1)
                        after(pool, s["g3"], u)
                        pool.tensor_tensor(tmp[0][:], tmp[0][:], tmp[1][:], ALU.add).then_inc(s["g5"], 1)
                    x = k.X[:].rearrange("p (s t) c -> p s t c", t=4)[:, bass.ds(n, 1), :, :]
                    alone(pool, k)
                    pool.wait_ge(s["g5"], (EXPERTS - 1) * (n + 1))
                    pool.tensor_tensor(x, x, tmp[0][:, None, :, :], ALU.add).then_inc(s["xb"], 1)

                def norm(n, slot):
                    normalise(pool, k, s, n, 4, k.Y[slot][:, 0:4, :], None, n - 1)
                norm(0, 0)

                def body(n, slot, first, last):
                    if not last:
                        norm(n + 1, 1 - slot)
                    bias(n, slot)
                pipeline(pool, steps, body)

            @block.tensor
            def _(pe):
                def tokens(n, slot):
                    pe.wait_ge(s["y"], n + 1)
                    after(pe, s["hT"], n)
                    for t in range(4):
                        last = pe.transpose(bank[4][0:C, t * P:(t + 1) * P], k.Y[slot][:, t, :], k.ident[:])
                    last.then_inc(s["T"], 1)

                def gate(n, slot):
                    pe.wait_ge(s["hT"], n + 1)
                    after(pe, s["gate"], GATE * (n - 1) + 1)
                    for t in range(4):
                        last = pe.matmul(bank[5][:, t * EXPERTS:(t + 1) * EXPERTS], k.hT[slot][:, t * P:(t + 1) * P], k.gw[:], start=True, stop=True)
                    last.then_inc(s["gl"], 1)

                def up(n, e, slot):
                    for j in range(KH):
                        v = KH * e + j
                        after(pe, s["gelu"], UP * n + v + 1 - NB)
                        pe.matmul(bank[v % NB][:], k.ew1[:, e, j * P:(j + 1) * P], k.hT[slot][:], start=True, stop=True).then_inc(s["up"], 1)

                def down(n, e):
                    u = EXPERTS * n + e
                    pe.wait_ge(s["gelu"], KH * (u + 1))
                    after(pe, s["acc"], 4 * (u - 1))
                    for t in range(4):
                        for j in range(KH):
                            last = pe.matmul(bank[6 + e % 2][:, t * C:(t + 1) * C], G[e % 2][:, j, t * P:(t + 1) * P], k.ew2[:, e, j, :],
                                             start=(j == 0), stop=(j == KH - 1))
                    last.then_inc(s["down"], 1)

                tokens(0, 0)
                gate(0, 0)

                def body(n, slot, first, last):
                    for e in range(EXPERTS):
                        up(n, e, slot)
                        if e:
                            down(n, e - 1)
                        elif not first:
                            down(n - 1, EXPERTS - 1)
                        if e == 0 and not last:
                            tokens(n + 1, 1 - slot)
                        if e == 1 and not last:
                            gate(n + 1, 1 - slot)
                pipeline(pe, steps, body)
                down(steps - 1, EXPERTS - 1)

            @block.scalar
            def _(act):
                def tokens(n, slot):
                    act.wait_ge(s["T"], n + 1)
                    after(act, s["up"], UP * (n - 1))
                    after(act, s["gl"], n - 1)
                    act.activation(k.hT[slot][:], bank[4][0:C, :], ACT.Copy).then_inc(s["hT"], 1)

                def exps(n, slot):
                    act.wait_ge(s["gate"], GATE * n + 3)
                    act.activation(L[slot][:], L[slot][:], ACT.Exp).then_inc(s["exp"], 1)

                tokens(0, 0)
                exps(0, 0)

                def body(n, slot, first, last):
                    for e in range(EXPERTS):
                        u = EXPERTS * n + e
                        after(act, s["down"], u - 1)
                        for j in range(KH):
                            act.wait_ge(s["up"], KH * u + j + 1)
                            act.activation(G[e % 2][:, j, :], bank[(KH * e + j) % NB][:], ACT.Gelu, bias=k.eb1[:, e, j:j + 1]).then_inc(s["gelu"], 1)
                        if e == 0 and not last:
                            tokens(n + 1, 1 - slot)
                        if e == 2 and not last:
                            exps(n + 1, 1 - slot)
                pipeline(act, steps, body)

            @block.vector
            def _(dve):
                def logits(n, slot):
                    dve.wait_ge(s["gl"], n + 1)
                    after(dve, s["xb"], n - 1)
                    after(dve, s["acc"], 4 * EXPERTS * (n - 1))
                    dve.tensor_tensor(L[slot][:], bank[5][:, 0:4 * EXPERTS].rearrange("p (t e) -> p t e", e=EXPERTS),
                                      k.gb[:, None, :].broadcast_to(full), ALU.add).then_inc(s["gate"], 1)
                    dve.wait_ge(s["gate"], GATE * n + 1)
                    dve.tensor_reduce(one[:, :, 0], L[slot][:], AX.X, ALU.max).then_inc(s["gate"], 1)
                    dve.wait_ge(s["gate"], GATE * n + 2)
                    dve.tensor_tensor(L[slot][:], L[slot][:], one[:].broadcast_to(full), ALU.subtract).then_inc(s["gate"], 1)

                def top2(n, slot):
                    w = L[slot]
                    dve.wait_ge(s["exp"], n + 1)
                    dve.tensor_reduce(one[:, :, 0], w[:], AX.X, ALU.add).then_inc(s["gate"], 1)
                    dve.wait_ge(s["gate"], GATE * n + 4)
                    dve.reciprocal(one[:], one[:]).then_inc(s["gate"], 1)
                    dve.wait_ge(s["gate"], GATE * n + 5)
                    dve.tensor_tensor(w[:], w[:], one[:].broadcast_to(full), ALU.mult).then_inc(s["gate"], 1)
                    dve.wait_ge(s["gate"], GATE * n + 6)
                    other, own = w[:, :, None, :].broadcast_to(square), w[:, :, :, None].broadcast_to(square)
                    dve.tensor_tensor(ge[:], other, own, ALU.is_ge).then_inc(s["gate"], 1)
                    dve.tensor_tensor(gt[:], other, own, ALU.is_gt).then_inc(s["gate"], 1)
                    dve.wait_ge(s["gate"], GATE * n + 8)
                    dve.tensor_tensor(ge[:], ge[:], k.lower[:, None, :, :].broadcast_to(square), ALU.mult).then_inc(s["gate"], 1)
                    dve.wait_ge(s["gate"], GATE * n + 9)
                    dve.tensor_tensor(gt[:], gt[:], ge[:], ALU.max).then_inc(s["gate"], 1)
                    dve.wait_ge(s["gate"], GATE * n + 10)
                    dve.tensor_reduce(rank[:], gt[:], AX.X, ALU.add).then_inc(s["gate"], 1)
                    dve.wait_ge(s["gate"], GATE * n + 11)
                    dve.tensor_scalar(rank[:], rank[:], 2.0, None, ALU.is_lt).then_inc(s["gate"], 1)
                    dve.wait_ge(s["gate"], GATE * n + 12)
                    dve.tensor_tensor(w[:], w[:], rank[:], ALU.mult).then_inc(s["gate"], 1)
                    dve.wait_ge(s["gate"], GATE * n + 13)
                    dve.tensor_reduce(one[:, :, 0], w[:], AX.X, ALU.add).then_inc(s["gate"], 1)
                    dve.wait_ge(s["gate"], GATE * n + 14)
                    dve.tensor_scalar(one[:], one[:], 1e-9, None, ALU.add).then_inc(s["gate"], 1)
                    dve.wait_ge(s["gate"], GATE * n + 15)
                    dve.reciprocal(one[:], one[:]).then_inc(s["gate"], 1)
                    dve.wait_ge(s["gate"], GATE * n + 16)
                    dve.tensor_tensor(w[:], w[:], one[:].broadcast_to(full), ALU.mult).then_inc(s["gate"], 1)

                def accumulate(n, e, slot):
                    u = EXPERTS * n + e
                    if e == 0:
                        dve.wait_ge(s["xb"], n + 1)
                        dve.wait_ge(s["gate"], GATE * (n + 1))
                    dve.wait_ge(s["down"], u + 1)
                    after(dve, s["acc"], 4 * u)
                    for t in range(4):
                        x = k.X[:, bass.ds(n * 4 + t, 1), :]
                        dve.scalar_tensor_tensor(out=x, in0=bank[6 + e % 2][:, None, t * C:(t + 1) * C], scalar=L[slot][:, t, e:e + 1],
                                                 in1=x, op0=ALU.mult, op1=ALU.add).then_inc(s["acc"], 1)

                logits(0, 0)
                top2(0, 0)

                def body(n, slot, first, last):
                    if not first:
                        accumulate(n - 1, EXPERTS - 1, 1 - slot)
                    accumulate(n, 0, slot)
                    if not last:
                        logits(n + 1, 1 - slot)
                    accumulate(n, 1, slot)
                    if not last:
                        top2(n + 1, 1 - slot)
                    accumulate(n, 2, slot)
                pipeline(dve, steps, body)
                accumulate(steps - 1, EXPERTS - 1, 1)

            @block.sync
            def _(sp):
                dst = out.rearrange("b (y i) c d -> (i c) (b y) d", y=2)
                for n in range(steps):
                    sp.wait_ge(s["acc"], 4 * EXPERTS * (n + 1))
                    sp.dma_start(dst[:, 4 * n:4 * n + 4, :], k.X[:, 4 * n:4 * n + 4, :]).then_inc(s["st"], 16)
                sp.wait_ge(s["st"], 16 * steps)


def build(nc, a, out):
    with ExitStack() as ctx:
        k = Core(nc, ctx)
        bank = [ctx.enter_context(nc.psum_tensor(f"bank{i}", [P, 512], F32)) for i in range(8)]
        setup(k, bank, a)
        k.end_phase()
        phases = ((window_attention, (), None), (mlp, ("ml0", k.mlp0), (4, k.mlp0["b2"])), (conv_mixer, (), (2, k.bout)),
                  (mlp, ("ml1", k.mlp1), (4, k.mlp1["b2"])), (full_attention, (), (2, k.bp2)), (binary_ffn, (), (GT, None)),
                  (causal_attention, (), (2, k.bp3)), (experts, (out,), (4, None)))
        for i, (phase, more, norm) in enumerate(phases):
            k.next_norm = phases[i + 1][2] if phase is not experts else None
            phase(k, bank, *more)
            k.end_phase()
        k.clear_retired()
        nc.all_engine_barrier()


def constants():
    f = np.float32
    decay, gain = 0.6, 0.4
    d = np.abs(np.arange(SIDE)[:, None] - np.arange(SIDE)[None, :])
    scan = gain * decay ** d * (1 + (d == 0))
    eye = np.eye(SIDE)
    mixer = np.eye(TOK) + 0.25 * (np.kron(eye, scan) + np.kron(scan, eye))
    tok = np.arange(TOK).reshape(2, WS, 2, WS).transpose(0, 2, 1, 3).reshape(-1)
    return {
        "ident": np.eye(P, dtype=f),
        "mixer": mixer.astype(f),
        "perm": (tok[0:P, None] == np.arange(P)[None, :]).astype(f),
        "headmask": (np.arange(C)[:, None] // D0 == np.arange(H0)[None, :]).astype(f),
        "ingroup": (np.arange(C)[:, None] // D3 == np.arange(H3)[None, :]).astype(f),
        "groupmask": ((np.arange(C)[:, None] // D3 == np.arange(H3)[None, :]) * float(C) ** -0.5).astype(f),
        "causal": np.where(np.arange(P)[:, None] >= np.arange(P)[None, :], 0.0, -1e30).astype(f),
        "lower": (np.arange(EXPERTS)[None, :] < np.arange(EXPERTS)[:, None]).astype(f),
    }


def kernel(**inputs):
    import concourse.bacc as bacc
    from concourse.bass_utils import run_bass_kernel_spmd

    nc = bacc.Bacc("TRN2", target_bir_lowering=False, num_devices=1)
    arrays = {name: np.ascontiguousarray(value) for name, value in inputs.items()}
    arrays.update(constants())
    a = {name: nc.dram_tensor(f"in_{name}", v.shape, mybir.dt.from_np(v.dtype), kind="ExternalInput").ap()
         for name, v in arrays.items()}
    out = nc.dram_tensor("out_tokens", (IMAGES, SIDE, SIDE, C), F32, kind="ExternalOutput").ap()
    build(nc, a, out)
    r = run_bass_kernel_spmd(nc, [{f"in_{name}": v for name, v in arrays.items()}], core_ids=[0])
    return r.results[0]["out_tokens"]
```
